# Optimizing a Trainium2 kernel written in Bass

```python
import numpy as np
import jax
import jax.numpy as jnp

def _softmax(x, axis=-1):
    return jax.nn.softmax(x, axis=axis)

def _gelu(x):
    return jax.nn.gelu(x, approximate=True)

def _silu(x):
    return jax.nn.silu(x)

def _sigmoid(x):
    return jax.nn.sigmoid(x)

def _layernorm(x, axis=-1, eps=1e-05):
    m = jnp.mean(x, axis=axis, keepdims=True)
    v = jnp.var(x, axis=axis, keepdims=True)
    return (x - m) / jnp.sqrt(v + eps)

def _scatter_add(tgt, idx, src, axis=0):
    return tgt.at[idx].add(src)

def _segment_sum(src, seg, n):
    return jax.ops.segment_sum(src, seg, n)
kernel_name = 'mk_xattn_ffn_d4_seqx_r8_9e7d58'

def setup_inputs(seed: int=0):
    np.random.seed(seed)
    _w = jnp.asarray

    def _rec_inputs():
        import jax
        import jax.numpy as jnp
        _rk = jax.random.key(seed)
        x = 0.002226 + 0.9996 * jax.random.normal(jax.random.fold_in(_rk, 1), (4, 512, 128), jnp.float32)
        _lenS = 512 - jax.random.randint(jax.random.fold_in(_rk, 7), (4,), 0, max(1, 512 // 4) + 1, jnp.int32)
        _lenS2 = 154 - jax.random.randint(jax.random.fold_in(_rk, 8), (4,), 0, max(1, 154 // 4) + 1, jnp.int32)
        _ctx_1024P = jax.random.normal(jax.random.fold_in(_rk, 11), (4, 16, 128), jnp.float32)
        _ctx_1024c = jax.random.dirichlet(jax.random.fold_in(_rk, 511), 0.3 * jnp.ones((16,), jnp.float32), (4, 154))
        _ctx_1024t = jnp.einsum('bsk,bkd->bsd', _ctx_1024c, _ctx_1024P)
        _ctx_1024t = _ctx_1024t * jax.lax.rsqrt(jnp.mean(jnp.square(_ctx_1024t)) + 1e-12) * 0.953939
        ctx_1024 = -0.000125008 + 0.999885 * (_ctx_1024t + 0.3 * jax.random.normal(jax.random.fold_in(_rk, 611), (4, 154, 128), jnp.float32))
        fside_BxSxS2_0 = jax.random.uniform(jax.random.fold_in(_rk, 12), (4, 512, 154), jnp.float32, 0.0, 1)
        _validS = jnp.arange(512)[None, :] < _lenS[:, None]
        _validS2 = jnp.arange(154)[None, :] < _lenS2[:, None]
        _causal = jnp.tril(jnp.ones((512, 512), dtype=bool))
        mask_BxSxS2_ik1 = jnp.where(jnp.broadcast_to(_validS2[:, None, :], (4, 512, 154)), 1, 0).astype(jnp.int32)
        mask_SxS2_fk0 = jnp.where(jnp.broadcast_to(_validS2[0:1, :], (512, 154)), -1000000000.0, 0.0).astype(jnp.float32)
        mask_1x1xSxS2_ik0 = jnp.where(jnp.broadcast_to(_validS2[0:1, None, None, :], (1, 1, 512, 154)), 0, 1).astype(jnp.int32)
        return (x, ctx_1024, fside_BxSxS2_0, mask_BxSxS2_ik1, mask_SxS2_fk0, mask_1x1xSxS2_ik0)
    x, ctx_1024, fside_BxSxS2_0, mask_BxSxS2_ik1, mask_SxS2_fk0, mask_1x1xSxS2_ik0 = _rec_inputs()

    def _L0_xattn_setup():
        import jax, jax.numpy as jnp
        import numpy as np
        B, M, N, DIM, DH, H = (8, 512, 64, 128, 128, 8)
        INNER = DH * H
        EPS = 1e-05

        def _layernorm(x, g, b):
            mu = jnp.mean(x, axis=-1, keepdims=True)
            var = jnp.var(x, axis=-1, keepdims=True)
            return (x - mu) * jax.lax.rsqrt(var + EPS) * g + b
        key = jax.random.key(seed)
        ks = jax.random.split(key, 8)
        sd = 0.02
        return {'x': jax.random.normal(ks[0], (B, M, DIM), jnp.float32), 'latents': jax.random.normal(ks[1], (B, N, DIM), jnp.float32), 'gamma_media': jnp.ones((DIM,), jnp.float32), 'beta_media': jnp.zeros((DIM,), jnp.float32), 'gamma_lat': jnp.ones((DIM,), jnp.float32), 'beta_lat': jnp.zeros((DIM,), jnp.float32), 'Wq': jax.random.normal(ks[2], (DIM, INNER), jnp.float32) * sd, 'bq': jnp.zeros((INNER,), jnp.float32), 'Wkv': jax.random.normal(ks[3], (DIM, 2 * INNER), jnp.float32) * sd, 'bkv': jnp.zeros((2 * INNER,), jnp.float32), 'Wo': jax.random.normal(ks[4], (INNER, DIM), jnp.float32) * sd, 'bo': jnp.zeros((DIM,), jnp.float32)}
    _L0_xattn_all = _L0_xattn_setup()
    _L0_xattn_in = {k: v for k, v in _L0_xattn_all.items() if k in ('gamma_media', 'beta_media', 'gamma_lat', 'beta_lat', 'Wq', 'bq', 'Wkv', 'bkv', 'Wo', 'bo')}
    del _L0_xattn_all

    def _L0_ffn_setup():
        import math
        import jax, jax.numpy as jnp
        import numpy as np
        B, T, D, H, E, K, S = (4, 512, 128, 256, 16, 2, 2)
        ROUTE_SCALE = 1.0

        def _swiglu(x, w1, w3, w2):
            return jax.nn.silu(x @ w1) * (x @ w3) @ w2
        key = jax.random.key(seed)
        ks = jax.random.split(key, 9)
        s = 0.02
        return {'x': jax.random.normal(ks[0], (B, T, D), jnp.float32), 'gate_w': jax.random.normal(ks[1], (D, E), jnp.float32) * s, 'gate_b': jnp.zeros((E,), jnp.float32), 'ew1': jax.random.normal(ks[2], (E, D, H), jnp.float32) * s, 'ew3': jax.random.normal(ks[3], (E, D, H), jnp.float32) * s, 'ew2': jax.random.normal(ks[4], (E, H, D), jnp.float32) * s, 'sw1': jax.random.normal(ks[5], (S, D, H), jnp.float32) * s, 'sw3': jax.random.normal(ks[6], (S, D, H), jnp.float32) * s, 'sw2': jax.random.normal(ks[7], (S, H, D), jnp.float32) * s}
    _L0_ffn_all = _L0_ffn_setup()
    _L0_ffn_in = {k: v for k, v in _L0_ffn_all.items() if k in ('gate_w', 'gate_b', 'ew1', 'ew3', 'ew2', 'sw1', 'sw3', 'sw2')}
    del _L0_ffn_all

    def _L1_xattn_setup():
        import jax, jax.numpy as jnp
        import numpy as np
        NUM_HEADS = 16
        HIDDEN = 128
        B, S = (2, 256)

        def _split_heads(x, H):
            b, s, d = x.shape
            return x.reshape(b, s, H, d // H).transpose(0, 2, 1, 3)
        key = jax.random.key(seed)
        ks = jax.random.split(key, 14)
        D = HIDDEN
        scale = 1.0 / np.sqrt(D)
        inp = {'query': jax.random.normal(ks[0], (B, S, D), jnp.float32), 'key_in': jax.random.normal(ks[1], (B, S, D), jnp.float32), 'value': jax.random.normal(ks[2], (B, S, D), jnp.float32), 'group_prob': jax.random.uniform(ks[3], (B, S, S), jnp.float32), 'mask': jax.random.randint(ks[4], (B, S, S), 0, 2, jnp.int32), 'wq_k': jax.random.normal(ks[5], (D, D), jnp.float32) * scale, 'wq_b': jnp.zeros((D,), jnp.float32), 'wk_k': jax.random.normal(ks[6], (D, D), jnp.float32) * scale, 'wk_b': jnp.zeros((D,), jnp.float32), 'wv_k': jax.random.normal(ks[7], (D, D), jnp.float32) * scale, 'wv_b': jnp.zeros((D,), jnp.float32), 'wo_k': jax.random.normal(ks[8], (D, D), jnp.float32) * scale, 'wo_b': jnp.zeros((D,), jnp.float32)}
        return inp
    _L1_xattn_all = _L1_xattn_setup()
    _L1_xattn_in = {k: v for k, v in _L1_xattn_all.items() if k in ('wq_k', 'wq_b', 'wk_k', 'wk_b', 'wv_k', 'wv_b', 'wo_k', 'wo_b')}
    del _L1_xattn_all

    def _L1_ffn_setup():
        import jax, jax.numpy as jnp
        import numpy as np
        D = 128
        H = 16
        HD = D // H
        E = 32
        ES = 128
        K = 4
        B, S = (2, 128)
        ROPE_BASE = 10000.0

        def _layernorm(x, g, b):
            m = x.mean(-1, keepdims=True)
            v = ((x - m) ** 2).mean(-1, keepdims=True)
            return (x - m) * jax.lax.rsqrt(v + 1e-05) * g + b

        def _forward(src, wq, wk, wv, wp, wo, ln1_g, ln1_b, ln2_g, ln2_b, sel_w, keys, values):
            Bs, Ss, Ds = src.shape
            scale = 1.0 / jnp.sqrt(jnp.array(HD, dtype=src.dtype))
            x = _layernorm(src, ln1_g, ln1_b)
            q = (x @ wq).reshape(Bs, Ss, H, HD)
            k = (x @ wk).reshape(Bs, Ss, H, HD)
            v = (x @ wv).reshape(Bs, Ss, H, HD)
            pos = jnp.arange(Ss - 1, -Ss, -1, dtype=src.dtype)
            inv_freq = 1.0 / ROPE_BASE ** (jnp.arange(0, Ds, 2, dtype=src.dtype) / Ds)
            ang = pos[:, None] * inv_freq[None, :]
            pe = jnp.concatenate([jnp.sin(ang), jnp.cos(ang)], axis=-1)
            p = (pe @ wp).reshape(2 * Ss - 1, H, HD)
            ac = jnp.einsum('bihd,bjhd->bhij', q, k)
            bd_full = jnp.einsum('bihd,phd->bhip', q, p)
            rel = jnp.arange(Ss)[:, None] - jnp.arange(Ss)[None, :] + (Ss - 1)
            bd = bd_full[:, :, jnp.arange(Ss)[:, None], rel]
            att = jax.nn.softmax((ac + bd) * scale, axis=-1)
            attn_out = jnp.einsum('bhij,bjhd->bihd', att, v).reshape(Bs, Ss, Ds) @ wo
            src = src + attn_out
            x2 = _layernorm(src, ln2_g, ln2_b)
            sel = jax.nn.sigmoid(x2 @ sel_w)
            scores, idx = jax.lax.top_k(sel, K)
            gate = (jax.nn.one_hot(idx, E, dtype=sel.dtype) * scores[..., None]).sum(-2)
            h = jax.nn.relu(jnp.einsum('bsd,edh->bseh', x2, keys))
            moe_out = jnp.einsum('bseh,ehd,bse->bsd', h, values, gate)
            return src + moe_out
        key = jax.random.key(seed)
        ks = jax.random.split(key, 10)
        std_scale = np.sqrt(2.0 / 18)
        w_std = std_scale / np.sqrt(D)
        return {'src': jax.random.normal(ks[0], (B, S, D), jnp.float32), 'wq': jax.random.normal(ks[1], (D, H * HD), jnp.float32) * w_std, 'wk': jax.random.normal(ks[2], (D, H * HD), jnp.float32) * w_std, 'wv': jax.random.normal(ks[3], (D, H * HD), jnp.float32) * w_std, 'wp': jax.random.normal(ks[4], (D, H * HD), jnp.float32) * w_std, 'wo': jax.random.normal(ks[5], (H * HD, D), jnp.float32) * w_std, 'ln1_g': jnp.ones((D,), jnp.float32), 'ln1_b': jnp.zeros((D,), jnp.float32), 'ln2_g': jnp.ones((D,), jnp.float32), 'ln2_b': jnp.zeros((D,), jnp.float32), 'sel_w': jax.random.normal(ks[6], (D, E), jnp.float32) / np.sqrt(D), 'keys': jax.random.normal(ks[7], (E, D, ES), jnp.float32) * w_std, 'values': jax.random.normal(ks[8], (E, ES, D), jnp.float32) * (std_scale / np.sqrt(ES))}
    _L1_ffn_all = _L1_ffn_setup()
    _L1_ffn_in = {k: v for k, v in _L1_ffn_all.items() if k in ('wq', 'wk', 'wv', 'wp', 'wo', 'ln1_g', 'ln1_b', 'ln2_g', 'ln2_b', 'sel_w', 'keys', 'values')}
    del _L1_ffn_all

    def _L2_xattn_setup():
        import jax, jax.numpy as jnp
        import numpy as np
        M = 128
        N = 128
        B, S = (4, 256)
        key = jax.random.key(seed)
        ks = jax.random.split(key, 7)
        scale = 1.0 / np.sqrt(M)
        q = jax.random.normal(ks[0], (B, S, M), dtype=jnp.float32)
        k = jax.random.normal(ks[1], (B, S, M), dtype=jnp.float32)
        v = jax.random.normal(ks[2], (B, S, N), dtype=jnp.float32)
        causal = jnp.tril(jnp.ones((S, S), dtype=bool))
        attn_mask = jnp.where(causal, 0.0, -1000000000.0).astype(jnp.float32)
        Wq = jax.random.normal(ks[3], (N, M), dtype=jnp.float32) * scale
        Wk = jax.random.normal(ks[4], (N, M), dtype=jnp.float32) * scale
        Wv = jax.random.normal(ks[5], (N, N), dtype=jnp.float32) * scale
        bv = jax.random.normal(ks[6], (N,), dtype=jnp.float32) * scale
        return {'q': q, 'k': k, 'v': v, 'attn_mask': attn_mask, 'Wq': Wq, 'Wk': Wk, 'Wv': Wv, 'bv': bv}
    _L2_xattn_all = _L2_xattn_setup()
    _L2_xattn_in = {k: v for k, v in _L2_xattn_all.items() if k in ('Wq', 'Wk', 'Wv', 'bv')}
    del _L2_xattn_all

    def _L2_ffn_setup():
        import jax, jax.numpy as jnp
        import numpy as np
        ALPHA = 1.0
        key = jax.random.key(seed)
        ks = jax.random.split(key, 7)
        B, S, IN, OUT = (8, 1024, 128, 128)
        RANK, DDIM, UDIM = (4, 100, 50)
        return {'hidden_states': jax.random.normal(ks[0], (B, S, IN), dtype=jnp.float32), 'W': jax.random.normal(ks[1], (OUT, IN), dtype=jnp.float32) * 0.02, 'b': jax.random.normal(ks[2], (OUT,), dtype=jnp.float32) * 0.02, 'lora_down': jax.random.normal(ks[3], (RANK, DDIM), dtype=jnp.float32) * 0.1, 'lora_up': jax.random.normal(ks[4], (UDIM, RANK), dtype=jnp.float32) * 0.1, 'down_aux': jax.random.normal(ks[5], (DDIM, IN), dtype=jnp.float32) * 0.03, 'up_aux': jax.random.normal(ks[6], (OUT, UDIM), dtype=jnp.float32) * 0.03}
    _L2_ffn_all = _L2_ffn_setup()
    _L2_ffn_in = {k: v for k, v in _L2_ffn_all.items() if k in ('W', 'b', 'lora_down', 'lora_up', 'down_aux', 'up_aux')}
    del _L2_ffn_all

    def _L3_xattn_setup():
        import jax, jax.numpy as jnp
        import numpy as np
        D_MODEL = 128
        HEADS = 16
        D_K = D_MODEL // HEADS
        B, S = (4, 256)
        key = jax.random.key(seed)
        ks = jax.random.split(key, 12)
        xav = float(np.sqrt(6.0 / (D_MODEL + D_MODEL)))
        inp = {'query': jax.random.normal(ks[0], (B, S, D_MODEL), jnp.float32), 'key': jax.random.normal(ks[1], (B, S, D_MODEL), jnp.float32), 'value': jax.random.normal(ks[2], (B, S, D_MODEL), jnp.float32), 'mask': jnp.tril(jnp.ones((S, S), jnp.int32))[None, None], 'Wq': jax.random.uniform(ks[3], (D_MODEL, D_MODEL), jnp.float32, -xav, xav), 'bq': jnp.zeros((D_MODEL,), jnp.float32), 'Wk': jax.random.uniform(ks[4], (D_MODEL, D_MODEL), jnp.float32, -xav, xav), 'bk': jnp.zeros((D_MODEL,), jnp.float32), 'Wv': jax.random.uniform(ks[5], (D_MODEL, D_MODEL), jnp.float32, -xav, xav), 'bv': jnp.zeros((D_MODEL,), jnp.float32), 'Wo': jax.random.uniform(ks[6], (D_MODEL, D_MODEL), jnp.float32, -xav, xav), 'bo': jnp.zeros((D_MODEL,), jnp.float32)}
        return inp
    _L3_xattn_all = _L3_xattn_setup()
    _L3_xattn_in = {k: v for k, v in _L3_xattn_all.items() if k in ('Wq', 'bq', 'Wk', 'bk', 'Wv', 'bv', 'Wo', 'bo')}
    del _L3_xattn_all

    def _L3_ffn_setup():
        import jax, jax.numpy as jnp
        import numpy as np

        def _bitlinear(x, w_latent):
            scale = jax.lax.stop_gradient(jnp.clip(jnp.mean(jnp.abs(w_latent), axis=1, keepdims=True), 1e-05, None))
            tern = jnp.clip(jnp.round(w_latent / scale), -1.0, 1.0)
            w = w_latent + jax.lax.stop_gradient(tern - w_latent)
            return x @ (w * scale).T
        key = jax.random.key(seed)
        ks = jax.random.split(key, 6)
        dim, hidden, rank = (128, 512, 16)
        B, S = (4, 512)
        x = jax.random.normal(ks[0], (B, S, dim), dtype=jnp.float32)
        w_fc = 0.02 * jax.random.normal(ks[1], (hidden, dim), dtype=jnp.float32)
        w_proj = 0.02 * jax.random.normal(ks[2], (dim, hidden), dtype=jnp.float32)
        u = 0.02 * jax.random.normal(ks[3], (hidden, rank), dtype=jnp.float32)
        v = 0.02 * jax.random.normal(ks[4], (rank, dim), dtype=jnp.float32)
        fast_b = jax.random.normal(ks[5], (rank, rank), dtype=jnp.float32)
        gate = jnp.float32(0.05)
        return {'x': x, 'fast_b': fast_b, 'w_fc': w_fc, 'w_proj': w_proj, 'u': u, 'v': v, 'gate': gate}
    _L3_ffn_all = _L3_ffn_setup()
    _L3_ffn_in = {k: v for k, v in _L3_ffn_all.items() if k in ('fast_b', 'w_fc', 'w_proj', 'u', 'v', 'gate')}
    del _L3_ffn_all
    return {'x': x, 'ctx_1024': ctx_1024, 'fside_BxSxS2_0': fside_BxSxS2_0, 'mask_BxSxS2_ik1': mask_BxSxS2_ik1, 'mask_SxS2_fk0': mask_SxS2_fk0, 'mask_1x1xSxS2_ik0': mask_1x1xSxS2_ik0, 'L0_xattn_gamma_media': _L0_xattn_in['gamma_media'], 'L0_xattn_beta_media': _L0_xattn_in['beta_media'], 'L0_xattn_gamma_lat': _L0_xattn_in['gamma_lat'], 'L0_xattn_beta_lat': _L0_xattn_in['beta_lat'], 'L0_xattn_Wq': _L0_xattn_in['Wq'], 'L0_xattn_bq': _L0_xattn_in['bq'], 'L0_xattn_Wkv': _L0_xattn_in['Wkv'], 'L0_xattn_bkv': _L0_xattn_in['bkv'], 'L0_xattn_Wo': _L0_xattn_in['Wo'], 'L0_xattn_bo': _L0_xattn_in['bo'], 'L0_ffn_gate_w': _L0_ffn_in['gate_w'], 'L0_ffn_gate_b': _L0_ffn_in['gate_b'], 'L0_ffn_ew1': _L0_ffn_in['ew1'], 'L0_ffn_ew3': _L0_ffn_in['ew3'], 'L0_ffn_ew2': _L0_ffn_in['ew2'], 'L0_ffn_sw1': _L0_ffn_in['sw1'], 'L0_ffn_sw3': _L0_ffn_in['sw3'], 'L0_ffn_sw2': _L0_ffn_in['sw2'], 'L1_xattn_wq_k': _L1_xattn_in['wq_k'], 'L1_xattn_wq_b': _L1_xattn_in['wq_b'], 'L1_xattn_wk_k': _L1_xattn_in['wk_k'], 'L1_xattn_wk_b': _L1_xattn_in['wk_b'], 'L1_xattn_wv_k': _L1_xattn_in['wv_k'], 'L1_xattn_wv_b': _L1_xattn_in['wv_b'], 'L1_xattn_wo_k': _L1_xattn_in['wo_k'], 'L1_xattn_wo_b': _L1_xattn_in['wo_b'], 'L1_ffn_wq': _L1_ffn_in['wq'], 'L1_ffn_wk': _L1_ffn_in['wk'], 'L1_ffn_wv': _L1_ffn_in['wv'], 'L1_ffn_wp': _L1_ffn_in['wp'], 'L1_ffn_wo': _L1_ffn_in['wo'], 'L1_ffn_ln1_g': _L1_ffn_in['ln1_g'], 'L1_ffn_ln1_b': _L1_ffn_in['ln1_b'], 'L1_ffn_ln2_g': _L1_ffn_in['ln2_g'], 'L1_ffn_ln2_b': _L1_ffn_in['ln2_b'], 'L1_ffn_sel_w': _L1_ffn_in['sel_w'], 'L1_ffn_keys': _L1_ffn_in['keys'], 'L1_ffn_values': _L1_ffn_in['values'], 'L2_xattn_Wq': _L2_xattn_in['Wq'], 'L2_xattn_Wk': _L2_xattn_in['Wk'], 'L2_xattn_Wv': _L2_xattn_in['Wv'], 'L2_xattn_bv': _L2_xattn_in['bv'], 'L2_ffn_W': _L2_ffn_in['W'], 'L2_ffn_b': _L2_ffn_in['b'], 'L2_ffn_lora_down': _L2_ffn_in['lora_down'], 'L2_ffn_lora_up': _L2_ffn_in['lora_up'], 'L2_ffn_down_aux': _L2_ffn_in['down_aux'], 'L2_ffn_up_aux': _L2_ffn_in['up_aux'], 'L3_xattn_Wq': _L3_xattn_in['Wq'], 'L3_xattn_bq': _L3_xattn_in['bq'], 'L3_xattn_Wk': _L3_xattn_in['Wk'], 'L3_xattn_bk': _L3_xattn_in['bk'], 'L3_xattn_Wv': _L3_xattn_in['Wv'], 'L3_xattn_bv': _L3_xattn_in['bv'], 'L3_xattn_Wo': _L3_xattn_in['Wo'], 'L3_xattn_bo': _L3_xattn_in['bo'], 'L3_ffn_fast_b': _L3_ffn_in['fast_b'], 'L3_ffn_w_fc': _L3_ffn_in['w_fc'], 'L3_ffn_w_proj': _L3_ffn_in['w_proj'], 'L3_ffn_u': _L3_ffn_in['u'], 'L3_ffn_v': _L3_ffn_in['v'], 'L3_ffn_gate': _L3_ffn_in['gate']}

def reference(x, ctx_1024, fside_BxSxS2_0, mask_BxSxS2_ik1, mask_SxS2_fk0, mask_1x1xSxS2_ik0, L0_xattn_gamma_media, L0_xattn_beta_media, L0_xattn_gamma_lat, L0_xattn_beta_lat, L0_xattn_Wq, L0_xattn_bq, L0_xattn_Wkv, L0_xattn_bkv, L0_xattn_Wo, L0_xattn_bo, L0_ffn_gate_w, L0_ffn_gate_b, L0_ffn_ew1, L0_ffn_ew3, L0_ffn_ew2, L0_ffn_sw1, L0_ffn_sw3, L0_ffn_sw2, L1_xattn_wq_k, L1_xattn_wq_b, L1_xattn_wk_k, L1_xattn_wk_b, L1_xattn_wv_k, L1_xattn_wv_b, L1_xattn_wo_k, L1_xattn_wo_b, L1_ffn_wq, L1_ffn_wk, L1_ffn_wv, L1_ffn_wp, L1_ffn_wo, L1_ffn_ln1_g, L1_ffn_ln1_b, L1_ffn_ln2_g, L1_ffn_ln2_b, L1_ffn_sel_w, L1_ffn_keys, L1_ffn_values, L2_xattn_Wq, L2_xattn_Wk, L2_xattn_Wv, L2_xattn_bv, L2_ffn_W, L2_ffn_b, L2_ffn_lora_down, L2_ffn_lora_up, L2_ffn_down_aux, L2_ffn_up_aux, L3_xattn_Wq, L3_xattn_bq, L3_xattn_Wk, L3_xattn_bk, L3_xattn_Wv, L3_xattn_bv, L3_xattn_Wo, L3_xattn_bo, L3_ffn_fast_b, L3_ffn_w_fc, L3_ffn_w_proj, L3_ffn_u, L3_ffn_v, L3_ffn_gate):
    import jax
    import jax.numpy as jnp

    def _L0_xattn_ref(x, latents, gamma_media, beta_media, gamma_lat, beta_lat, Wq, bq, Wkv, bkv, Wo, bo):
        import jax, jax.numpy as jnp
        import numpy as np
        B, M, N, DIM, DH, H = (8, 512, 64, 128, 128, 8)
        INNER = DH * H
        EPS = 1e-05

        def _layernorm(x, g, b):
            mu = jnp.mean(x, axis=-1, keepdims=True)
            var = jnp.var(x, axis=-1, keepdims=True)
            return (x - mu) * jax.lax.rsqrt(var + EPS) * g + b
        b = x.shape[0]
        xn = _layernorm(x, gamma_media, beta_media)
        ln = _layernorm(latents, gamma_lat, beta_lat)
        q = ln @ Wq + bq
        kv_input = jnp.concatenate([xn, ln], axis=1)
        kv = kv_input @ Wkv + bkv
        k, v = jnp.split(kv, 2, axis=-1)

        def to_heads(t):
            return t.reshape(b, t.shape[1], H, DH).transpose(0, 2, 1, 3)
        q, k, v = (to_heads(q), to_heads(k), to_heads(v))
        q = q * DH ** (-0.5)
        sim = jnp.einsum('bhid,bhjd->bhij', q, k)
        attn = jax.nn.softmax(sim, axis=-1)
        out = jnp.einsum('bhij,bhjd->bhid', attn, v)
        out = out.transpose(0, 2, 1, 3).reshape(b, -1, INNER)
        return out @ Wo + bo

    def _L0_ffn_ref(x, gate_w, gate_b, ew1, ew3, ew2, sw1, sw3, sw2):
        import math
        import jax, jax.numpy as jnp
        import numpy as np
        B, T, D, H, E, K, S = (4, 512, 128, 256, 16, 2, 2)
        ROUTE_SCALE = 1.0

        def _swiglu(x, w1, w3, w2):
            return jax.nn.silu(x @ w1) * (x @ w3) @ w2
        Bx, Tx, Dx = x.shape
        flat = x.reshape(-1, Dx)
        N = flat.shape[0]
        n_experts = gate_w.shape[1]
        logits = flat @ gate_w
        scores = jax.nn.softmax(logits.astype(jnp.float32), -1) + gate_b
        _, topi = jax.lax.top_k(scores, K)
        weights = jnp.take_along_axis(logits, topi, axis=-1) * ROUTE_SCALE
        weights = weights.astype(flat.dtype)
        capacity = math.ceil(N * K / n_experts * 1.25)

        def per_expert(gid, w1, w3, w2):
            match = topi == gid
            assigned = match.any(-1)
            w_tok = jnp.sum(jnp.where(match, weights, 0.0), -1)
            wm = jnp.where(assigned, w_tok, -jnp.inf)
            vals, idx = jax.lax.top_k(wm, capacity)
            valid = assigned[idx]
            xs = flat[idx]
            y = _swiglu(xs, w1, w3, w2) * jnp.where(valid, vals, 0.0)[:, None]
            return (idx, y)
        idxs, ys = jax.vmap(per_expert)(jnp.arange(n_experts), ew1, ew3, ew2)
        out = jnp.zeros_like(flat).at[idxs.reshape(-1)].add(ys.reshape(-1, Dx))
        shared = jax.vmap(lambda w1, w3, w2: _swiglu(flat, w1, w3, w2))(sw1, sw3, sw2)
        out = out + shared.mean(0)
        return out.reshape(Bx, Tx, Dx)

    def _L1_xattn_ref(query, key_in, value, group_prob, mask, wq_k, wq_b, wk_k, wk_b, wv_k, wv_b, wo_k, wo_b):
        import jax, jax.numpy as jnp
        import numpy as np
        NUM_HEADS = 16
        HIDDEN = 128
        B, S = (2, 256)

        def _split_heads(x, H):
            b, s, d = x.shape
            return x.reshape(b, s, H, d // H).transpose(0, 2, 1, 3)
        H = NUM_HEADS
        dh = query.shape[-1] // H
        q = _split_heads(query @ wq_k + wq_b, H)
        k = _split_heads(key_in @ wk_k + wk_b, H)
        v = _split_heads(value @ wv_k + wv_b, H)
        logits = jnp.einsum('bhqd,bhkd->bhqk', q, k) / jnp.sqrt(jnp.asarray(dh, q.dtype))
        neg = (1.0 - mask.astype(q.dtype)) * -1000000000.0
        logits = logits + neg[:, None, :, :]
        attn = jax.nn.softmax(logits, axis=-1)
        attn = attn * group_prob[:, None, :, :]
        out = jnp.einsum('bhqk,bhkd->bhqd', attn, v)
        out = out.transpose(0, 2, 1, 3).reshape(query.shape[0], -1, H * dh)
        return out @ wo_k + wo_b

    def _L1_ffn_ref(src, wq, wk, wv, wp, wo, ln1_g, ln1_b, ln2_g, ln2_b, sel_w, keys, values):
        import jax, jax.numpy as jnp
        import numpy as np
        D = 128
        H = 16
        HD = D // H
        E = 32
        ES = 128
        K = 4
        B, S = (2, 128)
        ROPE_BASE = 10000.0

        def _layernorm(x, g, b):
            m = x.mean(-1, keepdims=True)
            v = ((x - m) ** 2).mean(-1, keepdims=True)
            return (x - m) * jax.lax.rsqrt(v + 1e-05) * g + b

        def _forward(src, wq, wk, wv, wp, wo, ln1_g, ln1_b, ln2_g, ln2_b, sel_w, keys, values):
            Bs, Ss, Ds = src.shape
            scale = 1.0 / jnp.sqrt(jnp.array(HD, dtype=src.dtype))
            x = _layernorm(src, ln1_g, ln1_b)
            q = (x @ wq).reshape(Bs, Ss, H, HD)
            k = (x @ wk).reshape(Bs, Ss, H, HD)
            v = (x @ wv).reshape(Bs, Ss, H, HD)
            pos = jnp.arange(Ss - 1, -Ss, -1, dtype=src.dtype)
            inv_freq = 1.0 / ROPE_BASE ** (jnp.arange(0, Ds, 2, dtype=src.dtype) / Ds)
            ang = pos[:, None] * inv_freq[None, :]
            pe = jnp.concatenate([jnp.sin(ang), jnp.cos(ang)], axis=-1)
            p = (pe @ wp).reshape(2 * Ss - 1, H, HD)
            ac = jnp.einsum('bihd,bjhd->bhij', q, k)
            bd_full = jnp.einsum('bihd,phd->bhip', q, p)
            rel = jnp.arange(Ss)[:, None] - jnp.arange(Ss)[None, :] + (Ss - 1)
            bd = bd_full[:, :, jnp.arange(Ss)[:, None], rel]
            att = jax.nn.softmax((ac + bd) * scale, axis=-1)
            attn_out = jnp.einsum('bhij,bjhd->bihd', att, v).reshape(Bs, Ss, Ds) @ wo
            src = src + attn_out
            x2 = _layernorm(src, ln2_g, ln2_b)
            sel = jax.nn.sigmoid(x2 @ sel_w)
            scores, idx = jax.lax.top_k(sel, K)
            gate = (jax.nn.one_hot(idx, E, dtype=sel.dtype) * scores[..., None]).sum(-2)
            h = jax.nn.relu(jnp.einsum('bsd,edh->bseh', x2, keys))
            moe_out = jnp.einsum('bseh,ehd,bse->bsd', h, values, gate)
            return src + moe_out
        return _forward(src, wq, wk, wv, wp, wo, ln1_g, ln1_b, ln2_g, ln2_b, sel_w, keys, values)

    def _L2_xattn_ref(q, k, v, attn_mask, Wq, Wk, Wv, bv):
        import jax, jax.numpy as jnp
        import numpy as np
        M = 128
        N = 128
        B, S = (4, 256)
        qp = jnp.einsum('bsm,nm->bsn', q, Wq)
        kp = jnp.einsum('bsm,nm->bsn', k, Wk)
        vp = jnp.einsum('bsn,on->bso', v, Wv) + bv
        scores = jnp.einsum('bqn,bkn->bqk', qp, kp) / jnp.sqrt(jnp.float32(N))
        scores = scores + attn_mask
        w = jax.nn.softmax(scores, axis=-1)
        return jnp.einsum('bqk,bkn->bqn', w, vp)

    def _L2_ffn_ref(hidden_states, W, b, lora_down, lora_up, down_aux, up_aux):
        import jax, jax.numpy as jnp
        import numpy as np
        ALPHA = 1.0
        lilora_weight = up_aux @ (lora_up @ (lora_down @ down_aux))
        base = jnp.einsum('bsi,oi->bso', hidden_states, W) + b
        delta = jnp.einsum('bsi,oi->bso', hidden_states, lilora_weight)
        return base + ALPHA * delta

    def _L3_xattn_ref(query, key, value, mask, Wq, bq, Wk, bk, Wv, bv, Wo, bo):
        import jax, jax.numpy as jnp
        import numpy as np
        D_MODEL = 128
        HEADS = 16
        D_K = D_MODEL // HEADS
        B, S = (4, 256)
        b, s, d = query.shape
        Q = (jnp.einsum('bsd,ed->bse', query, Wq) + bq).reshape(b, s, HEADS, D_K).transpose(0, 2, 1, 3)
        K = (jnp.einsum('bsd,ed->bse', key, Wk) + bk).reshape(b, -1, HEADS, D_K).transpose(0, 2, 1, 3)
        V = (jnp.einsum('bsd,ed->bse', value, Wv) + bv).reshape(b, -1, HEADS, D_K).transpose(0, 2, 1, 3)
        scale = 1.0 / jnp.sqrt(jnp.asarray(D_K, query.dtype))
        scores = jnp.einsum('bhqd,bhkd->bhqk', Q, K) * scale
        scores = jnp.where(mask == 0, -jnp.inf, scores)
        attn = jax.nn.softmax(scores, axis=-1)
        attn = jnp.where(jnp.isnan(attn), jnp.zeros_like(attn), attn)
        out = jnp.einsum('bhqk,bhkd->bhqd', attn, V)
        out = out.transpose(0, 2, 1, 3).reshape(b, s, d)
        return jnp.einsum('bsd,ed->bse', out, Wo) + bo

    def _L3_ffn_ref(x, fast_b, w_fc, w_proj, u, v, gate):
        import jax, jax.numpy as jnp
        import numpy as np

        def _bitlinear(x, w_latent):
            scale = jax.lax.stop_gradient(jnp.clip(jnp.mean(jnp.abs(w_latent), axis=1, keepdims=True), 1e-05, None))
            tern = jnp.clip(jnp.round(w_latent / scale), -1.0, 1.0)
            w = w_latent + jax.lax.stop_gradient(tern - w_latent)
            return x @ (w * scale).T
        h = _bitlinear(x, w_fc) + gate * (x @ v.T @ fast_b.T @ u.T)
        r = jnp.maximum(h, 0.0)
        return _bitlinear(r * r, w_proj)
    x = x + _L0_xattn_ref(ctx_1024, _layernorm(x, axis=-1), L0_xattn_gamma_media, L0_xattn_beta_media, L0_xattn_gamma_lat, L0_xattn_beta_lat, L0_xattn_Wq, L0_xattn_bq, L0_xattn_Wkv, L0_xattn_bkv, L0_xattn_Wo, L0_xattn_bo)
    x = x + _L0_ffn_ref(_layernorm(x, axis=-1), L0_ffn_gate_w, L0_ffn_gate_b, L0_ffn_ew1, L0_ffn_ew3, L0_ffn_ew2, L0_ffn_sw1, L0_ffn_sw3, L0_ffn_sw2)
    x = x + _L1_xattn_ref(_layernorm(x, axis=-1), ctx_1024, ctx_1024, fside_BxSxS2_0, mask_BxSxS2_ik1, L1_xattn_wq_k, L1_xattn_wq_b, L1_xattn_wk_k, L1_xattn_wk_b, L1_xattn_wv_k, L1_xattn_wv_b, L1_xattn_wo_k, L1_xattn_wo_b)
    x = x + _L1_ffn_ref(_layernorm(x, axis=-1), L1_ffn_wq, L1_ffn_wk, L1_ffn_wv, L1_ffn_wp, L1_ffn_wo, L1_ffn_ln1_g, L1_ffn_ln1_b, L1_ffn_ln2_g, L1_ffn_ln2_b, L1_ffn_sel_w, L1_ffn_keys, L1_ffn_values)
    x = x + _L2_xattn_ref(_layernorm(x, axis=-1), ctx_1024, ctx_1024, mask_SxS2_fk0, L2_xattn_Wq, L2_xattn_Wk, L2_xattn_Wv, L2_xattn_bv)
    x = x + _L2_ffn_ref(_layernorm(x, axis=-1), L2_ffn_W, L2_ffn_b, L2_ffn_lora_down, L2_ffn_lora_up, L2_ffn_down_aux, L2_ffn_up_aux)
    x = x + _L3_xattn_ref(_layernorm(x, axis=-1), ctx_1024, ctx_1024, mask_1x1xSxS2_ik0, L3_xattn_Wq, L3_xattn_bq, L3_xattn_Wk, L3_xattn_bk, L3_xattn_Wv, L3_xattn_bv, L3_xattn_Wo, L3_xattn_bo)
    x = x + _L3_ffn_ref(_layernorm(x, axis=-1), L3_ffn_fast_b, L3_ffn_w_fc, L3_ffn_w_proj, L3_ffn_u, L3_ffn_v, L3_ffn_gate)
    return x

_drawn_inputs = setup_inputs


def setup_inputs(seed=0):
    import zlib

    import numpy as np

    out = dict(_drawn_inputs(seed))
    spreads = {'L0_xattn_gamma_media': (1.0, 0.6),
     'L0_xattn_beta_media': (0.0, 0.8),
     'L0_xattn_gamma_lat': (1.0, 0.6),
     'L0_xattn_beta_lat': (0.0, 0.561),
     'L0_xattn_bq': (0.0, 0.8),
     'L0_xattn_bkv': (0.0, 0.1),
     'L0_xattn_bo': (0.0, 0.1),
     'L0_ffn_gate_b': (0.0, 0.8),
     'L1_xattn_wq_b': (0.0, 1.878),
     'L1_xattn_wk_b': (0.0, 2.0),
     'L1_xattn_wv_b': (0.0, 0.645),
     'L1_xattn_wo_b': (0.0, 0.282),
     'L1_ffn_ln1_g': (1.0, 0.6),
     'L1_ffn_ln1_b': (0.0, 0.8),
     'L1_ffn_ln2_g': (1.0, 0.6),
     'L1_ffn_ln2_b': (0.0, 1.831),
     'L3_xattn_bq': (0.0, 2.0),
     'L3_xattn_bk': (0.0, 2.0),
     'L3_xattn_bv': (0.0, 0.8),
     'L3_xattn_bo': (0.0, 0.8)}
    factors = {'L0_xattn_Wq': 8.0,
     'L0_ffn_gate_w': 8.0,
     'L0_ffn_ew1': 8.0,
     'L0_ffn_ew3': 8.0,
     'L0_ffn_ew2': 8.0,
     'L0_ffn_sw1': 8.0,
     'L0_ffn_sw3': 7.56,
     'L0_ffn_sw2': 7.574,
     'L1_ffn_wq': 8.0,
     'L1_ffn_wk': 8.0,
     'L1_ffn_wv': 3.163,
     'L1_ffn_wp': 8.0,
     'L1_ffn_wo': 3.092,
     'L2_ffn_b': 50.6,
     'L2_ffn_lora_down': 8.0,
     'L2_ffn_lora_up': 8.0,
     'L2_ffn_down_aux': 8.0,
     'L2_ffn_up_aux': 8.0,
     'L3_ffn_fast_b': 8.0,
     'L3_ffn_w_fc': 8.0,
     'L3_ffn_w_proj': 8.0,
     'L3_ffn_u': 8.0,
     'L3_ffn_v': 8.0,
     'fside_BxSxS2_0': 3.617,
     'L1_ffn_sel_w': 3.232,
     'L1_ffn_keys': 3.652,
     'L1_ffn_values': 3.175,
     'L2_xattn_bv': 8.0,
     'L2_ffn_W': 8.0,
     'L3_xattn_Wq': 8.0,
     'L3_xattn_Wk': 8.0,
     'L3_xattn_Wv': 5.603,
     'L3_xattn_Wo': 5.653}
    for name, (base, spread) in spreads.items():
        noise = np.random.default_rng([zlib.crc32(name.encode()), seed]).standard_normal(out[name].shape)
        drawn = base * np.exp(spread * noise) if base else spread * noise
        out[name] = jnp.asarray(drawn.astype(out[name].dtype))
    for name, factor in factors.items():
        out[name] = (out[name] * factor).astype(out[name].dtype)
    return out
```

```python
from contextlib import ExitStack

import concourse.bass as bass
import numpy as np
from concourse import mybir

F32 = mybir.dt.float32
BF16 = mybir.dt.bfloat16
I32 = mybir.dt.int32
U32 = mybir.dt.uint32
ALU = mybir.AluOpType
ACT = mybir.ActivationFunctionType
AX_X = mybir.AxisListType.X

P = 128
D = 128
B = 4
S = 512
TB = S // P
NT = B * TB
NTOK = B * S
SC = 154
TAIL = SC - P
H16 = 16
DH = D // H16
E0, K0, HID0, S0 = 16, 2, 256, 2
CAP = -(-NTOK * K0 * 5 // (E0 * 4))
E1, K1 = 32, 4
HID3 = 512
SLOTS = E0 * CAP
MAG_BITS = 31
HUGE = 1.0e38
EPS = 1e-5


def ds(i, n=P):
    return bass.ds(i * n, n)


class Steps:

    def __init__(self, eng, sem):
        self.eng, self.sem, self.start, self.index, self.per, self.n = eng, sem, 0, None, 0, 0

    def then(self, ins):
        self.n += 1
        ins.then_inc(self.sem, 1)
        at = self.start + self.n
        self.eng.wait_ge(self.sem, at if self.index is None else self.index * self.per + at)
        return ins

    def turn(self, index, per):
        self.start, self.index, self.per, self.n = self.start + self.n if self.index is None else self.start, index, per, 0

    def turns_end(self, turns):
        assert self.n == self.per, (self.n, self.per)
        self.start, self.index, self.n = self.start + turns * self.per, None, 0


def free_at_first(eng, *sems, by=1):
    for s in sems:
        eng.sem_inc(s, by)


class Scope(ExitStack):

    def __init__(self, k):
        super().__init__()
        self.nc, self.sems = k.nc, []

    def __exit__(self, *error):
        if error[0] is None:
            numbers = sorted(s.num for s in self.sems)
            while numbers:
                run = next((i for i in range(1, len(numbers)) if numbers[i] != numbers[i - 1] + 1), len(numbers))
                self.nc.all_engine_barrier(sems_to_clear=range(numbers[0], numbers[run - 1] + 1))
                numbers = numbers[run:]
        return super().__exit__(*error)


class Core:

    def __init__(self, nc, ctx, dram):
        self.nc, self.dram, self.ctx = nc, dram, ctx
        self.x = self.sb("x_rows", [P, NT * D])
        self.xT = self.sb("xn_cols", [P, NTOK])
        self.norm = self.sb("norm_tile", [P, TB, D])
        self.stats = self.sb("bn_stats_out", [P, NT * 6])
        self.mv = self.sb("mean_var", [P, NT, 2])
        self.rstd = self.sb("rstd", [P, 4, NT])
        self.ident = self.sb("identity", [P, P])
        self.headmask = self.sb("headmask", [P, H16])
        self.ctxT = self.sb("ctx_cols", [P, B * SC])
        self.psum = ctx.enter_context(nc.psum_tensor("psum", [P, 8, 512], F32))
        self.bank = [self.psum[:, i, :] for i in range(8)]
        self.norms = 0
        self.ln_order = self.sem("ln_order")
        self.ln_var = self.sem("ln_var")
        self.ln_sqrt = self.sem("ln_sqrt")
        self.ln_normed = self.sem("ln_normed")
        self.ln_turned = self.sem("ln_turned")
        self.ln_stored = self.sem("ln_stored")
        self.ln_steps = 0

    def sb(self, name, shape, dt=F32, ctx=None):
        return (ctx or self.ctx).enter_context(self.nc.sbuf_tensor(name, shape, dt))

    def sem(self, name, ctx=None):
        s = (ctx or self.ctx).enter_context(self.nc.semaphore(name))
        if ctx is not None:
            ctx.sems.append(s)
        return s


def load(k, ctx, name, parts=P):
    return k.sb(name, [parts, k.dram[name].shape[1]], F32, ctx)


def fetch(k, pairs, ctx):
    nc = k.nc
    done = k.sem("fetched_" + pairs[0][0], ctx)
    with nc.Block() as block:
        @block.sync
        def _(sp):
            for name, home in pairs:
                sp.dma_start(home[:], k.dram[name]).then_inc(done, 16)
            sp.wait_ge(done, 16 * len(pairs))


def normalize(k, src, gain=None, bias=None, rows=None):
    nc = k.nc
    n, k.norms = k.norms, k.norms + 1
    steps0 = k.ln_steps
    NEWTON = 4
    k.ln_steps += 3 + NEWTON + 1
    r = k.rstd
    with nc.Block() as block:
        @block.vector
        def _(dve):
            step = Steps(dve, k.ln_order)
            step.start = steps0
            with dve.Fori(0, NT) as T:
                last = nc.vector.bn_stats(k.stats[:, ds(T, 6)], src[:, ds(T)])
            step.then(nc.vector.memset(r[:, 3, :], 1.0))
            for T in range(NT):
                nc.vector.bn_aggr(k.mv[:, T, :], k.stats[:, ds(T, 6)])
            step.then(nc.vector.memset(r[:, 3, :], 1.0))
            nc.vector.tensor_scalar(r[:, 0, :], k.mv[:, :, 1], EPS, None, ALU.add).then_inc(k.ln_var, 1)
            dve.wait_ge(k.ln_var, n + 1)
            dve.wait_ge(k.ln_sqrt, n + 1)
            step.then(nc.vector.reciprocal(r[:, 1, :], r[:, 1, :]))
            step.then(nc.vector.tensor_tensor(r[:, 2, :], r[:, 1, :], r[:, 1, :], ALU.mult))
            step.then(nc.vector.tensor_tensor(r[:, 2, :], r[:, 2, :], r[:, 0, :], ALU.mult))
            step.then(nc.vector.tensor_scalar(r[:, 2, :], r[:, 2, :], -0.5, 1.5, ALU.mult, ALU.add))
            step.then(nc.vector.tensor_tensor(r[:, 3, :], r[:, 2, :], r[:, 1, :], ALU.mult))
            step.then(nc.vector.memset(k.stats[:, 0:1], 0.0))
            with dve.Fori(0, B) as b:
                dve.wait_ge(k.ln_turned, n * B + b + 1)
                for j in range(TB):
                    T = b * TB + j
                    if rows is not None:
                        nc.vector.tensor_scalar(rows[:, ds(T)], src[:, ds(T)], k.mv[:, bass.ds(T, 1), 0],
                                                r[:, 3, bass.ds(T, 1)], ALU.subtract, ALU.mult)
                    nc.vector.tensor_scalar(k.norm[:, j, :], src[:, ds(T)], k.mv[:, bass.ds(T, 1), 0],
                                            r[:, 3, bass.ds(T, 1)], ALU.subtract,
                                            ALU.mult).then_inc(k.ln_normed, 1)

        @block.scalar
        def _(act):
            act.wait_ge(k.ln_var, n + 1)
            nc.scalar.activation(r[:, 1, :], r[:, 0, :], ACT.Sqrt).then_inc(k.ln_sqrt, 1)
            with act.Fori(0, B) as b:
                act.wait_ge(k.ln_turned, n * B + b + 2)
                if gain is None:
                    ins = nc.scalar.copy(k.xT[:, ds(b, S)], k.bank[0])
                else:
                    ins = nc.scalar.activation(k.xT[:, ds(b, S)], k.bank[0], ACT.Identity, scale=gain, bias=bias)
                ins.then_inc(k.ln_stored, 1)

        @block.tensor
        def _(pe):
            with pe.Fori(0, B) as b:
                pe.wait_ge(k.ln_stored, n * B + b + 1)
                for j in range(TB):
                    pe.wait_ge(k.ln_normed, n * NT + b * TB + j + 1)
                    ins = nc.tensor.transpose(k.bank[0][:, ds(j)], k.norm[:, j, :], k.ident[:])
                ins.then_inc(k.ln_turned, 1)


def first_hit(nc, step, left, hit, best, first, iota, far, shape):
    step.then(nc.vector.tensor_reduce(best[:], left[:], AX_X, ALU.max))
    step.then(nc.vector.tensor_tensor(hit[:], left[:], best[:, :, None].broadcast_to(shape), ALU.is_equal))
    step.then(nc.vector.scalar_tensor_tensor(hit[:], hit[:], -100.0, far[:, None, :].broadcast_to(shape), ALU.mult, ALU.add))
    step.then(nc.vector.tensor_reduce(first[:], hit[:], AX_X, ALU.min))
    step.then(nc.vector.tensor_tensor(hit[:], iota[:, None, :].broadcast_to(shape), first[:, :, None].broadcast_to(shape), ALU.is_equal))


def stage_0x(k):
    nc = k.nc
    H = 8
    KEYS = SC + S
    CHUNKS = -(-KEYS // P)
    LAST = KEYS - (CHUNKS - 1) * P
    HALF = KEYS // 2
    AHEAD = 2
    scale = P ** -0.5
    with Scope(k) as ctx:
        names = ("a0_ln", "a0_wq", "a0_bq", "a0_wkv", "a0_bkv", "a0_wo", "a0_bo")
        ln, wq, bq, wkv, bkv, wo, bo = homes = [load(k, ctx, n) for n in names]
        CT = 2 * B
        rows = k.sb("a0_ctx_rows", [P, CT, D], F32, ctx)
        cT = k.sb("a0_ctxT", [P, B * SC], F32, ctx)
        xn = k.sb("a0_xn", [P, NT * D], F32, ctx)
        fetched, rows_in = k.sem("a0_fetched", ctx), k.sem("a0_rows_in", ctx)
        with nc.Block() as block:
            @block.sync
            def _(sp):
                for n, home in zip(names, homes):
                    sp.dma_start(home[:], k.dram[n]).then_inc(fetched, 16)
                sp.wait_ge(fetched, 16 * len(names))

            @block.scalar
            def _(act):
                r = rows[:].rearrange("p (b c) d -> p b c d", c=2)
                act.dma_start(r[:, :, 0, :], k.dram["ctx"][:, 0:P, :].rearrange("b p d -> p b d")).then_inc(rows_in, 16)
                act.dma_start(r[0:TAIL, :, 1, :], k.dram["ctx"][:, P:SC, :].rearrange("b p d -> p b d")).then_inc(rows_in, 16)
                act.wait_ge(rows_in, 32)

        sizes = [(P, TAIL)[i % 2] for i in range(CT)]
        stats = k.sb("a0_ctx_stats", [P, CT, 6], F32, ctx)
        mv = k.sb("a0_ctx_mv", [P, CT, 2], F32, ctx)
        r = k.sb("a0_ctx_rstd", [P, 4, CT], F32, ctx)
        order, var, root, turned, stored = (k.sem(f"a0_ctx_{n}", ctx) for n in ("order", "var", "root", "turned", "stored"))
        with nc.Block() as block:
            @block.vector
            def _(dve):
                step = Steps(dve, order)
                nc.vector.memset(stats[:], 0.0)
                step.then(nc.vector.memset(mv[:], 1.0))
                for i, n in enumerate(sizes):
                    ins = nc.vector.bn_stats(stats[0:n, i, :], rows[0:n, i, :])
                step.then(ins)
                for i, n in enumerate(sizes):
                    ins = nc.vector.bn_aggr(mv[0:n, i, :], stats[0:n, i, :])
                step.then(ins)
                nc.vector.tensor_scalar(r[:, 0, :], mv[:, :, 1], EPS, None, ALU.add).then_inc(var, 1)
                dve.wait_ge(root, 1)
                step.then(nc.vector.reciprocal(r[:, 1, :], r[:, 1, :]))
                step.then(nc.vector.tensor_tensor(r[:, 2, :], r[:, 1, :], r[:, 1, :], ALU.mult))
                step.then(nc.vector.tensor_tensor(r[:, 2, :], r[:, 2, :], r[:, 0, :], ALU.mult))
                step.then(nc.vector.tensor_scalar(r[:, 2, :], r[:, 2, :], -0.5, 1.5, ALU.mult, ALU.add))
                step.then(nc.vector.tensor_tensor(r[:, 3, :], r[:, 2, :], r[:, 1, :], ALU.mult))
                for i, n in enumerate(sizes):
                    nc.vector.tensor_scalar(rows[0:n, i, :], rows[0:n, i, :], mv[0:n, i, 0:1], r[0:n, 3, i:i + 1],
                                            ALU.subtract, ALU.mult).then_inc(stored, 1)

            @block.scalar
            def _(act):
                act.wait_ge(var, 1)
                nc.scalar.activation(r[:, 1, :], r[:, 0, :], ACT.Sqrt).then_inc(root, 1)
                for b in range(B):
                    act.wait_ge(turned, b + 1)
                    nc.scalar.activation(cT[:, ds(b, SC)], k.bank[b][:, 0:SC], ACT.Identity, scale=ln[:, 0:1], bias=ln[:, 1:2])

            @block.tensor
            def _(pe):
                for i, n in enumerate(sizes):
                    pe.wait_ge(stored, i + 1)
                    ins = nc.tensor.transpose(k.bank[i // 2][:, (i % 2) * P:(i % 2) * P + n], rows[0:n, i, :], k.ident[0:n, 0:n])
                    if i % 2:
                        ins.then_inc(turned, 1)
        normalize(k, k.x, rows=xn)
        normalize(k, xn, ln[:, 2:3], ln[:, 3:4])

        kT = k.sb("a0_kT", [P, H, KEYS], F32, ctx)
        vT = k.sb("a0_vT", [P, 2, KEYS], F32, ctx)
        vo = k.sb("a0_vo", [P, CHUNKS, H, D], F32, ctx)
        qT = k.sb("a0_qT", [P, H, P], F32, ctx)
        probs = k.sb("a0_probs", [P, 2, KEYS], F32, ctx)
        probsT = k.sb("a0_probsT", [P, 2, CHUNKS, P], F32, ctx)
        small = k.sb("a0_small", [P, 4, H], F32, ctx)
        s = {n: k.sem(f"a0_{n}", ctx) for n in ("k_made", "k_taken", "v_made", "v_taken", "vo_made", "vo_taken", "q_made", "q_taken",
                                                "scored", "maxed", "exped", "turned", "copied_a", "copied_v", "mixed", "added",
                                                "order", "bias")}

        def tiles(eng, b):
            with eng.Fori(0, TB) as t:
                yield b * TB + t

        with nc.Block() as block:
            @block.tensor
            def _(pe):
                free_at_first(pe, s["vo_made"])
                with pe.Fori(0, B) as b:
                    def keys_values(h):
                        pe.wait_ge(s["k_taken"], b * H + h + 1)
                        nc.tensor.matmul(k.bank[0][:, 0:SC], wkv[:, ds(h)], cT[:, ds(b, SC)], start=True, stop=True)
                        nc.tensor.matmul(k.bank[1], wkv[:, ds(h)], k.xT[:, ds(b, S)], start=True, stop=True).then_inc(s["k_made"], 1)
                        pe.wait_ge(s["v_taken"], b * H + h + 1)
                        nc.tensor.matmul(k.bank[2][:, 0:SC], wkv[:, ds(H + h)], cT[:, ds(b, SC)], start=True, stop=True)
                        nc.tensor.matmul(k.bank[3], wkv[:, ds(H + h)], k.xT[:, ds(b, S)], start=True, stop=True).then_inc(s["v_made"], 1)

                    keys_values(0)
                    for h in range(H):
                        if h + 1 < H:
                            keys_values(h + 1)
                        pe.wait_ge(s["v_taken"], b * H + h + 2)
                        pe.wait_ge(s["vo_taken"], b * H + h + 1)
                        for c in range(CHUNKS):
                            n = P if c < CHUNKS - 1 else LAST
                            ins = nc.tensor.matmul(k.bank[4 + c // 4][0:n, ds(c % 4)], vT[:, h % 2, c * P:c * P + n], wo[:, ds(h)],
                                                   start=True, stop=True)
                        ins.then_inc(s["vo_made"], 1)
                    for T in tiles(pe, b):
                        pe.wait_ge(s["vo_taken"], b * H + H + 1)
                        pe.wait_ge(s["k_taken"], b * H + H + 1)
                        for h in range(H):
                            ins = nc.tensor.matmul(k.bank[4 + h // 4][:, ds(h % 4)], wq[:, ds(h)], k.xT[:, ds(T)], start=True, stop=True)
                        ins.then_inc(s["q_made"], 1)
                        pe.wait_ge(s["q_taken"], T + 1)

                        def score(h):
                            pe.wait_ge(s["exped"], T * H + h + 1)
                            for i in range(2):
                                ins = nc.tensor.matmul(k.bank[2 * (h % 2) + i][:, 0:HALF], qT[:, h, :], kT[:, h, ds(i, HALF)],
                                                       start=True, stop=True)
                            ins.then_inc(s["scored"], 1)

                        def mix(h):
                            pe.wait_ge(s["copied_a"], T * H + h + 2)
                            pe.wait_ge(s["copied_v"], T * H + h + 2)
                            pe.wait_ge(s["added"], T * H + h + 1)
                            for c in range(CHUNKS):
                                n = P if c < CHUNKS - 1 else LAST
                                ins = nc.tensor.matmul(k.bank[6 + h % 2][:, 0:D], probsT[0:n, h % 2, c, :], vo[0:n, c, h, :],
                                                       start=c == 0, stop=c == CHUNKS - 1)
                            ins.then_inc(s["mixed"], 1)

                        score(0)
                        for h in range(H):
                            if h + 1 < H:
                                score(h + 1)
                            pe.wait_ge(s["exped"], T * H + h + 1 + AHEAD)
                            pe.wait_ge(s["copied_a"], T * H + h + 1)
                            pe.wait_ge(s["copied_v"], T * H + h + 1)
                            for c in range(CHUNKS):
                                n = P if c < CHUNKS - 1 else LAST
                                ins = nc.tensor.transpose(k.bank[4 + c // 4][0:n, ds(c % 4)], probs[:, h % 2, c * P:c * P + n], k.ident[:])
                            ins.then_inc(s["turned"], 1)
                            if h > 0:
                                mix(h - 1)
                        mix(H - 1)

            @block.scalar
            def _(act):
                nc.scalar.copy(small[:, 2, :], k.ident[:, 0:H]).then_inc(s["exped"], AHEAD)
                free_at_first(act, s["k_taken"], s["vo_taken"], s["copied_a"])
                with act.Fori(0, B) as b:
                    for h in range(H):
                        act.wait_ge(s["k_made"], b * H + h + 1)
                        nc.scalar.activation(kT[:, h, 0:SC], k.bank[0][:, 0:SC], ACT.Identity, bias=bkv[:, h:h + 1])
                        nc.scalar.activation(kT[:, h, SC:KEYS], k.bank[1], ACT.Identity, bias=bkv[:, h:h + 1]).then_inc(s["k_taken"], 1)
                        act.wait_ge(s["vo_made"], b * H + h + 2)
                        nc.scalar.copy(vo[:, 0:4, h, :], k.bank[4].rearrange("p (c d) -> p c d", c=4))
                        nc.scalar.copy(vo[:, 4, h, :], k.bank[5][:, 0:D])
                        nc.scalar.copy(vo[0:LAST, 5, h, :], k.bank[5][0:LAST, ds(1)]).then_inc(s["vo_taken"], 1)
                    for T in tiles(act, b):
                        def exp(h):
                            act.wait_ge(s["maxed"], T * H + h + 1)
                            nc.scalar.activation(probs[:, h % 2, :].rearrange("p (i k) -> p i k", i=2), k.psum[:, 2 * (h % 2):2 * (h % 2) + 2, 0:HALF],
                                                 ACT.Exp, bias=small[:, 1, h:h + 1], scale=scale, accum_out=small[:, 2, h:h + 1]).then_inc(s["exped"], 1)

                        exp(0)
                        for h in range(H):
                            if h + 1 < H:
                                exp(h + 1)
                            act.wait_ge(s["turned"], T * H + h + 1)
                            nc.scalar.copy(probsT[:, h % 2, 0:4, :], k.bank[4].rearrange("p (c q) -> p c q", c=4)).then_inc(s["copied_a"], 1)

            @block.vector
            def _(dve):
                step = Steps(dve, s["order"])
                nc.vector.memset(small[:, 0, :], 0.0).then_inc(s["added"], AHEAD)
                free_at_first(dve, s["v_taken"], s["copied_v"])
                x = k.x[:].rearrange("p (t d) -> p t d", d=D)
                step.then(nc.vector.tensor_tensor(x, x, bo[:, None, :].broadcast_to([P, NT, D]), ALU.add))
                first = step.n
                with dve.Fori(0, B) as b:
                    for h in range(H):
                        dve.wait_ge(s["v_made"], b * H + h + 1)
                        dve.wait_ge(s["vo_made"], b * H + h + 1)
                        nc.vector.tensor_scalar(vT[:, h % 2, 0:SC], k.bank[2][:, 0:SC], bkv[:, H + h:H + h + 1], None, ALU.add)
                        nc.vector.tensor_scalar(vT[:, h % 2, SC:KEYS], k.bank[3], bkv[:, H + h:H + h + 1], None, ALU.add).then_inc(s["v_taken"], 1)
                    for T in tiles(dve, b):
                        step.start, step.index, step.per, step.n = first, T, 2 * H, 0
                        dve.wait_ge(s["q_made"], T + 1)
                        for i in range(2):
                            ins = nc.vector.tensor_tensor(qT[:, 4 * i:4 * i + 4, :], k.bank[4 + i].rearrange("p (h q) -> p h q", h=4),
                                                          bq[:, 4 * i:4 * i + 4, None].broadcast_to([P, 4, P]), ALU.add)
                        ins.then_inc(s["q_taken"], 1)

                        def maximum(h):
                            dve.wait_ge(s["scored"], T * H + h + 1)
                            step.then(nc.vector.tensor_reduce(small[:, 0, h:h + 1], k.psum[:, 2 * (h % 2):2 * (h % 2) + 2, 0:HALF],
                                                              mybir.AxisListType.XY, ALU.max, negate=True))
                            nc.vector.tensor_scalar(small[:, 1, h:h + 1], small[:, 0, h:h + 1], scale, None, ALU.mult).then_inc(s["maxed"], 1)

                        def add(h):
                            step.then(nc.vector.reciprocal(small[:, 3, h:h + 1], small[:, 2, h:h + 1]))
                            dve.wait_ge(s["mixed"], T * H + h + 1)
                            nc.vector.scalar_tensor_tensor(k.x[:, ds(T)], k.bank[6 + h % 2][:, 0:D], small[:, 3, h:h + 1], k.x[:, ds(T)],
                                                           ALU.mult, ALU.add).then_inc(s["added"], 1)

                        maximum(0)
                        for h in range(H):
                            if h + 1 < H:
                                maximum(h + 1)
                            dve.wait_ge(s["turned"], T * H + h + 1)
                            nc.vector.tensor_copy(probsT[:, h % 2, 4, :], k.bank[5][:, 0:P])
                            nc.vector.tensor_copy(probsT[0:LAST, h % 2, 5, :], k.bank[5][0:LAST, ds(1)]).then_inc(s["copied_v"], 1)
                            if h > 0:
                                add(h - 1)
                        add(H - 1)
                        assert step.n == 2 * H


def stage_1f(k):
    nc = k.nc
    with Scope(k) as ctx:
        src = k.sb("f1_src", [P, NT * D], F32, ctx)
        normalize(k, k.x, rows=src)
        relative_attention(k, src)
        relu_experts(k, src)
        with nc.Block() as block:
            @block.vector
            def _(dve):
                nc.vector.tensor_tensor(k.x[:], k.x[:], src[:], ALU.add)


def relative_attention(k, src):
    nc = k.nc
    scale = DH ** -0.5
    AHEAD = 2
    QUADS = H16 // 4
    W1 = H16 * (DH + 1)
    with Scope(k) as ctx:
        names = ("f1_ln1", "f1_wq", "f1_wk", "f1_wv", "f1_wo", "f1_wpT", "f1_wpT_swapped", "rot_cos", "rot_sin", "key_waves")
        ln, wq, wk, wv, wo, wpT, wpT_swapped, rot_cos, rot_sin, waves = homes = [load(k, ctx, n) for n in names]
        fetch(k, list(zip(names, homes)), ctx)
        normalize(k, src, ln[:, 0:1], ln[:, 1:2])
        kT = k.sb("f1_kT", [P, NTOK], F32, ctx)
        vals = k.sb("f1_vals", [P, NT, H16, DH + 1], F32, ctx)
        made, taken, ones = (k.sem(f"f1_kv_{n}", ctx) for n in ("made", "taken", "ones"))
        v_made, v_taken = k.sem("f1_v_made", ctx), k.sem("f1_v_taken", ctx)
        with nc.Block() as block:
            @block.tensor
            def _(pe):
                for b in range(B):
                    nc.tensor.matmul(k.bank[b], wk[:], k.xT[:, ds(b, S)], start=True, stop=True).then_inc(made, 1)
                for T in range(NT):
                    if T >= 4:
                        pe.wait_ge(v_taken, T - 3)
                    nc.tensor.matmul(k.bank[4 + T % 4][:, 0:D], k.xT[:, ds(T)], wv[:], start=True, stop=True).then_inc(v_made, 1)

            @block.scalar
            def _(act):
                for b in range(B):
                    act.wait_ge(made, b + 1)
                    nc.scalar.copy(kT[:, ds(b, S)], k.bank[b])

            @block.vector
            def _(dve):
                nc.vector.memset(vals[:], 1.0).then_inc(ones, 1)
                dve.wait_ge(ones, 1)
                for T in range(NT):
                    dve.wait_ge(v_made, T + 1)
                    nc.vector.tensor_copy(vals[:, T, :, 0:DH], k.bank[4 + T % 4][:, 0:D].rearrange("p (h d) -> p h d", d=DH)).then_inc(v_taken, 1)

        qT = k.sb("f1_qT", [P, P], F32, ctx)
        qT_head = k.sb("f1_qT_head", [P, H16, P], F32, ctx)
        turn_cos = k.sb("f1_turn_cos", [P, H16, P], F32, ctx)
        turn_sin = k.sb("f1_turn_sin", [P, H16, P], F32, ctx)
        turned_u = k.sb("f1_turned_u", [P, H16, P], F32, ctx)
        probs = k.sb("f1_probs", [P, 2, S], F32, ctx)
        probsT = k.sb("f1_probsT", [P, 2, TB, P], F32, ctx)
        negmax = k.sb("f1_negmax", [P, H16], F32, ctx)
        inv = k.sb("f1_inv", [P, H16], F32, ctx)
        outs = k.sb("f1_outs", [P, H16, DH], F32, ctx)
        outsT = k.sb("f1_outsT", [P, P], F32, ctx)
        s = {n: k.sem(f"f1_{n}", ctx) for n in ("q_made", "q_taken", "masked", "u_made", "u_read", "rotated", "scored", "maxed",
                                                "exped", "transposed", "copied", "mixed", "inverted", "normed", "out_turned",
                                                "out_copied", "projected", "added")}
        MIX, MISC = k.bank[6], k.bank[7]
        vals2 = vals[:].rearrange("p t h d -> p (t h d)")
        quad = lambda j: slice(4 * j, 4 * j + 4)

        def tiles(eng):
            with eng.Fori(0, B) as b:
                with eng.Fori(0, TB) as t:
                    yield b, t, b * TB + t

        with nc.Block() as block:
            @block.tensor
            def _(pe):
                for b, t, T in tiles(pe):
                    pe.wait_ge(s["added"], T + 1)
                    nc.tensor.matmul(MISC[:, 0:P], wq[:], k.xT[:, ds(T)], start=True, stop=True).then_inc(s["q_made"], 1)

                    def positions(j):
                        pe.wait_ge(s["masked"], T * QUADS + j + 1)
                        pe.wait_ge(s["u_read"], T * QUADS + j + 1)
                        nc.tensor.matmul(k.bank[0], wpT[:], qT_head[:, quad(j), :], start=True, stop=True)
                        nc.tensor.matmul(k.bank[1], wpT_swapped[:], qT_head[:, quad(j), :], start=True, stop=True).then_inc(s["u_made"], 1)

                    def score(h):
                        pe.wait_ge(s["rotated"], T * QUADS + h // 4 + 1)
                        pe.wait_ge(s["exped"], T * H16 + h + 1)
                        bank = k.bank[2 + h % 2]
                        nc.tensor.matmul(bank, qT_head[:, h, :], kT[:, ds(b, S)], start=True, stop=False)
                        nc.tensor.matmul(bank, turned_u[:, h, :], waves[:], start=False, stop=True).then_inc(s["scored"], 1)

                    def mix(h):
                        pe.wait_ge(s["copied"], T * H16 + h + 1)
                        if h == 0:
                            pe.wait_ge(s["normed"], T + 1)
                        for c in range(TB):
                            ins = nc.tensor.matmul(MIX[:, h * (DH + 1):(h + 1) * (DH + 1)], probsT[:, h % 2, c, :],
                                                   vals2[:, bass.ds((b * TB + c) * W1 + h * (DH + 1), DH + 1)],
                                                   start=c == 0, stop=c == TB - 1)
                        return ins

                    positions(0)
                    score(0)
                    for h in range(H16):
                        if h % 4 == 0 and h // 4 + 1 < QUADS:
                            positions(h // 4 + 1)
                        if h + 1 < H16:
                            score(h + 1)
                        pe.wait_ge(s["exped"], T * H16 + h + 1 + AHEAD)
                        for c in range(TB):
                            ins = nc.tensor.transpose(k.bank[4 + h % 2][:, ds(c)], probs[:, h % 2, ds(c)], k.ident[:])
                        ins.then_inc(s["transposed"], 1)
                        if h > 0:
                            mix(h - 1)
                    mix(H16 - 1).then_inc(s["mixed"], 1)
                    pe.wait_ge(s["normed"], T + 2)
                    nc.tensor.transpose(MISC[:, ds(1)], outs[:].rearrange("p h d -> p (h d)"), k.ident[:]).then_inc(s["out_turned"], 1)
                    pe.wait_ge(s["out_copied"], T + 1)
                    nc.tensor.matmul(MISC[:, ds(2)], outsT[:], wo[:], start=True, stop=True).then_inc(s["projected"], 1)

            @block.gpsimd
            def _(pool):
                for b, t, T in tiles(pool):
                    pool.wait_ge(s["q_taken"], T + 1)
                    for j in range(QUADS):
                        nc.gpsimd.tensor_tensor(qT_head[:, quad(j), :], qT[:, None, :].broadcast_to([P, 4, P]),
                                                k.headmask[:, quad(j), None].broadcast_to([P, 4, P]), ALU.mult).then_inc(s["masked"], 1)
                    for j in range(QUADS):
                        pool.wait_ge(s["u_read"], T * QUADS + j + 2)
                        nc.gpsimd.tensor_tensor(turned_u[:, quad(j), :], turn_cos[:, quad(j), :], turn_sin[:, quad(j), :],
                                                ALU.add).then_inc(s["rotated"], 1)

            @block.scalar
            def _(act):
                nc.scalar.copy(outsT[:, 0:1], k.ident[:, 0:1]).then_inc(s["exped"], AHEAD)
                for b, t, T in tiles(act):
                    act.wait_ge(s["q_made"], T + 1)
                    nc.scalar.activation(qT[:], MISC[:, 0:P], ACT.Copy, scale=scale).then_inc(s["q_taken"], 1)

                    def exp(h):
                        act.wait_ge(s["maxed"], T * H16 + h + 1)
                        nc.scalar.activation(probs[:, h % 2], k.bank[2 + h % 2], ACT.Exp, bias=negmax[:, h:h + 1]).then_inc(s["exped"], 1)

                    exp(0)
                    for h in range(H16):
                        if h + 1 < H16:
                            exp(h + 1)
                        act.wait_ge(s["transposed"], T * H16 + h + 1)
                        nc.scalar.copy(probsT[:, h % 2], k.bank[4 + h % 2]).then_inc(s["copied"], 1)
                    act.wait_ge(s["out_turned"], T + 1)
                    nc.scalar.copy(outsT[:], MISC[:, ds(1)]).then_inc(s["out_copied"], 1)

            @block.vector
            def _(dve):
                free_at_first(dve, s["added"], s["normed"], s["u_read"])
                for b, t, T in tiles(dve):
                    def rotate(j):
                        dve.wait_ge(s["u_made"], T * QUADS + j + 1)
                        for bank, table, home in ((0, rot_cos, turn_cos), (1, rot_sin, turn_sin)):
                            ins = nc.vector.tensor_tensor(home[:, quad(j), :], k.bank[bank].rearrange("p (h q) -> p h q", h=4),
                                                          table[:, None, ds(t)].broadcast_to([P, 4, P]), ALU.mult)
                        ins.then_inc(s["u_read"], 1)

                    rotate(0)
                    for h in range(H16):
                        dve.wait_ge(s["scored"], T * H16 + h + 1)
                        nc.vector.tensor_reduce(negmax[:, h:h + 1], k.bank[2 + h % 2], AX_X, ALU.max, negate=True).then_inc(s["maxed"], 1)
                        if h % 4 == 0 and h // 4 + 1 < QUADS:
                            rotate(h // 4 + 1)
                    dve.wait_ge(s["mixed"], T + 1)
                    mixed = MIX[:, 0:W1].rearrange("p (h d) -> p h d", h=H16)
                    nc.vector.reciprocal(inv[:], mixed[:, :, DH]).then_inc(s["inverted"], 1)
                    dve.wait_ge(s["inverted"], T + 1)
                    nc.vector.tensor_tensor(outs[:], mixed[:, :, 0:DH], inv[:, :, None].broadcast_to([P, H16, DH]), ALU.mult).then_inc(s["normed"], 1)
                    dve.wait_ge(s["projected"], T + 1)
                    nc.vector.tensor_tensor(src[:, ds(T)], MISC[:, ds(2)], src[:, ds(T)], ALU.add).then_inc(s["added"], 1)


def relu_experts(k, src):
    nc = k.nc
    AHEAD = 4
    with Scope(k) as ctx:
        ln, sel, iota = homes = [load(k, ctx, n) for n in ("f1_ln2", "m1_sel", "iota32")]
        fetch(k, list(zip(("f1_ln2", "m1_sel", "iota32"), homes)), ctx)
        normalize(k, src, ln[:, 0:1], ln[:, 1:2])
        shape = [P, NT, E1]
        chance = k.sb("m1_chance", shape, F32, ctx)
        left = k.sb("m1_left", shape, F32, ctx)
        hit = k.sb("m1_hit", shape, F32, ctx)
        gate = k.sb("m1_gate", shape, F32, ctx)
        far = k.sb("m1_far", [P, E1], F32, ctx)
        best = k.sb("m1_best", [P, NT], F32, ctx)
        first = k.sb("m1_first", [P, NT], F32, ctx)
        order, made, ready = (k.sem(f"m1_{n}", ctx) for n in ("order", "sel_made", "sel_ready"))
        with nc.Block() as block:
            @block.tensor
            def _(pe):
                for T in range(NT):
                    ins = nc.tensor.matmul(k.bank[0][:, ds(T, E1)], k.xT[:, ds(T)], sel[:], start=True, stop=True)
                ins.then_inc(made, 1)

            @block.scalar
            def _(act):
                act.wait_ge(made, 1)
                nc.scalar.activation(chance[:].rearrange("p t e -> p (t e)"), k.bank[0], ACT.Exp, scale=-1.0).then_inc(ready, 1)

            @block.vector
            def _(dve):
                step = Steps(dve, order)
                step.then(nc.vector.tensor_scalar(far[:], iota[:], 100.0, None, ALU.add))
                nc.vector.memset(gate[:], 0.0)
                dve.wait_ge(ready, 1)
                step.then(nc.vector.tensor_scalar(chance[:], chance[:], 1.0, None, ALU.add))
                step.then(nc.vector.reciprocal(chance[:], chance[:]))
                step.then(nc.vector.tensor_copy(left[:], chance[:]))
                for _ in range(K1):
                    first_hit(nc, step, left, hit, best, first, iota[:], far, shape)
                    nc.vector.scalar_tensor_tensor(left[:], hit[:], -HUGE, left[:], ALU.mult, ALU.add)
                    step.then(nc.vector.tensor_tensor(hit[:], hit[:], chance[:], ALU.mult))
                    step.then(nc.vector.tensor_tensor(gate[:], gate[:], hit[:], ALU.add))

        w = k.sb("m1_weights", [P, 2, P + D], F32, ctx)
        hT = k.sb("m1_hT", [P, B, S], F32, ctx)
        loaded = [k.sem(f"m1_loaded{u}", ctx) for u in range(2)]
        h_made, relued, y_made, y_read = (k.sem(f"m1_{n}", ctx) for n in ("h_made", "relued", "y_made", "y_read"))
        gate2 = gate[:].rearrange("p t e -> p (t e)")
        source = k.dram["m1_w"]
        with nc.Block() as block:
            @block.sync
            def _(sp):
                for u in range(2):
                    sp.dma_start(w[:, u, :], source[u]).then_inc(loaded[u], 16)
                with sp.Fori(0, E1 // 2 - 1) as turn:
                    for u in range(2):
                        e = turn * 2 + u
                        sp.wait_ge(y_made, e * B + B)
                        sp.dma_start(w[:, u, :], source[bass.ds(e + 2, 1)].rearrange("e p n -> (e p) n")).then_inc(loaded[u], 16)

            @block.tensor
            def _(pe):
                with pe.Fori(0, E1 // 2) as turn:
                    for u in range(2):
                        e = turn * 2 + u
                        pe.wait_ge(loaded[u], turn * 16 + 16)

                        def hidden(c):
                            pe.wait_ge(relued, e * B + c + 1)
                            nc.tensor.matmul(k.bank[c], w[:, u, 0:P], k.xT[:, ds(c, S)], start=True, stop=True).then_inc(h_made, 1)

                        def values(c):
                            pe.wait_ge(relued, e * B + c + 1 + AHEAD)
                            pe.wait_ge(y_read, e * B + c + 1)
                            for j in range(TB):
                                ins = nc.tensor.matmul(k.bank[4 + c][:, ds(j)], hT[:, c, ds(j)], w[:, u, P:P + D], start=True, stop=True)
                            ins.then_inc(y_made, 1)

                        hidden(0)
                        hidden(1)
                        for c in range(2, B):
                            hidden(c)
                            values(c - 2)
                        values(B - 2)
                        values(B - 1)

            @block.scalar
            def _(act):
                nc.scalar.copy(hT[:, 0, 0:1], k.ident[:, 0:1]).then_inc(relued, AHEAD)
                with act.Fori(0, E1) as e:
                    for c in range(B):
                        act.wait_ge(h_made, e * B + c + 1)
                        nc.scalar.activation(hT[:, c, :], k.bank[c], ACT.Relu).then_inc(relued, 1)

            @block.vector
            def _(dve):
                nc.vector.memset(best[:], 0.0).then_inc(y_read, AHEAD)
                with dve.Fori(0, E1) as e:
                    for c in range(B):
                        dve.wait_ge(y_made, e * B + c + 1)
                        for j in range(TB):
                            T = c * TB + j
                            ins = nc.vector.scalar_tensor_tensor(src[:, ds(T)], k.bank[4 + c][:, ds(j)], gate2[:, bass.ds(e + T * E1, 1)],
                                                                 src[:, ds(T)], ALU.mult, ALU.add)
                        ins.then_inc(y_read, 1)


def stage_0f(k):
    nc = k.nc
    with Scope(k) as ctx:
        xn = k.sb("m0_xn", [P, NT * D], F32, ctx)
        normalize(k, k.x, rows=xn)
        slots = nc.dram_tensor("m0_slots", (SLOTS + K0 * NTOK, D), F32).ap()
        answers = nc.dram_tensor("m0_answers", (SLOTS, D), F32).ap()
        put = k.sb("m0_put", [P, K0, NT], I32, ctx)
        get = k.sb("m0_get", [P, K0, NT], I32, ctx)
        weight = k.sb("m0_weight", [P, K0, NT], F32, ctx)
        route(k, slots, put, get, weight)
        shared_experts(k, slots, xn, put)
        routed_experts(k, slots, answers)
        answer = k.sb("m0_answer", [P, K0, NT, D], F32, ctx)
        gathered = k.sem("m0_gathered", ctx)
        order = k.sem("m0_add_order", ctx)
        with nc.Block() as block:
            @block.gpsimd
            def _(pool):
                for T in range(NT):
                    for c in range(K0):
                        pool.indirect_dma_start(out=answer[:, c, T, :], out_offset=None, in_=answers,
                                                in_offset=bass.IndirectOffsetOnAxis(ap=get[:, c, T:T + 1], axis=0)).then_inc(gathered, 16)
                pool.wait_ge(gathered, 16 * K0 * NT)

            @block.vector
            def _(dve):
                step = Steps(dve, order)
                dve.wait_ge(gathered, 16 * K0 * NT)
                for c in range(K0):
                    for T in range(NT):
                        ins = nc.vector.scalar_tensor_tensor(k.x[:, ds(T)], answer[:, c, T, :], weight[:, c, T:T + 1], k.x[:, ds(T)],
                                                             ALU.mult, ALU.add)
                    step.then(ins)


def route(k, slots, put, get, weight):
    nc = k.nc
    TE = [P, NT, E0]
    flat = lambda a: a[:].rearrange("p t e -> p (t e)")
    over_experts = lambda a: a[:, :, None].broadcast_to(TE)
    over_tiles = lambda a: a[:, None, :].broadcast_to(TE)
    with Scope(k) as ctx:
        names = ("m0_gate_w", "m0_gate_b", "iota16", "slot_base", "spare_slot", "before")
        gate_w, gate_b, iota, base, spare, before = homes = [load(k, ctx, n) for n in names]
        bits = k.sb("m0_bits", [P, MAG_BITS * E0], I32, ctx)
        zeros = k.sb("m0_zeros", [P, SLOTS], F32, ctx)
        fetched, emptied, zeroed = (k.sem(f"m0_{n}", ctx) for n in ("fetched", "emptied", "zeroed"))
        t = {n: k.sb(f"m0_{n}", TE, F32, ctx) for n in ("logit", "work", "score", "hit1", "hit2", "member", "signed", "keep", "number", "tmp")}
        e = {n: k.sb(f"m0_{n}", [P, E0], F32, ctx) for n in ("far", "count", "positive", "sign", "want", "cut", "above")}
        best, first, sums = (k.sb(f"m0_{n}", [P, NT], F32, ctx) for n in ("best", "first", "sums"))
        threshold = k.sb("m0_threshold", [P, E0], I32, ctx)
        trial = k.sb("m0_trial", [P, E0], I32, ctx)
        enough = k.sb("m0_enough", [P, E0], F32, ctx)
        taken = k.sb("m0_taken_bit", [P, E0], I32, ctx)
        mark = k.sb("m0_mark", TE, BF16, ctx)
        marks = k.sb("m0_marks", [P, NT, 2, E0], BF16, ctx)
        offset = k.sb("m0_offset", [P, NT + 1, 2 * E0], F32, ctx)
        rank = k.sb("m0_rank", [P, NT, 2, E0], F32, ctx)
        ones = k.sb("m0_ones", [P, P], BF16, ctx)
        before16 = k.sb("m0_before16", [P, P], BF16, ctx)
        order, logits_made, shifted, exped, marked, counted, mark2, rank_made = (
            k.sem(f"m0_{n}", ctx) for n in ("order", "logits_made", "shifted", "exped", "marked", "counted", "marked2", "rank_made"))
        with nc.Block() as block:
            @block.sync
            def _(sp):
                for n, home in zip(names, homes):
                    sp.dma_start(home[:], k.dram[n]).then_inc(fetched, 16)
                sp.dma_start(bits[:], k.dram["bits"]).then_inc(fetched, 16)
                sp.wait_ge(emptied, 1)
                sp.dma_start(slots[0:SLOTS, :].rearrange("(p s) d -> p (s d)", p=P), zeros[:]).then_inc(zeroed, 16)
                sp.wait_ge(zeroed, 16)

            @block.gpsimd
            def _(pool):
                nc.gpsimd.memset(zeros[:], 0.0).then_inc(emptied, 1)

            @block.scalar
            def _(act):
                act.wait_ge(shifted, 1)
                nc.scalar.activation(flat(t["score"]), flat(t["work"]), ACT.Exp).then_inc(exped, 1)

            @block.tensor
            def _(pe):
                pe.wait_ge(fetched, 16 * (len(names) + 1))
                for T in range(NT):
                    ins = nc.tensor.matmul(k.bank[0][:, ds(T, E0)], k.xT[:, ds(T)], gate_w[:], start=True, stop=True)
                ins.then_inc(logits_made, 1)
                pe.wait_ge(marked, 1)
                nc.tensor.matmul(k.bank[1][:, 0:NT * E0], ones[:], flat(mark), start=True, stop=True).then_inc(counted, 1)
                with pe.Fori(0, MAG_BITS) as i:
                    pe.wait_ge(marked, i + 2)
                    nc.tensor.matmul(k.bank[1][:, 0:NT * E0], ones[:], flat(mark), start=True, stop=True).then_inc(counted, 1)
                pe.wait_ge(mark2, 1)
                m = marks[:].rearrange("p t c e -> p (t c e)")
                nc.tensor.matmul(k.bank[2], ones[:], m, start=True, stop=True).then_inc(rank_made, 1)
                nc.tensor.matmul(k.bank[3], before16[:], m, start=True, stop=True).then_inc(rank_made, 1)

            @block.vector
            def _(dve):
                step = Steps(dve, order)
                then, v = step.then, nc.vector
                then(v.memset(ones[:], 1.0))
                dve.wait_ge(fetched, 16 * (len(names) + 1))
                then(v.tensor_copy(before16[:], before[:]))
                then(v.tensor_scalar(e["far"][:], iota[:], 100.0, None, ALU.add))
                dve.wait_ge(logits_made, 1)
                then(v.tensor_copy(flat(t["logit"]), k.bank[0][:, 0:NT * E0]))
                then(v.tensor_reduce(best[:], t["logit"][:], AX_X, ALU.max))
                v.tensor_tensor(t["work"][:], t["logit"][:], over_experts(best), ALU.subtract).then_inc(shifted, 1)
                dve.wait_ge(exped, 1)
                then(v.tensor_reduce(sums[:], t["score"][:], AX_X, ALU.add))
                then(v.reciprocal(sums[:], sums[:]))
                then(v.tensor_tensor(t["score"][:], t["score"][:], over_experts(sums), ALU.mult))
                then(v.tensor_tensor(t["score"][:], t["score"][:], over_tiles(gate_b), ALU.add))
                first_hit(nc, step, t["score"], t["hit1"], best, first, iota[:], e["far"], TE)
                then(v.scalar_tensor_tensor(t["score"][:], t["hit1"][:], -HUGE, t["score"][:], ALU.mult, ALU.add))
                first_hit(nc, step, t["score"], t["hit2"], best, first, iota[:], e["far"], TE)
                then(v.tensor_tensor(t["member"][:], t["hit1"][:], t["hit2"][:], ALU.add))
                then(v.tensor_scalar(t["tmp"][:], t["member"][:], HUGE, HUGE, ALU.mult, ALU.subtract))
                then(v.tensor_tensor(t["work"][:], t["logit"][:], t["member"][:], ALU.mult))
                then(v.tensor_tensor(t["work"][:], t["work"][:], t["tmp"][:], ALU.add))

                def count(n):
                    dve.wait_ge(counted, n)
                    then(v.tensor_reduce(e["count"][:], k.bank[1][:, 0:NT * E0].rearrange("p (t e) -> p e t", e=E0), AX_X, ALU.add))

                v.tensor_scalar(mark[:], t["work"][:], 0.0, None, ALU.is_ge).then_inc(marked, 1)
                count(1)
                then(v.tensor_scalar(e["positive"][:], e["count"][:], float(CAP), None, ALU.is_ge))
                v.tensor_scalar(e["sign"][:], e["positive"][:], 2.0, -1.0, ALU.mult, ALU.add)
                v.memset(threshold[:], 0)
                then(v.tensor_scalar(e["want"][:], e["positive"][:], float(2 * CAP - NTOK - 1), float(NTOK - CAP + 1), ALU.mult, ALU.add))
                then(v.tensor_tensor(t["signed"][:], t["work"][:], over_tiles(e["sign"]), ALU.mult))
                with dve.Fori(0, MAG_BITS) as i:
                    step.turn(i, 5)
                    then(v.tensor_tensor(trial[:], threshold[:], bits[:, ds(i, E0)], ALU.bitwise_or))
                    v.tensor_tensor(mark[:], t["signed"][:], over_tiles(trial[:].bitcast(F32)), ALU.is_ge).then_inc(marked, 1)
                    count(i + 2)
                    then(v.tensor_tensor(enough[:], e["count"][:], e["want"][:], ALU.is_ge))
                    then(v.tensor_tensor(taken[:], enough[:], bits[:, ds(i, E0)], ALU.mult))
                    then(v.tensor_tensor(threshold[:], threshold[:], taken[:], ALU.bitwise_or))
                step.turns_end(MAG_BITS)
                then(v.tensor_tensor(e["cut"][:], threshold[:].bitcast(F32), e["sign"][:], ALU.mult))
                then(v.tensor_tensor(t["tmp"][:], t["work"][:], over_tiles(e["cut"]), ALU.is_equal))
                then(v.tensor_tensor(t["tmp"][:], t["tmp"][:], t["member"][:], ALU.mult))
                v.tensor_copy(marks[:, :, 1, :], t["tmp"][:])
                then(v.tensor_tensor(t["keep"][:], t["work"][:], over_tiles(e["cut"]), ALU.is_gt))
                v.tensor_copy(marks[:, :, 0, :], t["keep"][:]).then_inc(mark2, 1)
                v.memset(offset[:, 0, :], 0.0)
                dve.wait_ge(rank_made, 2)
                totals = k.bank[2].rearrange("p (t c) -> p t c", t=NT)
                for T in range(NT):
                    if T == 0:
                        then(v.tensor_copy(offset[:, 1, :], totals[:, 0, :]))
                    else:
                        then(v.tensor_tensor(offset[:, T + 1, :], totals[:, T, :], offset[:, T, :], ALU.add))
                then(v.tensor_tensor(rank[:].rearrange("p t c e -> p t (c e)"), k.bank[3].rearrange("p (t c) -> p t c", t=NT),
                                     offset[:, 0:NT, :], ALU.add))
                above = offset[:, NT, 0:E0]
                then(v.tensor_tensor(rank[:, :, 1, :], rank[:, :, 1, :], above[:, None, :].broadcast_to(TE), ALU.add))
                then(v.scalar_tensor_tensor(t["tmp"][:], rank[:, :, 1, :], float(CAP), t["tmp"][:], ALU.is_lt, ALU.mult))
                then(v.tensor_tensor(t["number"][:], t["tmp"][:], rank[:, :, 1, :], ALU.mult))
                then(v.tensor_tensor(t["signed"][:], t["keep"][:], rank[:, :, 0, :], ALU.mult))
                then(v.tensor_tensor(t["number"][:], t["number"][:], t["signed"][:], ALU.add))
                then(v.tensor_tensor(t["number"][:], t["number"][:], over_tiles(base), ALU.add))
                then(v.tensor_tensor(t["keep"][:], t["keep"][:], t["tmp"][:], ALU.add))
                for c, hit in enumerate((t["hit1"], t["hit2"])):
                    then(v.tensor_tensor(hit[:], hit[:], t["keep"][:], ALU.mult))
                    then(v.tensor_tensor(t["tmp"][:], hit[:], t["number"][:], ALU.mult))
                    then(v.tensor_reduce(best[:], t["tmp"][:], AX_X, ALU.add))
                    then(v.tensor_copy(get[:, c, :], best[:]))
                    then(v.tensor_tensor(t["tmp"][:], hit[:], t["logit"][:], ALU.mult))
                    then(v.tensor_reduce(weight[:, c, :], t["tmp"][:], AX_X, ALU.add))
                    then(v.tensor_reduce(first[:], hit[:], AX_X, ALU.add))
                    then(v.tensor_scalar(first[:], first[:], -1.0, 1.0, ALU.mult, ALU.add))
                    then(v.scalar_tensor_tensor(first[:], spare[:], float(c * NTOK), first[:], ALU.add, ALU.mult))
                    then(v.tensor_tensor(best[:], best[:], first[:], ALU.add))
                    then(v.tensor_copy(put[:, c, :], best[:]))


def shared_experts(k, slots, xn, put):
    nc = k.nc
    HB = S0 * HID0 // P
    with Scope(k) as ctx:
        w1, w3, w2 = homes = [load(k, ctx, n) for n in ("s0_w1", "s0_w3", "s0_w2")]
        fetch(k, list(zip(("s0_w1", "s0_w3", "s0_w2"), homes)), ctx)
        silu = k.sb("s0_silu", [P, 2, S], F32, ctx)
        hidden = k.sb("s0_hidden", [P, HB, S], F32, ctx)
        scattered, made, silued, gated, summed, added = (k.sem(f"s0_{n}", ctx) for n in ("scattered", "made", "silued", "gated", "summed", "added"))
        with nc.Block() as block:
            @block.gpsimd
            def _(pool):
                for T in range(NT):
                    for c in range(K0):
                        pool.indirect_dma_start(out=slots, out_offset=bass.IndirectOffsetOnAxis(ap=put[:, c, T:T + 1], axis=0),
                                                in_=xn[:, ds(T)], in_offset=None).then_inc(scattered, 16)
                pool.wait_ge(scattered, 16 * K0 * NT)

            @block.tensor
            def _(pe):
                with pe.Fori(0, B) as b:
                    for n in range(HB):
                        pe.wait_ge(gated, b * HB + n + 1)
                        nc.tensor.matmul(k.bank[n % 2], w1[:, ds(n)], k.xT[:, ds(b, S)], start=True, stop=True)
                        nc.tensor.matmul(k.bank[2 + n % 2], w3[:, ds(n)], k.xT[:, ds(b, S)], start=True, stop=True).then_inc(made, 1)
                    pe.wait_ge(gated, b * HB + HB + 2)
                    pe.wait_ge(added, b + 1)
                    for j in range(TB):
                        for n in range(HB):
                            ins = nc.tensor.matmul(k.bank[4][:, ds(j)], hidden[:, n, ds(j)], w2[:, ds(n)], start=n == 0, stop=n == HB - 1)
                    ins.then_inc(summed, 1)

            @block.scalar
            def _(act):
                nc.scalar.copy(silu[:, 0, 0:1], k.ident[:, 0:1]).then_inc(gated, 2)
                with act.Fori(0, B) as b:
                    for n in range(HB):
                        act.wait_ge(made, b * HB + n + 1)
                        nc.scalar.activation(silu[:, n % 2, :], k.bank[n % 2], ACT.Silu).then_inc(silued, 1)

            @block.vector
            def _(dve):
                free_at_first(dve, added)
                with dve.Fori(0, B) as b:
                    for n in range(HB):
                        dve.wait_ge(silued, b * HB + n + 1)
                        nc.vector.tensor_tensor(hidden[:, n, :], k.bank[2 + n % 2], silu[:, n % 2, :], ALU.mult).then_inc(gated, 1)
                    dve.wait_ge(summed, b + 1)
                    nc.vector.scalar_tensor_tensor(k.x[:, ds(b, S)], k.bank[4], 1.0 / S0, k.x[:, ds(b, S)], ALU.mult, ALU.add).then_inc(added, 1)


def routed_experts(k, slots, answers):
    nc = k.nc
    HB = HID0 // P
    cuts = [(at, min(P, CAP - at)) for at in range(0, CAP, P)]
    with Scope(k) as ctx:
        w13 = k.sb("m0_w13", [P, 2, 2 * HID0], F32, ctx)
        w2 = k.sb("m0_w2", [P, 2, HB * D], F32, ctx)
        rows = k.sb("m0_rows", [P, 2, len(cuts), D], F32, ctx)
        rowsT = k.sb("m0_rowsT", [P, CAP], F32, ctx)
        silu = k.sb("m0_silu", [P, HB, CAP], F32, ctx)
        hidden = k.sb("m0_hidden", [P, HB, CAP], F32, ctx)
        result = k.sb("m0_result", [P, 2, len(cuts), D], F32, ctx)
        loaded = [k.sem(f"m0_loaded{u}", ctx) for u in range(2)]
        stored = [k.sem(f"m0_stored{u}", ctx) for u in range(2)]
        turned, copied, made, silued, gated, summed, taken = (k.sem(f"m0_{n}", ctx) for n in ("turned", "copied", "made", "silued", "gated", "summed", "taken"))
        PARTS = 2 + len(cuts)
        with nc.Block() as block:
            def load_expert(eng, u, e):
                one = lambda a: a[bass.ds(e, 1)].rearrange("e p n -> (e p) n") if not isinstance(e, int) else a[e]
                eng.dma_start(w13[:, u, :], one(k.dram["m0_w13"])).then_inc(loaded[u], 16)
                eng.dma_start(w2[:, u, :], one(k.dram["m0_w2"])).then_inc(loaded[u], 16)
                for i, (at, n) in enumerate(cuts):
                    eng.dma_start(rows[0:n, u, i, :], slots[bass.ds(e * CAP + at, n), :]).then_inc(loaded[u], 16)

            @block.sync
            def _(sp):
                load_expert(sp, 0, 0)
                load_expert(sp, 1, 1)
                with sp.Fori(0, E0 // 2 - 1) as turn:
                    for u in range(2):
                        sp.wait_ge(summed, turn * 2 + u + 1)
                        load_expert(sp, u, turn * 2 + u + 2)

            @block.scalar
            def _(act):
                free_at_first(act, *stored, by=16)
                with act.Fori(0, E0 // 2) as turn:
                    for u in range(2):
                        e = turn * 2 + u
                        act.wait_ge(turned, e + 1)
                        nc.scalar.copy(rowsT[:], k.bank[0][:, 0:CAP]).then_inc(copied, 1)
                        for n in range(HB):
                            act.wait_ge(made, e * HB + n + 1)
                            nc.scalar.activation(silu[:, n, :], k.bank[1 + n][:, 0:CAP], ACT.Silu).then_inc(silued, 1)
                        act.wait_ge(taken, e + 2)
                        for i, (at, n) in enumerate(cuts):
                            act.dma_start(answers[bass.ds(e * CAP + at, n), :], result[0:n, u, i, :]).then_inc(stored[u], 16)
                for u in range(2):
                    act.wait_ge(stored[u], 16 * len(cuts) * E0 // 2 + 16)

            @block.vector
            def _(dve):
                free_at_first(dve, taken)
                with dve.Fori(0, E0 // 2) as turn:
                    for u in range(2):
                        e = turn * 2 + u
                        for n in range(HB):
                            dve.wait_ge(silued, e * HB + n + 1)
                            nc.vector.tensor_tensor(hidden[:, n, :], k.bank[3 + n][:, 0:CAP], silu[:, n, :], ALU.mult).then_inc(gated, 1)
                        dve.wait_ge(summed, e + 1)
                        dve.wait_ge(stored[u], turn * (16 * len(cuts)) + 16)
                        for i, (at, n) in enumerate(cuts):
                            ins = nc.vector.tensor_copy(result[0:n, u, i, :], k.bank[5][0:n, ds(i)])
                        ins.then_inc(taken, 1)

            @block.tensor
            def _(pe):
                with pe.Fori(0, E0 // 2) as turn:
                    for u in range(2):
                        e = turn * 2 + u
                        pe.wait_ge(loaded[u], turn * (16 * PARTS) + 16 * PARTS)
                        for i, (at, n) in enumerate(cuts):
                            ins = nc.tensor.transpose(k.bank[0][:, at:at + n], rows[0:n, u, i, :], k.ident[0:n, 0:n])
                        ins.then_inc(turned, 1)
                        pe.wait_ge(copied, e + 1)
                        for n in range(HB):
                            nc.tensor.matmul(k.bank[1 + n][:, 0:CAP], w13[:, u, ds(n)], rowsT[:], start=True, stop=True)
                            nc.tensor.matmul(k.bank[3 + n][:, 0:CAP], w13[:, u, ds(HB + n)], rowsT[:], start=True, stop=True).then_inc(made, 1)
                        pe.wait_ge(gated, e * HB + HB)
                        pe.wait_ge(taken, e + 1)
                        for i, (at, m) in enumerate(cuts):
                            for n in range(HB):
                                ins = nc.tensor.matmul(k.bank[5][0:m, ds(i)], hidden[:, n, at:at + m], w2[:, u, ds(n)], start=n == 0, stop=n == HB - 1)
                        ins.then_inc(summed, 1)


def stage_3f(k):
    nc = k.nc
    NB = HID3 // P
    with Scope(k) as ctx:
        fc, proj, uT, v, bT, gate = homes = [load(k, ctx, n, k.dram[n].shape[0])
                                             for n in ("f3_fc", "f3_proj", "f3_uT", "f3_v", "f3_bT", "f3_gate")]
        fetch(k, list(zip(("f3_fc", "f3_proj", "f3_uT", "f3_v", "f3_bT", "f3_gate"), homes)), ctx)
        rank = v.shape[0]
        scale = k.sb("f3_scale", [P, 2, NB], F32, ctx)
        half = k.sb("f3_half", [P, 2, 2, NB], F32, ctx)
        below = k.sb("f3_below", [P, 2, HID3], F32, ctx)
        fv = k.sb("f3_fv", [rank, D], F32, ctx)
        fcT = k.sb("f3_fcT", [P, HID3], F32, ctx)
        projT = k.sb("f3_projT", [P, HID3], F32, ctx)
        order, ready, made, taken = (k.sem(f"f3_{n}", ctx) for n in ("order", "ready", "made", "taken"))
        with nc.Block() as block:
            @block.vector
            def _(dve):
                step = Steps(dve, order)
                step.then(nc.vector.tensor_reduce(scale[:, 0, :], fc[:].rearrange("p (b d) -> p b d", d=D), AX_X, ALU.add,
                                                  apply_absolute_value=True))
                nc.vector.tensor_reduce(scale[:, 1, 0:1], proj[:], AX_X, ALU.add, apply_absolute_value=True)
                step.then(nc.vector.memset(scale[:, 1, 1:NB], 1.0))
                nc.vector.tensor_scalar(scale[:, 0, :], scale[:, 0, :], 1.0 / D, 1e-5, ALU.mult, ALU.max)
                step.then(nc.vector.tensor_scalar(scale[:, 1, :], scale[:, 1, :], 1.0 / HID3, 1e-5, ALU.mult, ALU.max))
                nc.vector.tensor_scalar(half[:, 0], scale[:], 0.5, None, ALU.mult)
                step.then(nc.vector.tensor_scalar(half[:, 1], scale[:], -0.5, None, ALU.mult))
                blocks = [(0, fc, n, slice(n * P, (n + 1) * P), slice(n * P, (n + 1) * P)) for n in range(NB)]
                blocks += [(1, proj, 0, slice(0, HID3), slice(0, HID3))]
                for m, w, n, cols, _ in blocks:
                    ins = nc.vector.tensor_scalar(below[:, m, cols], w[:, cols], half[:, 1, m, n:n + 1], None, ALU.is_lt)
                step.then(ins)
                for m, w, n, cols, _ in blocks:
                    ins = nc.vector.scalar_tensor_tensor(below[:, m, cols], w[:, cols], half[:, 0, m, n:n + 1], below[:, m, cols],
                                                         ALU.is_gt, ALU.subtract)
                step.then(ins)
                for m, w in ((0, fc), (1, proj)):
                    ins = nc.vector.tensor_tensor(below[:, m, :], below[:, m, :], w[:], ALU.subtract)
                step.then(ins)
                for m, w in ((0, fc), (1, proj)):
                    ins = nc.vector.tensor_tensor(below[:, m, :], below[:, m, :], w[:], ALU.add)
                step.then(ins)
                for m, w, n, cols, _ in blocks:
                    ins = nc.vector.tensor_scalar(w[:, cols], below[:, m, cols], scale[:, m, n:n + 1], None, ALU.mult)
                ins.then_inc(ready, 1)
                dve.wait_ge(made, 1)
                nc.vector.tensor_copy(fv[:], k.bank[1][0:rank, 0:D]).then_inc(taken, 1)
                dve.wait_ge(made, 3)
                step.then(nc.vector.tensor_copy(fcT[:], k.bank[2]))
                nc.vector.tensor_copy(projT[:], k.bank[3])
                dve.wait_ge(made, 4)
                nc.vector.scalar_tensor_tensor(fcT[:], k.bank[4], gate[:, 0:1], fcT[:], ALU.mult, ALU.add).then_inc(taken, 1)

            @block.tensor
            def _(pe):
                nc.tensor.matmul(k.bank[1][0:rank, 0:D], bT[:], v[:], start=True, stop=True).then_inc(made, 1)
                pe.wait_ge(ready, 1)
                for w, bank in ((fc, 2), (proj, 3)):
                    for n in range(NB):
                        ins = nc.tensor.transpose(k.bank[bank][:, ds(n)], w[:, ds(n)], k.ident[:])
                    ins.then_inc(made, 1)
                pe.wait_ge(taken, 1)
                nc.tensor.matmul(k.bank[4], fv[:], uT[:], start=True, stop=True).then_inc(made, 1)
        normalize(k, k.x)
        r = k.sb("f3_r", [P, NB, S], F32, ctx)
        sq = k.sb("f3_sq", [P, NB, S], F32, ctx)
        hidden, relued, squared, out_made, added = (k.sem(f"f3_{n}", ctx) for n in ("hidden", "relued", "squared", "out_made", "added"))
        with nc.Block() as block:
            @block.tensor
            def _(pe):
                with pe.Fori(0, B) as b:
                    for n in range(NB):
                        pe.wait_ge(relued, b * NB + 1)
                        nc.tensor.matmul(k.bank[n], fcT[:, ds(n)], k.xT[:, ds(b, S)], start=True, stop=True).then_inc(hidden, 1)
                    pe.wait_ge(squared, b * NB + NB + 1)
                    pe.wait_ge(added, b + 1)
                    for j in range(TB):
                        for n in range(NB):
                            ins = nc.tensor.matmul(k.bank[4][:, ds(j)], sq[:, n, ds(j)], projT[:, ds(n)], start=n == 0, stop=n == NB - 1)
                    ins.then_inc(out_made, 1)

            @block.scalar
            def _(act):
                free_at_first(act, relued)
                with act.Fori(0, B) as b:
                    for n in range(NB):
                        act.wait_ge(hidden, b * NB + n + 1)
                        act.wait_ge(squared, b * NB + 1)
                        nc.scalar.activation(r[:, n, :], k.bank[n], ACT.Relu).then_inc(relued, 1)

            @block.vector
            def _(dve):
                free_at_first(dve, squared, added)
                with dve.Fori(0, B) as b:
                    for n in range(NB):
                        dve.wait_ge(relued, b * NB + n + 2)
                        nc.vector.tensor_tensor(sq[:, n, :], r[:, n, :], r[:, n, :], ALU.mult).then_inc(squared, 1)
                    dve.wait_ge(out_made, b + 1)
                    nc.vector.tensor_tensor(k.x[:, ds(b, S)], k.bank[4], k.x[:, ds(b, S)], ALU.add).then_inc(added, 1)


def stage_lora(k):
    nc = k.nc
    with Scope(k) as ctx:
        names = ("lora_wT", "lora_b", "lora_downT", "lora_down_aux", "lora_upT", "lora_up_auxT")
        w, b, downT, down_aux, upT, up_auxT = (load(k, ctx, n, k.dram[n].shape[0]) for n in names)
        fetch(k, list(zip(names, (w, b, downT, down_aux, upT, up_auxT))), ctx)
        rank, mid = upT.shape[0], upT.shape[1]
        a = k.sb("lora_a", [rank, D], F32, ctx)
        c = k.sb("lora_c", [mid, D], F32, ctx)
        w_all = k.sb("lora_w_all", [P, D], F32, ctx)
        made = k.sem("lora_made", ctx)
        taken = k.sem("lora_taken", ctx)
        with nc.Block() as block:
            @block.tensor
            def _(pe):
                nc.tensor.matmul(k.bank[1][0:rank, 0:D], downT[:], down_aux[:], start=True, stop=True).then_inc(made, 1)
                pe.wait_ge(taken, 1)
                nc.tensor.matmul(k.bank[2][0:mid, 0:D], upT[:], a[:], start=True, stop=True).then_inc(made, 1)
                pe.wait_ge(taken, 2)
                nc.tensor.matmul(k.bank[3][:, 0:D], c[:], up_auxT[:], start=True, stop=True).then_inc(made, 1)

            @block.vector
            def _(dve):
                dve.wait_ge(made, 1)
                nc.vector.tensor_copy(a[:], k.bank[1][0:rank, 0:D]).then_inc(taken, 1)
                dve.wait_ge(made, 2)
                nc.vector.tensor_copy(c[:], k.bank[2][0:mid, 0:D]).then_inc(taken, 1)
                dve.wait_ge(made, 3)
                nc.vector.tensor_tensor(w_all[:], k.bank[3][:, 0:D], w[:], ALU.add).then_inc(taken, 1)
        normalize(k, k.x)
        multiplied = k.sem("lora_multiplied", ctx)
        added = k.sem("lora_added", ctx)
        with nc.Block() as block:
            @block.tensor
            def _(pe):
                for T in range(NT):
                    if T % TB == 0 and T >= 2 * TB:
                        pe.wait_ge(added, T // TB - 1)
                    ins = nc.tensor.matmul(k.bank[T // TB % 2][:, ds(T % TB)], k.xT[:, ds(T)], w_all[:],
                                           start=True, stop=True)
                    if T % TB == TB - 1:
                        ins.then_inc(multiplied, 1)

            @block.vector
            def _(dve):
                order = Steps(dve, k.sem("lora_order", ctx))
                x = k.x[:].rearrange("p (t d) -> p t d", d=D)
                for b4 in range(B):
                    part = x[:, b4 * TB:(b4 + 1) * TB, :]
                    order.then(nc.vector.tensor_tensor(part, part, b[:, None, :].broadcast_to([P, TB, D]), ALU.add))
                    dve.wait_ge(multiplied, b4 + 1)
                    nc.vector.tensor_tensor(part, k.bank[b4 % 2].rearrange("p (t d) -> p t d", d=D), part,
                                            ALU.add).then_inc(added, 1)


def cross_attention(k, name, heads, mask, mask_kind, scale, biased, weighted, project):
    nc = k.nc
    dh = D // heads
    HG = min(heads, 4)
    NG = heads // HG
    PER_BANK = min(HG, 2)
    AHEAD = 2
    mask_tiles = k.dram[mask].shape[0] // P
    with Scope(k) as ctx:
        wq, wk, wv, bv = (load(k, ctx, f"{name}_{w}") for w in ("wq", "wk", "wv", "bv"))
        pairs = [(f"{name}_wq", wq), (f"{name}_wk", wk), (f"{name}_wv", wv), (f"{name}_bv", bv)]
        if biased:
            bq, bk = load(k, ctx, f"{name}_bq"), load(k, ctx, f"{name}_bk")
            pairs += [(f"{name}_bq", bq), (f"{name}_bk", bk)]
        if project:
            wo, bo = load(k, ctx, f"{name}_wo"), load(k, ctx, f"{name}_bo")
            pairs += [(f"{name}_wo", wo), (f"{name}_bo", bo)]
        mask_raw = k.sb(f"{name}_mask_raw", [P, mask_tiles, SC], k.dram[mask].dtype, ctx)
        added = mask_raw if mask_kind == "float" else k.sb(f"{name}_mask", [P, mask_tiles, SC], F32, ctx)
        prob = k.sb(f"{name}_prob", [P, NT, SC], F32, ctx) if weighted else None
        fetched = k.sem(f"{name}_fetched", ctx)
        fetched_masks = k.sem(f"{name}_fetched_masks", ctx)
        with nc.Block() as block:
            @block.sync
            def _(sp):
                for n, home in pairs:
                    sp.dma_start(home[:], k.dram[n]).then_inc(fetched, 16)
                sp.wait_ge(fetched, 16 * len(pairs))

            @block.scalar
            def _(act):
                act.dma_start(mask_raw[:], k.dram[mask].rearrange("(t p) s -> p t s", p=P)).then_inc(fetched_masks, 16)
                if weighted:
                    act.dma_start(prob[:], k.dram["prob"].rearrange("(t p) s -> p t s", p=P)).then_inc(fetched_masks, 16)
                act.wait_ge(fetched_masks, 32 if weighted else 16)

        normalize(k, k.x)

        kT = k.sb(f"{name}_kT", [P, B * SC], F32, ctx)
        keys = k.sb(f"{name}_keys", [P, B, heads, SC], F32, ctx) if heads > 1 else kT[:].rearrange("p (b h s) -> p b h s", b=B, h=1)
        vals = k.sb(f"{name}_vals", [P, B * 2, heads, dh + 1], F32, ctx)
        made = k.sem(f"{name}_kv_made", ctx)
        taken = k.sem(f"{name}_kv_taken", ctx)
        order = k.sem(f"{name}_kv_order", ctx)
        HALF = B * SC // 2
        chunks = ((0, P), (P, TAIL))
        with nc.Block() as block:
            @block.tensor
            def _(pe):
                for i in range(2):
                    nc.tensor.matmul(k.bank[i][:, 0:HALF], wk[:], k.ctxT[:, ds(i, HALF)], start=True,
                                     stop=True).then_inc(made, 1)
                for b in range(B):
                    for c, (at, n) in enumerate(chunks):
                        i = 2 * b + c
                        if i >= 4:
                            pe.wait_ge(taken, 2 + i - 3)
                        nc.tensor.matmul(k.bank[2 + i % 4][0:n, 0:D], k.ctxT[:, b * SC + at:b * SC + at + n], wv[:],
                                         start=True, stop=True).then_inc(made, 1)

            @block.vector
            def _(dve):
                step = Steps(dve, order)
                step.then(nc.vector.memset(vals[:], 1.0))
                for i in range(2):
                    dve.wait_ge(made, i + 1)
                    if biased:
                        ins = nc.vector.tensor_scalar(kT[:, ds(i, HALF)], k.bank[i][:, 0:HALF], bk[:, 0:1], None, ALU.add)
                    else:
                        ins = nc.vector.tensor_copy(kT[:, ds(i, HALF)], k.bank[i][:, 0:HALF])
                    ins.then_inc(taken, 1)
                for b in range(B):
                    for c, (at, n) in enumerate(chunks):
                        i = 2 * b + c
                        dve.wait_ge(made, 2 + i + 1)
                        nc.vector.tensor_tensor(vals[0:n, i, :, 0:dh],
                                                k.bank[2 + i % 4][0:n, 0:D].rearrange("p (h d) -> p h d", h=heads),
                                                bv[0:n, :].rearrange("p (h d) -> p h d", h=heads), ALU.add).then_inc(taken, 1)
                if mask_kind == "int":
                    nc.vector.tensor_scalar(added[:], mask_raw[:], 1.0, 1e9, ALU.subtract, ALU.mult)
                elif mask_kind == "where":
                    nc.vector.tensor_scalar(added[:], mask_raw[:], 0.0, -HUGE, ALU.is_equal, ALU.mult)

            if heads > 1:
                @block.gpsimd
                def _(pool):
                    for b in range(B):
                        pool.wait_ge(taken, b // 2 + 1)
                        nc.gpsimd.tensor_tensor(
                            keys[:, b, :, :], kT[:, None, ds(b, SC)].broadcast_to([P, heads, SC]),
                            k.headmask[:, :, None].broadcast_to([P, heads, SC]), ALU.mult)

        qT = k.sb(f"{name}_qT", [P, P], F32, ctx)
        probs = k.sb(f"{name}_probs", [P, 2, HG, SC], F32, ctx)
        used = k.sb(f"{name}_weighted", [P, 2, HG, SC], F32, ctx) if weighted else probs
        probsT = [k.sb(f"{name}_probsT{c}", [P, HG, P], F32, ctx) for c in range(2)]
        top = k.sb(f"{name}_top", [P, heads], F32, ctx)
        sums = k.sb(f"{name}_sums", [P, heads], F32, ctx)
        inv = k.sb(f"{name}_inv", [P, heads], F32, ctx)
        outs = k.sb(f"{name}_outs", [P, heads, dh], F32, ctx)
        outsT = k.sb(f"{name}_outsT", [P, P], F32, ctx)
        s = {n: k.sem(f"{name}_{n}", ctx) for n in ("q_made", "q_taken", "scored", "score_read", "centred", "exped",
                                                    "weighed", "turned", "copied", "mixed", "normed", "out_turned",
                                                    "out_copied", "projected", "added", "order", "summed", "prob_copied")}
        prob_tile = k.sb(f"{name}_prob_tile", [P, SC], F32, ctx) if weighted else None
        kv = keys[:] if heads > 1 else keys
        keys2 = kv.rearrange("p b h s -> p (b h s)")
        vals2 = vals[:].rearrange("p c h d -> p (c h d)")
        W1 = heads * (dh + 1)
        prob2 = prob[:].rearrange("p t s -> p (t s)") if weighted else None
        added2 = added[:].rearrange("p t s -> p (t s)")
        MIX, MISC = k.bank[6], k.bank[7]

        def tiles(eng):
            with eng.Fori(0, B) as b:
                with eng.Fori(0, TB // 2) as half:
                    for u in range(2):
                        yield b, b * TB + half * 2 + u, half * 2 + u, u

        def scores(g, u):
            slot = (u * NG + g) % 2
            return [k.bank[2 * slot + i][:, 0:PER_BANK * SC] for i in range(HG // PER_BANK)]

        with nc.Block() as block:
            @block.tensor
            def _(pe):
                for b, T, _, u in tiles(pe):
                    if project:
                        pe.wait_ge(s["added"], T + 1)
                    nc.tensor.matmul(MISC[:, 0:P], wq[:], k.xT[:, ds(T)], start=True, stop=True).then_inc(s["q_made"], 1)
                    pe.wait_ge(s["q_taken"], T + 1)

                    def score(g):
                        pe.wait_ge(s["score_read"], T * NG + g + 1)
                        for i, bank in enumerate(scores(g, u)):
                            at = (b * heads + g * HG + i * PER_BANK) * SC
                            ins = nc.tensor.matmul(bank, qT[:], keys2[:, bass.ds(at, PER_BANK * SC)], start=True, stop=True)
                        ins.then_inc(s["scored"], 1)

                    score(0)
                    for g in range(NG):
                        if g + 1 < NG:
                            score(g + 1)
                        pe.wait_ge(s["weighed" if weighted else "exped"], T * NG + g + 1 + weighted)
                        pe.wait_ge(s["copied"], T * NG + g + AHEAD)
                        slot = (u * NG + g) % 2
                        for h in range(HG):
                            nc.tensor.transpose(k.bank[4][:, ds(h)], used[:, slot, h, 0:P], k.ident[:])
                            ins = nc.tensor.transpose(k.bank[5][0:TAIL, ds(h)], used[:, slot, h, P:SC], k.ident[:])
                        ins.then_inc(s["turned"], 1)
                        pe.wait_ge(s["copied"], T * NG + g + 1 + AHEAD)
                        if g == 0:
                            pe.wait_ge(s["normed"], T + 1)
                        for h in range(HG):
                            hh = g * HG + h
                            mix = MIX[:, hh * (dh + 1):(hh + 1) * (dh + 1)]
                            for c, (at, n) in enumerate(chunks):
                                v = vals2[0:n, bass.ds((b * 2 + c) * W1 + hh * (dh + 1), dh + 1)]
                                ins = nc.tensor.matmul(mix, probsT[c][0:n, h, :], v, start=c == 0, stop=c == 1)
                    ins.then_inc(s["mixed"], 1)
                    if project:
                        pe.wait_ge(s["normed"], T + 2)
                        nc.tensor.transpose(MISC[:, ds(1)], outs[:].rearrange("p h d -> p (h d)"), k.ident[:]).then_inc(s["out_turned"], 1)
                        pe.wait_ge(s["out_copied"], T + 1)
                        nc.tensor.matmul(MISC[:, ds(2)], outsT[:], wo[:], start=True, stop=True).then_inc(s["projected"], 1)

            @block.scalar
            def _(act):
                nc.scalar.copy(outsT[:, 0:1], k.ident[:, 0:1]).then_inc(s["copied"], AHEAD)
                for b, T, _, u in tiles(act):
                    act.wait_ge(s["q_made"], T + 1)
                    if biased:
                        ins = nc.scalar.activation(qT[:], MISC[:, 0:P], ACT.Identity, bias=bq[:, 0:1])
                    else:
                        ins = nc.scalar.copy(qT[:], MISC[:, 0:P])
                    ins.then_inc(s["q_taken"], 1)

                    def exp(g):
                        act.wait_ge(s["centred"], T * NG + g + 1)
                        slot = (u * NG + g) % 2
                        nc.scalar.activation(probs[:, slot], probs[:, slot], ACT.Exp).then_inc(s["exped"], 1)

                    exp(0)
                    for g in range(NG):
                        if g + 1 < NG:
                            exp(g + 1)
                        act.wait_ge(s["turned"], T * NG + g + 1)
                        nc.scalar.copy(probsT[0][:], k.bank[4][:, 0:HG * P])
                        nc.scalar.copy(probsT[1][0:TAIL], k.bank[5][0:TAIL, 0:HG * P]).then_inc(s["copied"], 1)
                    if project:
                        act.wait_ge(s["out_turned"], T + 1)
                        nc.scalar.copy(outsT[:], MISC[:, ds(1)]).then_inc(s["out_copied"], 1)

            @block.vector
            def _(dve):
                step = Steps(dve, s["order"])
                nc.vector.memset(sums[:], 1.0).then_inc(s["score_read"], AHEAD)
                nc.vector.memset(inv[:], 1.0).then_inc(s["summed"], AHEAD)
                free_at_first(dve, s["normed"], s["added"])
                if project:
                    x = k.x[:].rearrange("p (t d) -> p t d", d=D)
                    step.then(nc.vector.tensor_tensor(x, x, bo[:, None, :].broadcast_to([P, NT, D]), ALU.add))
                per = NG + 1 + (mask_kind == "where")
                start = step.n
                for b, T, t, u in tiles(dve):
                    step.start, step.index, step.per, step.n = start, T, per, 0

                    def total(g):
                        dve.wait_ge(s["exped"], T * NG + g + 1)
                        nc.vector.tensor_reduce(sums[:, g * HG:(g + 1) * HG], probs[:, (u * NG + g) % 2], AX_X, ALU.add).then_inc(s["summed"], 1)

                    for g in range(NG):
                        slot = (u * NG + g) % 2
                        tile = probs[:, slot]
                        mt = added2[:, ds(T if mask_tiles == NT else t, SC)]
                        dve.wait_ge(s["scored"], T * NG + g + 1)
                        dve.wait_ge(s["copied"], T * NG + g + 1)
                        if weighted:
                            dve.wait_ge(s["summed"], T * NG + g + 1)
                        for i, bank in enumerate(scores(g, u)):
                            ins = nc.vector.scalar_tensor_tensor(
                                tile[:, i * PER_BANK:(i + 1) * PER_BANK, :], bank.rearrange("p (h s) -> p h s", s=SC), scale,
                                mt[:, None, :].broadcast_to([P, PER_BANK, SC]), ALU.mult, ALU.add)
                        ins.then_inc(s["score_read"], 1)
                        dve.wait_ge(s["score_read"], T * NG + g + 1 + AHEAD)
                        hs = slice(g * HG, (g + 1) * HG)
                        step.then(nc.vector.tensor_reduce(top[:, hs], tile, AX_X, ALU.max))
                        nc.vector.tensor_tensor(tile, tile, top[:, hs, None].broadcast_to([P, HG, SC]), ALU.subtract).then_inc(s["centred"], 1)
                        if weighted and g > 0:
                            total(g - 1)
                    if weighted:
                        total(NG - 1)
                        dve.wait_ge(s["summed"], (T + 1) * NG + AHEAD)
                    dve.wait_ge(s["mixed"], T + 1)
                    mix = MIX[:, 0:W1].rearrange("p (h d) -> p h d", h=heads)
                    step.then(nc.vector.reciprocal(inv[:], sums[:] if weighted else mix[:, :, dh]))
                    if mask_kind == "where":
                        step.then(nc.vector.scalar_tensor_tensor(inv[:], top[:], -HUGE / 4, inv[:], ALU.is_gt, ALU.mult))
                    if project:
                        nc.vector.tensor_tensor(outs[:], mix[:, :, 0:dh], inv[:, :, None].broadcast_to([P, heads, dh]),
                                                ALU.mult).then_inc(s["normed"], 1)
                        dve.wait_ge(s["projected"], T + 1)
                        nc.vector.tensor_tensor(k.x[:, ds(T)], MISC[:, ds(2)], k.x[:, ds(T)], ALU.add).then_inc(s["added"], 1)
                    else:
                        nc.vector.scalar_tensor_tensor(k.x[:, ds(T)], MIX[:, 0:D], inv[:, 0:1], k.x[:, ds(T)],
                                                       ALU.mult, ALU.add).then_inc(s["normed"], 1)
                    assert step.n == NG + 1 + (mask_kind == "where")

            if weighted:
                @block.gpsimd
                def _(pool):
                    free_at_first(pool, s["weighed"])
                    for b, T, t, u in tiles(pool):
                        pool.wait_ge(s["weighed"], T * NG + 1)
                        nc.gpsimd.tensor_copy(prob_tile[:], prob2[:, ds(T, SC)]).then_inc(s["prob_copied"], 1)
                        pool.wait_ge(s["prob_copied"], T + 1)
                        for g in range(NG):
                            slot = (u * NG + g) % 2
                            pool.wait_ge(s["exped"], T * NG + g + 1)
                            pool.wait_ge(s["copied"], T * NG + g + 1)
                            nc.gpsimd.tensor_tensor(used[:, slot], probs[:, slot],
                                                    prob_tile[:, None, :].broadcast_to([P, HG, SC]),
                                                    ALU.mult).then_inc(s["weighed"], 1)


def stage_1x(k):
    cross_attention(k, "a1", H16, "mask1", "int", DH ** -0.5, biased=True, weighted=True, project=True)


def stage_2x(k):
    cross_attention(k, "a2", 1, "mask2", "float", D ** -0.5, biased=False, weighted=False, project=False)


def stage_3x(k):
    cross_attention(k, "a3", H16, "mask3", "where", DH ** -0.5, biased=True, weighted=False, project=True)


def program(nc, dram, out):
    with ExitStack() as ctx:
        k = Core(nc, ctx, dram)
        loaded = k.sem("x_loaded")
        stored = k.sem("x_stored")
        x_tiles = k.x[:].rearrange("p (t d) -> p t d", d=D)
        with nc.Block() as block:
            @block.tensor
            def _(pe):
                free_at_first(pe, k.ln_turned, k.ln_stored)

            @block.sync
            def _(sp):
                sp.dma_start(x_tiles, dram["x"].rearrange("(t p) d -> p t d", p=P)).then_inc(loaded, 16)
                sp.dma_start(k.ident[:], dram["identity"]).then_inc(loaded, 16)
                sp.dma_start(k.headmask[:], dram["headmask"]).then_inc(loaded, 16)
                sp.dma_start(k.ctxT[:], dram["ctxT"]).then_inc(loaded, 16)
                sp.wait_ge(loaded, 64)
        for stage in (stage_0x, stage_0f, stage_1x, stage_1f, stage_2x, stage_lora, stage_3x, stage_3f):
            stage(k)
        with nc.Block() as block:
            @block.sync
            def _(sp):
                sp.dma_start(out.rearrange("(t p) d -> p t d", p=P), x_tiles).then_inc(stored, 16)
                sp.wait_ge(stored, 16)


def constants():
    part = np.arange(P)
    freq = (1.0 / np.float32(10000.0) ** (np.arange(0, D, 2, dtype=np.float32) / np.float32(D))).astype(np.float64)
    angle = np.concatenate([freq, freq])[:, None] * np.arange(S)[None, :]
    sign = np.where(part < D // 2, 1.0, -1.0)[:, None]
    f = {
        "identity": np.eye(P),
        "headmask": (part[:, None] // DH == np.arange(H16)[None, :]),
        "rot_cos": np.cos(angle),
        "rot_sin": np.sin(angle) * sign,
        "key_waves": np.where(part[:, None] < D // 2, np.sin(angle), np.cos(angle)),
        "before": part[:, None] < part[None, :],
        "iota32": np.tile(np.arange(E1), (P, 1)),
        "iota16": np.tile(np.arange(E0), (P, 1)),
        "slot_base": np.tile(np.arange(E0) * CAP, (P, 1)),
        "spare_slot": SLOTS + np.arange(NT)[None, :] * P + part[:, None],
    }
    c = {n: np.ascontiguousarray(v, dtype=np.float32) for n, v in f.items()}
    bits = (1 << (MAG_BITS - 1 - np.arange(MAG_BITS))).astype(np.int32)
    c["bits"] = np.ascontiguousarray(np.tile(np.repeat(bits, E0), (P, 1)))
    return c


def laid_out(i):
    row = lambda v: np.broadcast_to(v.reshape(1, -1), (P, v.size))
    col = lambda v: v.reshape(-1, P).T
    a = {
        "x": i["x"].reshape(NTOK, D),
        "ctx": i["ctx_1024"],
        "ctxT": i["ctx_1024"].reshape(B * SC, D).T,
        "prob": i["fside_BxSxS2_0"].reshape(NTOK, SC),
        "mask1": i["mask_BxSxS2_ik1"].reshape(NTOK, SC),
        "mask2": i["mask_SxS2_fk0"],
        "mask3": i["mask_1x1xSxS2_ik0"].reshape(S, SC),
        "a0_ln": np.stack([i["L0_xattn_gamma_media"], i["L0_xattn_beta_media"], i["L0_xattn_gamma_lat"], i["L0_xattn_beta_lat"]], 1),
        "a0_wq": i["L0_xattn_Wq"], "a0_bq": col(i["L0_xattn_bq"]),
        "a0_wkv": i["L0_xattn_Wkv"], "a0_bkv": col(i["L0_xattn_bkv"]),
        "a0_wo": i["L0_xattn_Wo"].reshape(8, P, D).transpose(1, 0, 2).reshape(P, -1), "a0_bo": row(i["L0_xattn_bo"]),
        "m0_gate_w": i["L0_ffn_gate_w"], "m0_gate_b": row(i["L0_ffn_gate_b"]),
        "m0_w13": np.concatenate([i["L0_ffn_ew1"], i["L0_ffn_ew3"]], 2),
        "m0_w2": i["L0_ffn_ew2"].reshape(E0, 2, P, D).transpose(0, 2, 1, 3).reshape(E0, P, 2 * D),
        "s0_w1": i["L0_ffn_sw1"].transpose(1, 0, 2).reshape(P, -1),
        "s0_w3": i["L0_ffn_sw3"].transpose(1, 0, 2).reshape(P, -1),
        "s0_w2": i["L0_ffn_sw2"].reshape(S0 * 2, P, D).transpose(1, 0, 2).reshape(P, -1),
        "a1_wq": i["L1_xattn_wq_k"], "a1_bq": col(i["L1_xattn_wq_b"]), "a1_wk": i["L1_xattn_wk_k"],
        "a1_bk": col(i["L1_xattn_wk_b"]), "a1_wv": i["L1_xattn_wv_k"], "a1_bv": row(i["L1_xattn_wv_b"]),
        "a1_wo": i["L1_xattn_wo_k"], "a1_bo": row(i["L1_xattn_wo_b"]),
        "f1_ln1": np.stack([i["L1_ffn_ln1_g"], i["L1_ffn_ln1_b"]], 1), "f1_ln2": np.stack([i["L1_ffn_ln2_g"], i["L1_ffn_ln2_b"]], 1),
        "f1_wq": i["L1_ffn_wq"], "f1_wk": i["L1_ffn_wk"], "f1_wv": i["L1_ffn_wv"], "f1_wo": i["L1_ffn_wo"],
        "f1_wpT": i["L1_ffn_wp"].T, "f1_wpT_swapped": np.roll(i["L1_ffn_wp"], D // 2, axis=0).T,
        "m1_sel": i["L1_ffn_sel_w"],
        "m1_w": np.concatenate([i["L1_ffn_keys"], i["L1_ffn_values"]], 2),
        "a2_wq": i["L2_xattn_Wq"].T, "a2_wk": i["L2_xattn_Wk"].T, "a2_wv": i["L2_xattn_Wv"].T, "a2_bv": row(i["L2_xattn_bv"]),
        "lora_wT": i["L2_ffn_W"].T, "lora_b": row(i["L2_ffn_b"]), "lora_downT": i["L2_ffn_lora_down"].T,
        "lora_down_aux": i["L2_ffn_down_aux"], "lora_upT": i["L2_ffn_lora_up"].T, "lora_up_auxT": i["L2_ffn_up_aux"].T,
        "a3_wq": i["L3_xattn_Wq"].T, "a3_bq": col(i["L3_xattn_bq"]), "a3_wk": i["L3_xattn_Wk"].T, "a3_bk": col(i["L3_xattn_bk"]),
        "a3_wv": i["L3_xattn_Wv"].T, "a3_bv": row(i["L3_xattn_bv"]), "a3_wo": i["L3_xattn_Wo"].T, "a3_bo": row(i["L3_xattn_bo"]),
        "f3_fc": i["L3_ffn_w_fc"].reshape(HID3 // P, P, D).transpose(1, 0, 2).reshape(P, -1),
        "f3_proj": i["L3_ffn_w_proj"], "f3_uT": i["L3_ffn_u"].T, "f3_v": i["L3_ffn_v"], "f3_bT": i["L3_ffn_fast_b"].T,
        "f3_gate": row(i["L3_ffn_gate"]),
    }
    return {n: np.ascontiguousarray(v) for n, v in a.items()} | constants()


def kernel(**inputs):
    import concourse.bacc as bacc
    from concourse.bass_utils import run_bass_kernel_spmd

    nc = bacc.Bacc("TRN2", target_bir_lowering=False, num_devices=1)
    arrays = laid_out({n: np.asarray(v) for n, v in inputs.items()})
    dram = {n: nc.dram_tensor(n + "_dram", a.shape, mybir.dt.from_np(a.dtype), kind="ExternalInput").ap()
            for n, a in arrays.items()}
    out = nc.dram_tensor("out_dram", (NTOK, D), F32, kind="ExternalOutput").ap()
    program(nc, dram, out)
    r = run_bass_kernel_spmd(nc, [{n + "_dram": a for n, a in arrays.items()}], core_ids=[0])
    return r.results[0]["out_dram"].reshape(B, S, D)
```

```python
from contextlib import ExitStack

import concourse.bass as bass
import numpy as np
from concourse import mybir

F32 = mybir.dt.float32
F32R = mybir.dt.float32r
BF16 = mybir.dt.bfloat16
I32 = mybir.dt.int32
U32 = mybir.dt.uint32
ALU = mybir.AluOpType
ACT = mybir.ActivationFunctionType
AX_X = mybir.AxisListType.X

P = 128
D = 128
B = 4
S = 512
TB = S // P
NT = B * TB
NTOK = B * S
SC = 154
TAIL = SC - P
H16 = 16
DH = D // H16
E0, K0, HID0, S0 = 16, 2, 256, 2
CAP = -(-NTOK * K0 * 5 // (E0 * 4))
E1, K1 = 32, 4
HID3 = 512
SLOTS = E0 * CAP
MAG_BITS = 31
HUGE = 1.0e38
EPS = 1e-5


def ds(i, n=P):
    return bass.ds(i * n, n)


class Steps:

    def __init__(self, eng, sem):
        self.eng, self.sem, self.start, self.index, self.per, self.n = eng, sem, 0, None, 0, 0

    def then(self, ins):
        self.n += 1
        ins.then_inc(self.sem, 1)
        at = self.start + self.n
        self.eng.wait_ge(self.sem, at if self.index is None else self.index * self.per + at)
        return ins

    def turn(self, index, per):
        self.start, self.index, self.per, self.n = self.start + self.n if self.index is None else self.start, index, per, 0

    def turns_end(self, turns):
        assert self.n == self.per, (self.n, self.per)
        self.start, self.index, self.n = self.start + turns * self.per, None, 0


def free_at_first(eng, *sems, by=1):
    for s in sems:
        eng.sem_inc(s, by)


def over_batches(eng, heads, lead, first, steps, last):
    with eng.Fori(0, B) as b:
        first(b)
        if lead:
            steps(b, 0, 0, lead)
        with eng.Fori(0, TB - 1) as t:
            steps(b, t, lead, heads + lead)
        steps(b, TB - 1, lead, heads)
        last(b)


class Scope(ExitStack):

    def __init__(self, k):
        super().__init__()
        self.nc, self.sems = k.nc, []

    def __exit__(self, *error):
        if error[0] is None:
            numbers = sorted(s.num for s in self.sems)
            while numbers:
                run = next((i for i in range(1, len(numbers)) if numbers[i] != numbers[i - 1] + 1), len(numbers))
                self.nc.all_engine_barrier(sems_to_clear=range(numbers[0], numbers[run - 1] + 1))
                numbers = numbers[run:]
        return super().__exit__(*error)


class Core:

    def __init__(self, nc, ctx, dram):
        self.nc, self.dram, self.ctx = nc, dram, ctx
        self.x = self.sb("x_rows", [P, NT * D])
        self.xT = self.sb("xn_cols", [P, NTOK])
        self.norm = self.sb("norm_rows", [P, NT * D])
        self.stats = self.sb("bn_stats_out", [P, NT * 6])
        self.mv = self.sb("mean_var", [P, NT, 2])
        self.rstd = self.sb("rstd", [P, 4, NT])
        self.ident = self.sb("identity", [P, P])
        self.headmask = self.sb("headmask", [P, H16])
        self.ctxT = self.sb("ctx_cols", [P, B * SC])
        self.psum = ctx.enter_context(nc.psum_tensor("psum", [P, 8, 512], F32))
        self.bank = [self.psum[:, i, :] for i in range(8)]
        self.norms = self.ln_turns = 0
        self.ln_order = self.sem("ln_order")
        self.ln_var = self.sem("ln_var")
        self.ln_sqrt = self.sem("ln_sqrt")
        self.ln_normed = self.sem("ln_normed")
        self.ln_turned = self.sem("ln_turned")
        self.ln_steps = 0

    def sb(self, name, shape, dt=F32, ctx=None):
        return (ctx or self.ctx).enter_context(self.nc.sbuf_tensor(name, shape, dt))

    def sem(self, name, ctx=None):
        s = (ctx or self.ctx).enter_context(self.nc.semaphore(name))
        if ctx is not None:
            ctx.sems.append(s)
        return s


def load(k, ctx, name, parts=P):
    return k.sb(name, [parts, k.dram[name].shape[1]], F32, ctx)


def fetch(k, pairs, ctx):
    nc = k.nc
    done = k.sem("fetched_" + pairs[0][0], ctx)
    with nc.Block() as block:
        @block.sync
        def _(sp):
            for name, home in pairs:
                sp.dma_start(home[:], k.dram[name]).then_inc(done, 16)
            sp.wait_ge(done, 16 * len(pairs))


def normalize(k, src, gain=None, bias=None, rows=None, turned=True, loads=None):
    nc = k.nc
    n, k.norms = k.norms, k.norms + 1
    turns, k.ln_turns = k.ln_turns, k.ln_turns + turned
    steps0 = k.ln_steps
    k.ln_steps += 7
    r = k.rstd
    to = k.norm[:] if rows is None else rows
    pairs, ctx = loads or ((), None)
    loaded = k.sem("fetched_" + pairs[0][0], ctx) if pairs else None
    with nc.Block() as block:
        @block.sync
        def _(sp):
            for name, home in pairs:
                sp.dma_start(home[:], k.dram[name]).then_inc(loaded, 16)
            if pairs:
                sp.wait_ge(loaded, 16 * len(pairs))

        @block.vector
        def _(dve):
            step = Steps(dve, k.ln_order)
            step.start = steps0
            for T in range(NT):
                ins = nc.vector.bn_stats(k.stats[:, ds(T, 6)], src[:, ds(T)])
            step.then(ins)
            for T in range(NT):
                ins = nc.vector.bn_aggr(k.mv[:, T, :], k.stats[:, ds(T, 6)])
            step.then(ins)
            nc.vector.tensor_scalar(r[:, 0, :], k.mv[:, :, 1], EPS, None, ALU.add).then_inc(k.ln_var, 1)
            dve.wait_ge(k.ln_var, n + 1)
            dve.wait_ge(k.ln_sqrt, n + 1)
            step.then(nc.vector.reciprocal(r[:, 1, :], r[:, 1, :]))
            step.then(nc.vector.tensor_tensor(r[:, 2, :], r[:, 1, :], r[:, 1, :], ALU.mult))
            step.then(nc.vector.tensor_tensor(r[:, 2, :], r[:, 2, :], r[:, 0, :], ALU.mult))
            step.then(nc.vector.tensor_scalar(r[:, 2, :], r[:, 2, :], -0.5, 1.5, ALU.mult, ALU.add))
            step.then(nc.vector.tensor_tensor(r[:, 3, :], r[:, 2, :], r[:, 1, :], ALU.mult))
            for T in range(NT):
                nc.vector.tensor_scalar(to[:, ds(T)], src[:, ds(T)], k.mv[:, T, 0:1], r[:, 3, T:T + 1], ALU.subtract,
                                        ALU.mult).then_inc(k.ln_normed, 1)

        @block.scalar
        def _(act):
            act.wait_ge(k.ln_var, n + 1)
            nc.scalar.activation(r[:, 1, :], r[:, 0, :], ACT.Sqrt).then_inc(k.ln_sqrt, 1)
            if turned:
                if gain is not None and pairs:
                    act.wait_ge(loaded, 16 * len(pairs))
                for b in range(B):
                    act.wait_ge(k.ln_turned, turns * B + b + 1)
                    if gain is None:
                        nc.scalar.copy(k.xT[:, ds(b, S)], k.bank[b])
                    else:
                        nc.scalar.activation(k.xT[:, ds(b, S)], k.bank[b], ACT.Identity, scale=gain, bias=bias)

        if turned:
            @block.tensor
            def _(pe):
                for T in range(NT):
                    pe.wait_ge(k.ln_normed, n * NT + T + 1)
                    ins = nc.tensor.transpose(k.bank[T // TB][:, ds(T % TB)], to[:, ds(T)], k.ident[:])
                    if T % TB == TB - 1:
                        ins.then_inc(k.ln_turned, 1)


def add_projection(k, ctx, name, outs, wo, home):
    nc = k.nc
    outsT = k.sb(f"{name}_outsT", [P, NT * P], F32, ctx)
    out_turned, out_copied, projected = (k.sem(f"{name}_{n}", ctx) for n in ("out_turned", "out_copied", "projected"))
    with nc.Block() as block:
        @block.tensor
        def _(pe):
            for T in range(NT):
                ins = nc.tensor.transpose(k.bank[T // TB][:, ds(T % TB)], outs[:, T, :], k.ident[:])
                if T % TB == TB - 1:
                    ins.then_inc(out_turned, 1)
            for b in range(B):
                pe.wait_ge(out_copied, b + 1)
                for t in range(TB):
                    ins = nc.tensor.matmul(k.bank[4 + b][:, ds(t)], outsT[:, ds(b * TB + t)], wo[:], start=True, stop=True)
                ins.then_inc(projected, 1)

        @block.scalar
        def _(act):
            for b in range(B):
                act.wait_ge(out_turned, b + 1)
                nc.scalar.copy(outsT[:, ds(b, S)], k.bank[b]).then_inc(out_copied, 1)

        @block.vector
        def _(dve):
            for b in range(B):
                dve.wait_ge(projected, b + 1)
                nc.vector.tensor_tensor(home[:, ds(b, S)], k.bank[4 + b], home[:, ds(b, S)], ALU.add)


def first_hit(nc, step, left, hit, best, first, iota, far, shape):
    step.then(nc.vector.tensor_reduce(best[:], left[:], AX_X, ALU.max))
    step.then(nc.vector.tensor_tensor(hit[:], left[:], best[:, :, None].broadcast_to(shape), ALU.is_equal))
    step.then(nc.vector.scalar_tensor_tensor(hit[:], hit[:], -100.0, far[:, None, :].broadcast_to(shape), ALU.mult, ALU.add))
    step.then(nc.vector.tensor_reduce(first[:], hit[:], AX_X, ALU.min))
    step.then(nc.vector.tensor_tensor(hit[:], iota[:, None, :].broadcast_to(shape), first[:, :, None].broadcast_to(shape), ALU.is_equal))


def stage_0x(k):
    nc = k.nc
    H = 8
    KEYS = SC + S
    CHUNKS = -(-KEYS // P)
    LAST = KEYS - (CHUNKS - 1) * P
    HALF = KEYS // 2
    WIDE = HALF + HALF % 2
    HB = TB * H
    scale = P ** -0.5
    with Scope(k) as ctx:
        names = ("a0_ln", "a0_wq", "a0_bq", "a0_wk", "a0_wvT", "a0_bk", "a0_bv", "a0_wo", "a0_bo")
        ln, wq, bq, wk, wvT, bk, bv, wo, bo = homes = [load(k, ctx, n) for n in names]
        CT = 2 * B
        rows = k.sb("a0_ctx_rows", [P, CT, D], F32, ctx)
        cT = k.sb("a0_ctxT", [P, B * SC], F32, ctx)
        xn = k.sb("a0_xn", [P, NT * D], F32, ctx)
        fetched, rows_in = k.sem("a0_fetched", ctx), k.sem("a0_rows_in", ctx)
        with nc.Block() as block:
            @block.sync
            def _(sp):
                for n, home in zip(names, homes):
                    sp.dma_start(home[:], k.dram[n]).then_inc(fetched, 16)
                sp.wait_ge(fetched, 16 * len(names))

            @block.scalar
            def _(act):
                r = rows[:].rearrange("p (b c) d -> p b c d", c=2)
                act.dma_start(r[:, :, 0, :], k.dram["ctx"][:, 0:P, :].rearrange("b p d -> p b d")).then_inc(rows_in, 16)
                act.dma_start(r[0:TAIL, :, 1, :], k.dram["ctx"][:, P:SC, :].rearrange("b p d -> p b d")).then_inc(rows_in, 16)
                act.wait_ge(rows_in, 32)

        sizes = [(P, TAIL)[i % 2] for i in range(CT)]
        stats = k.sb("a0_ctx_stats", [P, CT, 6], F32, ctx)
        mv = k.sb("a0_ctx_mv", [P, CT, 2], F32, ctx)
        r = k.sb("a0_ctx_rstd", [P, 4, CT], F32, ctx)
        order, var, root, turned, stored = (k.sem(f"a0_ctx_{n}", ctx) for n in ("order", "var", "root", "turned", "stored"))
        with nc.Block() as block:
            @block.vector
            def _(dve):
                step = Steps(dve, order)
                nc.vector.memset(stats[:], 0.0)
                step.then(nc.vector.memset(mv[:], 1.0))
                for i, n in enumerate(sizes):
                    ins = nc.vector.bn_stats(stats[0:n, i, :], rows[0:n, i, :])
                step.then(ins)
                for i, n in enumerate(sizes):
                    ins = nc.vector.bn_aggr(mv[0:n, i, :], stats[0:n, i, :])
                step.then(ins)
                nc.vector.tensor_scalar(r[:, 0, :], mv[:, :, 1], EPS, None, ALU.add).then_inc(var, 1)
                dve.wait_ge(root, 1)
                step.then(nc.vector.reciprocal(r[:, 1, :], r[:, 1, :]))
                step.then(nc.vector.tensor_tensor(r[:, 2, :], r[:, 1, :], r[:, 1, :], ALU.mult))
                step.then(nc.vector.tensor_tensor(r[:, 2, :], r[:, 2, :], r[:, 0, :], ALU.mult))
                step.then(nc.vector.tensor_scalar(r[:, 2, :], r[:, 2, :], -0.5, 1.5, ALU.mult, ALU.add))
                step.then(nc.vector.tensor_tensor(r[:, 3, :], r[:, 2, :], r[:, 1, :], ALU.mult))
                for i, n in enumerate(sizes):
                    nc.vector.tensor_scalar(rows[0:n, i, :], rows[0:n, i, :], mv[0:n, i, 0:1], r[0:n, 3, i:i + 1],
                                            ALU.subtract, ALU.mult).then_inc(stored, 1)

            @block.scalar
            def _(act):
                act.wait_ge(var, 1)
                nc.scalar.activation(r[:, 1, :], r[:, 0, :], ACT.Sqrt).then_inc(root, 1)
                for b in range(B):
                    act.wait_ge(turned, b + 1)
                    nc.scalar.activation(cT[:, ds(b, SC)], k.bank[b][:, 0:SC], ACT.Identity, scale=ln[:, 0:1], bias=ln[:, 1:2])

            @block.tensor
            def _(pe):
                for i, n in enumerate(sizes):
                    pe.wait_ge(stored, i + 1)
                    ins = nc.tensor.transpose(k.bank[i // 2][:, (i % 2) * P:(i % 2) * P + n], rows[0:n, i, :], k.ident[0:n, 0:n])
                    if i % 2:
                        ins.then_inc(turned, 1)
        normalize(k, k.x, rows=xn, turned=False)
        normalize(k, xn, ln[:, 2:3], ln[:, 3:4])

        w_vo = k.sb("a0_w_vo", [P, H, D], F32, ctx)
        b_vo = k.sb("a0_b_vo", [P, H, D], F32, ctx)
        bv_columns = k.sb("a0_bv_columns", [P, H, P], F32, ctx)
        bq_scaled = k.sb("a0_bq_scaled", [P, H], F32, ctx)
        k_high = k.sb("a0_k_high", [P, H, 2 * WIDE], F32R, ctx)
        k_low = k.sb("a0_k_low", [P, H, 2 * WIDE], F32R, ctx)
        spread, scaled, folded, folded_b = (k.sem(f"a0_{n}", ctx) for n in ("bv_spread", "bq_scaled", "w_folded", "b_folded"))
        with nc.Block() as block:
            @block.tensor
            def _(pe):
                for h in range(H):
                    ins = nc.tensor.matmul(k.bank[h // 4][:, ds(h % 4)], wvT[:, ds(h)], wo[:, ds(h)], start=True, stop=True)
                ins.then_inc(folded, 1)
                pe.wait_ge(spread, 1)
                for h in range(H):
                    ins = nc.tensor.matmul(k.bank[2 + h // 4][:, ds(h % 4)], bv_columns[:, h, :], wo[:, ds(h)], start=True, stop=True)
                ins.then_inc(folded_b, 1)

            @block.scalar
            def _(act):
                act.wait_ge(folded, 1)
                for i in range(2):
                    nc.scalar.copy(w_vo[:, 4 * i:4 * i + 4, :], k.bank[i].rearrange("p (h d) -> p h d", h=4))

            @block.vector
            def _(dve):
                nc.vector.tensor_copy(bv_columns[:], bv[:, :, None].broadcast_to([P, H, P])).then_inc(spread, 1)
                nc.vector.tensor_scalar(bq_scaled[:], bq[:], scale, None, ALU.mult).then_inc(scaled, 1)
                dve.wait_ge(scaled, 1)
                x = k.x[:].rearrange("p (t d) -> p t d", d=D)
                nc.vector.tensor_tensor(x, x, bo[:, None, :].broadcast_to([P, NT, D]), ALU.add)
                for cut in (k_high, k_low):
                    for i in range(2):
                        nc.vector.tensor_scalar(cut[:, :, i * WIDE + HALF], bq_scaled[:], 0.0, None, ALU.mult)
                dve.wait_ge(folded_b, 1)
                for i in range(2):
                    nc.vector.tensor_copy(b_vo[:, 4 * i:4 * i + 4, :], k.bank[2 + i].rearrange("p (h d) -> p h d", h=4))

        inputs = k.sb("a0_inputs", [P, KEYS], F32, ctx)
        q_all = k.sb("a0_q", [P, H, S], F32, ctx)
        q_high = k.sb("a0_q_high", [P, H, P], F32R, ctx)
        q_low = k.sb("a0_q_low", [P, H, P], F32R, ctx)
        q_now = k.sb("a0_q_now", [P, 4, P], F32, ctx)
        one = k.sb("a0_one", [P, 4], F32, ctx)
        vo = k.sb("a0_vo", [P, CHUNKS, H * D], F32, ctx)
        probs = k.sb("a0_probs", [P, 2, KEYS], F32, ctx)
        probsT = k.sb("a0_probsT", [P, 2, CHUNKS, P], F32, ctx)
        negmax = k.sb("a0_negmax", [P, H], F32, ctx)
        sums = k.sb("a0_sums", [P, H], F32, ctx)
        inv = k.sb("a0_inv", [P, H], F32, ctx)
        s = {n: k.sem(f"a0_{n}", ctx) for n in ("inputs_ready", "k_made", "k_high_made", "k_low_made", "q_made", "q_taken", "q_cut", "q_fetched",
                                                "q_high_made", "vo_made", "vo_taken", "scored", "maxed", "exped", "turned",
                                                "copied_a", "copied_v", "mixed", "inverted", "added")}
        w_vo2 = w_vo[:].rearrange("p h d -> p (h d)")
        b_vo2 = b_vo[:].rearrange("p h d -> p (h d)")
        q_flat = q_all[:].rearrange("p h n -> p (h n)")
        PARTS = ((0, 0, 0, SC), (1, 0, SC, HALF - SC), (1, HALF - SC, WIDE, HALF))
        rows_of = lambda c: P if c < CHUNKS - 1 else LAST

        def heads_before(b, t, h):
            return b * HB + t * H + h

        def ahead(t, h):
            return h < H or not isinstance(t, int) or t < TB - 1

        with nc.Block() as block:
            @block.tensor
            def _(pe):
                def score(b, t, h):
                    if h % 4 == 0:
                        pe.wait_ge(s["q_cut"], (b * TB + t) * 2 + h // 4 + 2)
                    pe.wait_ge(s["exped"], heads_before(b, t, h) + 1)
                    n = h % H
                    for i in range(2):
                        bank = k.bank[2 * (h % 2) + i][:, 0:WIDE]
                        nc.tensor.matmul(bank, q_high[:, n, :], k_high[:, n, ds(i, WIDE)], start=True, stop=False)
                        nc.tensor.matmul(bank, q_high[:, n, :], k_low[:, n, ds(i, WIDE)], start=False, stop=False)
                        ins = nc.tensor.matmul(bank, q_low[:, n, :], k_high[:, n, ds(i, WIDE)], start=False, stop=True)
                    ins.then_inc(s["scored"], 1)

                def turn(b, t, h):
                    pe.wait_ge(s["exped"], heads_before(b, t, h) + 3)
                    pe.wait_ge(s["copied_a"], heads_before(b, t, h) + 1)
                    pe.wait_ge(s["copied_v"], heads_before(b, t, h) + 1)
                    for c in range(CHUNKS):
                        n = rows_of(c)
                        ins = nc.tensor.transpose(k.bank[4 + c // 4][0:n, ds(c % 4)], probs[:, h % 2, c * P:c * P + n], k.ident[:])
                    ins.then_inc(s["turned"], 1)

                def mix(b, t, h):
                    pe.wait_ge(s["copied_a"], heads_before(b, t, h) + 2)
                    pe.wait_ge(s["copied_v"], heads_before(b, t, h) + 2)
                    pe.wait_ge(s["added"], heads_before(b, t, h) + 1)
                    for c in range(CHUNKS):
                        n = rows_of(c)
                        ins = nc.tensor.matmul(k.bank[6 + h % 2][:, 0:D], probsT[0:n, h % 2, c, :], vo[0:n, c, ds(h)],
                                               start=c == 0, stop=c == CHUNKS - 1)
                    ins.then_inc(s["mixed"], 1)

                def first(b):
                    pe.wait_ge(s["added"], b * HB + 2)
                    for h in range(H):
                        pe.wait_ge(s["k_low_made"], b * H + h + 1)
                        nc.tensor.matmul(k.bank[2 * (h % 2)][:, 0:SC], wk[:, ds(h)], cT[:, ds(b, SC)], start=True, stop=True)
                        nc.tensor.matmul(k.bank[2 * (h % 2) + 1], wk[:, ds(h)], k.xT[:, ds(b, S)], start=True, stop=True).then_inc(s["k_made"], 1)
                        pe.wait_ge(s["q_taken"], b * H + h + 1)
                        nc.tensor.matmul(k.bank[6 + h % 2], wq[:, ds(h)], k.xT[:, ds(b, S)], start=True, stop=True).then_inc(s["q_made"], 1)
                    pe.wait_ge(s["inputs_ready"], b + 1)
                    for c in range(CHUNKS):
                        n = rows_of(c)
                        if c == 1:
                            pe.wait_ge(s["q_taken"], b * H + H + 2)
                        pe.wait_ge(s["vo_taken"], b * CHUNKS + c + 1)
                        for i in range(2):
                            ins = nc.tensor.matmul(k.bank[4 + 2 * (c % 2) + i][0:n, :], inputs[:, c * P:c * P + n], w_vo2[:, ds(i, 4 * D)],
                                                   start=True, stop=True)
                        ins.then_inc(s["vo_made"], 1)
                    pe.wait_ge(s["k_low_made"], b * H + H + 2)
                    score(b, 0, 0)
                    pe.wait_ge(s["vo_taken"], b * CHUNKS + CHUNKS + 2)

                def steps(b, t, start, end):
                    for h in range(start, end):
                        if ahead(t, h + 1):
                            score(b, t, h + 1)
                        turn(b, t, h)
                        if h > 0:
                            mix(b, t, h - 1)

                over_batches(pe, H, 1, first, steps, lambda b: mix(b, TB - 1, H - 1))

            @block.gpsimd
            def _(pool):
                def cut(b, t, half):
                    heads = slice(4 * half, 4 * half + 4)
                    n = (b * TB + t) * 2 + half
                    if isinstance(t, int) and t == 0:
                        q = q_all[:, heads, 0:P]
                    else:
                        pool.wait_ge(s["q_cut"], n + 1)
                        q = q_now[:]
                        nc.gpsimd.tensor_copy(q, q_all[:, heads, bass.ds(t * P, P)]).then_inc(s["q_fetched"], 1)
                        pool.wait_ge(s["q_fetched"], b * (2 * TB - 2) + t * 2 + half - 1)
                    nc.gpsimd.tensor_tensor(q_high[:, heads, :], q, one[:, :, None].broadcast_to([P, 4, P]), ALU.mult).then_inc(s["q_high_made"], 1)
                    pool.wait_ge(s["q_high_made"], n + 1)
                    nc.gpsimd.tensor_tensor(q_low[:, heads, :], q, q_high[:, heads, :].bitcast(F32), ALU.subtract).then_inc(s["q_cut"], 1)

                def first(b):
                    nc.gpsimd.tensor_copy(inputs[:, 0:SC], cT[:, ds(b, SC)])
                    nc.gpsimd.tensor_copy(inputs[:, SC:KEYS], k.xT[:, ds(b, S)]).then_inc(s["inputs_ready"], 1)
                    pool.wait_ge(s["q_taken"], b * H + H + 2)
                    cut(b, 0, 0)
                    cut(b, 0, 1)

                def steps(b, t, start, end):
                    for half in range(2):
                        if ahead(t, H):
                            pool.wait_ge(s["scored"], heads_before(b, t, 4 * half + 4))
                            cut(b, t + 1, half)

                nc.gpsimd.memset(one[:], 1.0).then_inc(s["q_cut"], 1)
                pool.wait_ge(s["q_cut"], 1)
                over_batches(pool, H, 0, first, steps, lambda b: None)

            @block.scalar
            def _(act):
                def exp(b, t, h):
                    act.wait_ge(s["maxed"], heads_before(b, t, h) + 1)
                    n = h % H
                    nc.scalar.activation(probs[:, h % 2, :].rearrange("p (i k) -> p i k", i=2), k.psum[:, 2 * (h % 2):2 * (h % 2) + 2, 0:HALF],
                                         ACT.Exp, bias=negmax[:, n:n + 1], accum_out=sums[:, n:n + 1]).then_inc(s["exped"], 1)

                def first(b):
                    act.wait_ge(s["q_cut"], b * TB * 2 + 1)
                    for h in range(H):
                        act.wait_ge(s["k_made"], b * H + h + 1)
                        for bank, start, home, n in PARTS:
                            ins = nc.scalar.activation(k_high[:, h, home:home + n], k.bank[2 * (h % 2) + bank][:, start:start + n],
                                                       ACT.Identity, bias=bk[:, h:h + 1])
                        ins.then_inc(s["k_high_made"], 1)
                        act.wait_ge(s["q_made"], b * H + h + 1)
                        nc.scalar.activation(q_all[:, h, :], k.bank[6 + h % 2], ACT.Identity, scale=scale, bias=bq_scaled[:, h:h + 1]).then_inc(s["q_taken"], 1)
                    exp(b, 0, 0)

                def steps(b, t, start, end):
                    for h in range(start, end):
                        if ahead(t, h + 1):
                            exp(b, t, h + 1)
                        act.wait_ge(s["turned"], heads_before(b, t, h) + 1)
                        nc.scalar.copy(probsT[:, h % 2, 0:4, :], k.bank[4].rearrange("p (c q) -> p c q", c=4)).then_inc(s["copied_a"], 1)

                free_at_first(act, s["exped"], s["q_taken"], by=2)
                free_at_first(act, s["copied_a"])
                over_batches(act, H, 1, first, steps, lambda b: None)

            @block.vector
            def _(dve):
                def maximum(b, t, h):
                    n = h % H
                    dve.wait_ge(s["scored"], heads_before(b, t, h) + 1)
                    nc.vector.tensor_reduce(negmax[:, n:n + 1], k.psum[:, 2 * (h % 2):2 * (h % 2) + 2, 0:HALF],
                                            mybir.AxisListType.XY, ALU.max, negate=True).then_inc(s["maxed"], 1)

                def add(b, t, h):
                    nc.vector.reciprocal(inv[:, h:h + 1], sums[:, h:h + 1]).then_inc(s["inverted"], 1)
                    dve.wait_ge(s["inverted"], heads_before(b, t, h) + 1)
                    dve.wait_ge(s["mixed"], heads_before(b, t, h) + 1)
                    x = k.x[:, ds(b * TB + t)]
                    nc.vector.scalar_tensor_tensor(x, k.bank[6 + h % 2][:, 0:D], inv[:, h:h + 1], x, ALU.mult, ALU.add).then_inc(s["added"], 1)

                def first(b):
                    for h in range(H):
                        dve.wait_ge(s["k_high_made"], b * H + h + 1)
                        for bank, start, home, n in PARTS:
                            ins = nc.vector.scalar_tensor_tensor(k_low[:, h, home:home + n], k.bank[2 * (h % 2) + bank][:, start:start + n],
                                                                 bk[:, h:h + 1], k_high[:, h, home:home + n].bitcast(F32), ALU.add, ALU.subtract)
                        ins.then_inc(s["k_low_made"], 1)
                    for c in range(CHUNKS):
                        n = rows_of(c)
                        dve.wait_ge(s["vo_made"], b * CHUNKS + c + 1)
                        for i in range(2):
                            ins = nc.vector.tensor_tensor(vo[0:n, c, ds(i, 4 * D)], k.bank[4 + 2 * (c % 2) + i][0:n, :],
                                                          b_vo2[0:n, ds(i, 4 * D)], ALU.add)
                        ins.then_inc(s["vo_taken"], 1)
                    maximum(b, 0, 0)

                def steps(b, t, start, end):
                    for h in range(start, end):
                        if ahead(t, h + 1):
                            maximum(b, t, h + 1)
                        dve.wait_ge(s["turned"], heads_before(b, t, h) + 1)
                        nc.vector.tensor_copy(probsT[:, h % 2, 4:6, :], k.bank[5][:, 0:2 * P].rearrange("p (c q) -> p c q", c=2)).then_inc(s["copied_v"], 1)
                        if h > 0:
                            add(b, t, h - 1)

                free_at_first(dve, s["k_low_made"], s["vo_taken"], s["added"], by=2)
                free_at_first(dve, s["copied_v"])
                over_batches(dve, H, 1, first, steps, lambda b: add(b, TB - 1, H - 1))


def stage_1f(k):
    nc = k.nc
    with Scope(k) as ctx:
        src = k.sb("f1_src", [P, NT * D], F32, ctx)
        normalize(k, k.x, rows=src, turned=False)
        relative_attention(k, src)
        relu_experts(k, src)
        with nc.Block() as block:
            @block.vector
            def _(dve):
                nc.vector.tensor_tensor(k.x[:], k.x[:], src[:], ALU.add)


def relative_attention(k, src):
    nc = k.nc
    scale = DH ** -0.5
    QUADS = H16 // 4
    TERMS = 3
    R = TERMS * 4 * DH
    LOW_OF_Q, LOW_OF_K = slice(2 * R // 3, R), slice(R // 3, 2 * R // 3)
    W1 = H16 * (DH + 1)
    SCORES, RING = 2, 8
    HB = TB * H16
    with Scope(k) as ctx:
        names = ("f1_ln1", "f1_wq", "f1_wk", "f1_wv", "f1_wo", "rot_cos", "rot_sin", "key_waves")
        ln, wq, wk, wv, wo, rot_cos, rot_sin, waves = homes = [load(k, ctx, n) for n in names]
        position_names = ("f1_wpT", "f1_wpT_swapped")
        position_w = [k.sb(n, [R, QUADS * D], F32, ctx) for n in position_names]
        own_rows = load(k, ctx, "own_rows", R)
        normalize(k, src, ln[:, 0:1], ln[:, 1:2],
                  loads=(list(zip(names + position_names + ("own_rows",), homes + position_w + [own_rows])), ctx))
        q_stack = k.sb("f1_q_stack", [R, QUADS, NTOK], F32R, ctx)
        k_stack = k.sb("f1_k_stack", [R, QUADS, NTOK], F32R, ctx)
        w_stack = [k.sb(f"f1_w_stack{i}", [R, QUADS, D], F32R, ctx) for i in range(2)]
        waves_high = k.sb("f1_waves_high", [P, S], F32R, ctx)
        waves_low = k.sb("f1_waves_low", [P, S], F32R, ctx)
        vals = k.sb("f1_vals", [P, NT, H16, DH + 1], F32, ctx)
        made, high_made, split, ones, v_made, v_taken, high_w = (
            k.sem(f"f1_prepare_{n}", ctx) for n in ("made", "high_made", "split", "ones", "v_made", "v_taken", "high_weights"))
        work = [(b, j, w, home, low, factor) for b in range(B) for j in range(QUADS)
                for w, home, low, factor in ((wq, q_stack, LOW_OF_Q, scale), (wk, k_stack, LOW_OF_K, 1.0))]
        with nc.Block() as block:
            @block.tensor
            def _(pe):
                for n, (b, j, w, *_) in enumerate(work):
                    if n >= 4:
                        pe.wait_ge(split, n - 3)
                    nc.tensor.matmul(k.bank[n % 4][0:R], w[:, ds(j, R)], k.xT[:, ds(b, S)], start=True, stop=True).then_inc(made, 1)
                    if n % 2 == 1:
                        T = n // 2
                        if T >= 4:
                            pe.wait_ge(v_taken, T - 3)
                        nc.tensor.matmul(k.bank[4 + T % 4][:, 0:D], k.xT[:, ds(T)], wv[:], start=True, stop=True).then_inc(v_made, 1)

            @block.scalar
            def _(act):
                for i in range(2):
                    ins = nc.scalar.copy(w_stack[i][:].rearrange("r j d -> r (j d)"), position_w[i][:])
                nc.scalar.copy(waves_high[:], waves[:]).then_inc(high_w, 1)
                for n, (b, j, w, home, low, factor) in enumerate(work):
                    act.wait_ge(made, n + 1)
                    nc.scalar.activation(home[:, j, ds(b, S)], k.bank[n % 4][0:R], ACT.Copy, scale=factor).then_inc(high_made, 1)

            @block.vector
            def _(dve):
                nc.vector.memset(vals[:], 1.0).then_inc(ones, 1)
                dve.wait_ge(high_w, 1)
                for i in range(2):
                    cut = w_stack[i][LOW_OF_K].rearrange("r j d -> r (j d)")
                    nc.vector.tensor_tensor(cut, position_w[i][LOW_OF_K, :], cut.bitcast(F32), ALU.subtract)
                nc.vector.tensor_tensor(waves_low[:], waves[:], waves_high[:].bitcast(F32), ALU.subtract)
                dve.wait_ge(ones, 1)
                for n, (b, j, w, home, low, factor) in enumerate(work):
                    dve.wait_ge(high_made, n + 1)
                    cut = home[low, j, ds(b, S)]
                    nc.vector.scalar_tensor_tensor(cut, k.bank[n % 4][low], factor, cut.bitcast(F32), ALU.mult, ALU.subtract).then_inc(split, 1)
                    if n % 2 == 1:
                        T = n // 2
                        dve.wait_ge(v_made, T + 1)
                        nc.vector.tensor_copy(vals[:, T, :, 0:DH], k.bank[4 + T % 4][:, 0:D].rearrange("p (h d) -> p h d", d=DH)).then_inc(v_taken, 1)

        q_head = k.sb("f1_q_head", [R, H16, P], F32R, ctx)
        turn_cos = k.sb("f1_turn_cos", [P, 4, P], F32, ctx)
        turn_sin = k.sb("f1_turn_sin", [P, 4, P], F32, ctx)
        turned = k.sb("f1_turned_u", [P, 4, P], F32, ctx)
        turned_high = k.sb("f1_turned_high", [P, 2, 4, P], F32R, ctx)
        turned_low = k.sb("f1_turned_low", [P, 2, 4, P], F32R, ctx)
        probs = k.sb("f1_probs", [P, 2, S], F32, ctx)
        probsT = k.sb("f1_probsT", [P, RING, S], F32, ctx)
        mixT = k.sb("f1_mixT", [P, P], F32, ctx)
        negmax = k.sb("f1_negmax", [P, H16], F32, ctx)
        inv = k.sb("f1_inv", [P, H16], F32, ctx)
        outs = k.sb("f1_outs", [P, NT, D], F32, ctx)
        s = {n: k.sem(f"f1_{n}", ctx) for n in ("masked", "u_made", "u_read", "summed", "turned_high_made", "turned_split", "scored",
                                                "maxed", "exped", "transposed", "copied", "mixed", "mix_copied", "turned_back",
                                                "inverted", "normed", "bank_cleared")}
        MIX, MISC = k.bank[6], k.bank[7]
        vals2 = vals[:].rearrange("p t h d -> p (t h d)")
        batch_vals = k.sb("f1_batch_vals", [P, TB, H16, DH + 1], F32, ctx)
        k_keys = k_stack[:].rearrange("r j n -> r (j n)")
        q_flat = q_stack[:].rearrange("r j n -> r (j n)")
        outs_flat = outs[:].rearrange("p t d -> p (t d)")
        SLOT, MIXED = 8, 3
        LEAD = 4

        def heads_before(b, t, h):
            return b * HB + t * H16 + h

        def quads_before(b, t, j):
            return (b * TB + t) * QUADS + j

        def ahead(t, h):
            return h < H16 or not isinstance(t, int) or t < TB - 1

        with nc.Block() as block:
            @block.tensor
            def _(pe):
                def positions(b, t, j):
                    pe.wait_ge(s["masked"], quads_before(b, t, j) + 1)
                    pe.wait_ge(s["u_read"], quads_before(b, t, j) + 1)
                    q = q_head[:, 4 * (j % QUADS):4 * (j % QUADS) + 4, :]
                    nc.tensor.matmul(k.bank[0], w_stack[0][:, j % QUADS, :], q, start=True, stop=True)
                    nc.tensor.matmul(k.bank[1], w_stack[1][:, j % QUADS, :], q, start=True, stop=True).then_inc(s["u_made"], 1)

                def score(b, t, h):
                    j, i = h // 4, h % 4
                    if i == 0:
                        pe.wait_ge(s["turned_split"], quads_before(b, t, j) + 2)
                    pe.wait_ge(s["exped"], heads_before(b, t, h) + 1)
                    bank = k.bank[2 + h % 2]
                    nc.tensor.matmul(bank, q_head[:, h % H16, :], k_keys[:, bass.ds(j % QUADS * NTOK + b * S, S)], start=True, stop=False)
                    nc.tensor.matmul(bank, turned_high[:, j % 2, i, :], waves_high[:], start=False, stop=False)
                    nc.tensor.matmul(bank, turned_high[:, j % 2, i, :], waves_low[:], start=False, stop=False)
                    nc.tensor.matmul(bank, turned_low[:, j % 2, i, :], waves_high[:], start=False, stop=True).then_inc(s["scored"], 1)

                def turn(b, t, h):
                    pe.wait_ge(s["exped"], heads_before(b, t, h) + 1 + SCORES)
                    pe.wait_ge(s["copied"], heads_before(b, t, h) + 1)
                    for c in range(TB):
                        ins = nc.tensor.transpose(k.bank[4 + h % 2][:, ds(c)], probs[:, h % 2, ds(c)], k.ident[:])
                    ins.then_inc(s["transposed"], 1)

                def mix(b, t, j):
                    pe.wait_ge(s["copied"], heads_before(b, t, 4 * j + 3) + 1 + 2)
                    pe.wait_ge(s["mix_copied"], quads_before(b, t, j) + 1)
                    for c in range(TB):
                        for i in range(4):
                            h = 4 * j + i
                            ins = nc.tensor.matmul(MIX[32 * i:32 * i + DH + 1, 0:P], batch_vals[:, c, h, :], probsT[:, h % RING, ds(c)],
                                                   start=c == 0, stop=c == TB - 1)
                    ins.then_inc(s["mixed"], 1)

                def turn_back(b, t, j):
                    pe.wait_ge(s["mix_copied"], quads_before(b, t, j) + 2)
                    if j == 0:
                        pe.wait_ge(s["normed"], b * TB + t + 1)
                    nc.tensor.transpose(MISC[:, ds(j)], mixT[:], k.ident[:]).then_inc(s["turned_back"], 1)

                def first(b):
                    positions(b, 0, 0)
                    positions(b, 0, 1)
                    score(b, 0, 0)
                    score(b, 0, 1)
                    positions(b, 0, 2)

                def steps(b, t, start, end):
                    for h in range(start, end):
                        if ahead(t, h + 2):
                            score(b, t, h + 2)
                        turn(b, t, h)
                        if h % 4 == 1:
                            if h > 4:
                                mix(b, t, h // 4 - 1)
                        if h % 4 == 3:
                            if h >= 7:
                                turn_back(b, t, h // 4 - 1)
                            if ahead(t, h + 9):
                                positions(b, t, h // 4 + 3)

                def last(b):
                    mix(b, TB - 1, QUADS - 1)
                    turn_back(b, TB - 1, QUADS - 1)

                pe.wait_ge(s["bank_cleared"], 1)
                over_batches(pe, H16, LEAD, first, steps, last)

            @block.gpsimd
            def _(pool):
                def stacks(b, t, j):
                    nc.gpsimd.tensor_tensor(q_head[:, 4 * (j % QUADS):4 * (j % QUADS) + 4, :],
                                            q_flat[:, None, bass.ds(j % QUADS * NTOK + b * S + (t + j // QUADS) * P, P)].broadcast_to([R, 4, P]),
                                            own_rows[:, :, None].broadcast_to([R, 4, P]), ALU.mult).then_inc(s["masked"], 1)

                def cut(b, t, j):
                    pool.wait_ge(s["u_read"], quads_before(b, t, j) + 2)
                    pool.wait_ge(s["turned_split"], quads_before(b, t, j) + 1)
                    nc.gpsimd.tensor_tensor(turned[:], turn_cos[:], turn_sin[:], ALU.add).then_inc(s["summed"], 1)
                    pool.wait_ge(s["turned_high_made"], quads_before(b, t, j) + 1)
                    nc.gpsimd.tensor_tensor(turned_low[:, j % 2], turned[:], turned_high[:, j % 2].bitcast(F32),
                                            ALU.subtract).then_inc(s["turned_split"], 1)

                def first(b):
                    stacks(b, 0, 0)
                    stacks(b, 0, 1)
                    cut(b, 0, 0)
                    stacks(b, 0, 2)
                    cut(b, 0, 1)

                def steps(b, t, start, end):
                    for j in range(start // 4, end // 4):
                        if ahead(t, 4 * (j + 3)):
                            stacks(b, t, j + 3)
                        if ahead(t, 4 * (j + 2)):
                            cut(b, t, j + 2)

                free_at_first(pool, s["turned_split"])
                over_batches(pool, H16, 0, first, steps, lambda b: None)

            @block.scalar
            def _(act):
                def exp(b, t, h):
                    act.wait_ge(s["maxed"], heads_before(b, t, h) + 1)
                    nc.scalar.activation(probs[:, h % 2], k.bank[2 + h % 2], ACT.Exp, bias=negmax[:, h % H16:h % H16 + 1]).then_inc(s["exped"], 1)

                def mix_copy(b, t, j):
                    act.wait_ge(s["mixed"], quads_before(b, t, j) + MIXED)
                    act.wait_ge(s["turned_back"], quads_before(b, t, j) + 1)
                    nc.scalar.copy(mixT[:], MIX[:, 0:P]).then_inc(s["mix_copied"], 1)

                def first(b):
                    nc.scalar.copy(batch_vals[:].rearrange("p t h d -> p (t h d)"), vals2[:, ds(b, TB * W1)])
                    exp(b, 0, 0)

                def steps(b, t, start, end):
                    for h in range(start, end):
                        if ahead(t, h + 1):
                            exp(b, t, h + 1)
                        if h % 4 == 2 and h >= 6:
                            mix_copy(b, t, h // 4 - 1)
                        act.wait_ge(s["transposed"], heads_before(b, t, h) + 1)
                        if h % 4 == 0:
                            act.wait_ge(s["mixed"], quads_before(b, t, h // 4) + 1)
                        nc.scalar.copy(probsT[:, h % RING], k.bank[4 + h % 2]).then_inc(s["copied"], 1)

                free_at_first(act, s["exped"], s["copied"], by=SCORES)
                free_at_first(act, s["mix_copied"])
                free_at_first(act, s["mixed"], by=MIXED - 1)
                over_batches(act, H16, LEAD, first, steps, lambda b: mix_copy(b, TB - 1, QUADS - 1))

            @block.vector
            def _(dve):
                def rotate(b, t, j):
                    dve.wait_ge(s["u_made"], quads_before(b, t, j) + 1)
                    dve.wait_ge(s["summed"], quads_before(b, t, j) + 1)
                    start = (t + j // QUADS) * P
                    for bank, table, home in ((0, rot_cos, turn_cos), (1, rot_sin, turn_sin)):
                        ins = nc.vector.tensor_tensor(home[:], k.bank[bank].rearrange("p (h q) -> p h q", h=4),
                                                      table[:, None, bass.ds(start, P)].broadcast_to([P, 4, P]), ALU.mult)
                    ins.then_inc(s["u_read"], 1)

                def high(b, t, j):
                    dve.wait_ge(s["summed"], quads_before(b, t, j) + 2)
                    dve.wait_ge(s["scored"], heads_before(b, t, 4 * j) - 4 + SLOT)
                    nc.vector.tensor_copy(turned_high[:, j % 2], turned[:]).then_inc(s["turned_high_made"], 1)

                def norm(b, t):
                    T = b * TB + t
                    dve.wait_ge(s["turned_back"], quads_before(b, t, QUADS - 1) + 2)
                    mixed = MISC.rearrange("p (h d) -> p h d", h=H16)
                    nc.vector.reciprocal(inv[:], mixed[:, :, DH]).then_inc(s["inverted"], 1)
                    dve.wait_ge(s["inverted"], T + 1)
                    nc.vector.tensor_tensor(outs_flat[:, ds(T)].rearrange("p (h d) -> p h d", h=H16), mixed[:, :, 0:DH],
                                            inv[:, :, None].broadcast_to([P, H16, DH]), ALU.mult).then_inc(s["normed"], 1)

                def first(b):
                    rotate(b, 0, 0)
                    high(b, 0, 0)
                    rotate(b, 0, 1)

                def steps(b, t, start, end):
                    for h in range(start, end):
                        dve.wait_ge(s["scored"], heads_before(b, t, h) + 1 + SLOT)
                        nc.vector.tensor_reduce(negmax[:, h % H16:h % H16 + 1], k.bank[2 + h % 2], AX_X, ALU.max, negate=True).then_inc(s["maxed"], 1)
                        if h % 4 == 0 and ahead(t, h + 4):
                            high(b, t, h // 4 + 1)
                        if h % 4 == 2 and ahead(t, h + 6):
                            rotate(b, t, h // 4 + 2)
                        if h == H16 + 5:
                            norm(b, t)

                nc.vector.memset(MIX, 0.0).then_inc(s["bank_cleared"], 1)
                free_at_first(dve, s["normed"], s["u_read"], s["summed"], s["turned_back"])
                free_at_first(dve, s["scored"], by=SLOT)
                over_batches(dve, H16, LEAD + 2, first, steps, lambda b: norm(b, TB - 1))

        add_projection(k, ctx, "f1", outs, wo, src)


def relu_experts(k, src):
    nc = k.nc
    AHEAD = 4
    with Scope(k) as ctx:
        ln, sel, iota = homes = [load(k, ctx, n) for n in ("f1_ln2", "m1_sel", "iota32")]
        normalize(k, src, ln[:, 0:1], ln[:, 1:2], loads=(list(zip(("f1_ln2", "m1_sel", "iota32"), homes)), ctx))
        shape = [P, NT, E1]
        chance = k.sb("m1_chance", shape, F32, ctx)
        left = k.sb("m1_left", shape, F32, ctx)
        hit = k.sb("m1_hit", shape, F32, ctx)
        gate = k.sb("m1_gate", shape, F32, ctx)
        far = k.sb("m1_far", [P, E1], F32, ctx)
        best = k.sb("m1_best", [P, NT], F32, ctx)
        first = k.sb("m1_first", [P, NT], F32, ctx)
        order, made, ready = (k.sem(f"m1_{n}", ctx) for n in ("order", "sel_made", "sel_ready"))
        with nc.Block() as block:
            @block.tensor
            def _(pe):
                for T in range(NT):
                    ins = nc.tensor.matmul(k.bank[0][:, ds(T, E1)], k.xT[:, ds(T)], sel[:], start=True, stop=True)
                ins.then_inc(made, 1)

            @block.scalar
            def _(act):
                act.wait_ge(made, 1)
                nc.scalar.activation(chance[:].rearrange("p t e -> p (t e)"), k.bank[0], ACT.Exp, scale=-1.0).then_inc(ready, 1)

            @block.vector
            def _(dve):
                step = Steps(dve, order)
                step.then(nc.vector.tensor_scalar(far[:], iota[:], 100.0, None, ALU.add))
                nc.vector.memset(gate[:], 0.0)
                dve.wait_ge(ready, 1)
                step.then(nc.vector.tensor_scalar(chance[:], chance[:], 1.0, None, ALU.add))
                step.then(nc.vector.reciprocal(chance[:], chance[:]))
                step.then(nc.vector.tensor_copy(left[:], chance[:]))
                for _ in range(K1):
                    first_hit(nc, step, left, hit, best, first, iota[:], far, shape)
                    nc.vector.scalar_tensor_tensor(left[:], hit[:], -HUGE, left[:], ALU.mult, ALU.add)
                    step.then(nc.vector.tensor_tensor(hit[:], hit[:], chance[:], ALU.mult))
                    step.then(nc.vector.tensor_tensor(gate[:], gate[:], hit[:], ALU.add))

        w = k.sb("m1_weights", [P, 2, P + D], F32, ctx)
        hT = k.sb("m1_hT", [P, B, S], F32, ctx)
        loaded = [k.sem(f"m1_loaded{u}", ctx) for u in range(2)]
        h_made, relued, y_made, y_read = (k.sem(f"m1_{n}", ctx) for n in ("h_made", "relued", "y_made", "y_read"))
        gate2 = gate[:].rearrange("p t e -> p (t e)")
        source = k.dram["m1_w"]
        with nc.Block() as block:
            @block.sync
            def _(sp):
                for u in range(2):
                    sp.dma_start(w[:, u, :], source[u]).then_inc(loaded[u], 16)
                with sp.Fori(0, E1 // 2 - 1) as turn:
                    for u in range(2):
                        e = turn * 2 + u
                        sp.wait_ge(y_made, e * B + B)
                        sp.dma_start(w[:, u, :], source[bass.ds(e + 2, 1)].rearrange("e p n -> (e p) n")).then_inc(loaded[u], 16)

            @block.tensor
            def _(pe):
                with pe.Fori(0, E1 // 2) as turn:
                    for u in range(2):
                        e = turn * 2 + u
                        pe.wait_ge(loaded[u], turn * 16 + 16)

                        def hidden(c):
                            pe.wait_ge(relued, e * B + c + 1)
                            nc.tensor.matmul(k.bank[c], w[:, u, 0:P], k.xT[:, ds(c, S)], start=True, stop=True).then_inc(h_made, 1)

                        def values(c):
                            pe.wait_ge(relued, e * B + c + 1 + AHEAD)
                            pe.wait_ge(y_read, e * B + c + 1)
                            for j in range(TB):
                                ins = nc.tensor.matmul(k.bank[4 + c][:, ds(j)], hT[:, c, ds(j)], w[:, u, P:P + D], start=True, stop=True)
                            ins.then_inc(y_made, 1)

                        hidden(0)
                        hidden(1)
                        for c in range(2, B):
                            hidden(c)
                            values(c - 2)
                        values(B - 2)
                        values(B - 1)

            @block.scalar
            def _(act):
                nc.scalar.copy(hT[:, 0, 0:1], k.ident[:, 0:1]).then_inc(relued, AHEAD)
                with act.Fori(0, E1) as e:
                    for c in range(B):
                        act.wait_ge(h_made, e * B + c + 1)
                        nc.scalar.activation(hT[:, c, :], k.bank[c], ACT.Relu).then_inc(relued, 1)

            @block.vector
            def _(dve):
                nc.vector.memset(best[:], 0.0).then_inc(y_read, AHEAD)
                with dve.Fori(0, E1) as e:
                    for c in range(B):
                        dve.wait_ge(y_made, e * B + c + 1)
                        for j in range(TB):
                            T = c * TB + j
                            ins = nc.vector.scalar_tensor_tensor(src[:, ds(T)], k.bank[4 + c][:, ds(j)], gate2[:, bass.ds(e + T * E1, 1)],
                                                                 src[:, ds(T)], ALU.mult, ALU.add)
                        ins.then_inc(y_read, 1)


def stage_0f(k):
    nc = k.nc
    with Scope(k) as ctx:
        xn = k.sb("m0_xn", [P, NT * D], F32, ctx)
        normalize(k, k.x, rows=xn)
        slots = nc.dram_tensor("m0_slots", (SLOTS + K0 * NTOK, D), F32).ap()
        answers = nc.dram_tensor("m0_answers", (SLOTS, D), F32).ap()
        put = k.sb("m0_put", [P, K0, NT], I32, ctx)
        get = k.sb("m0_get", [P, K0, NT], I32, ctx)
        weight = k.sb("m0_weight", [P, K0, NT], F32, ctx)
        route(k, slots, put, get, weight)
        shared_experts(k, slots, xn, put)
        routed_experts(k, slots, answers)
        answer = k.sb("m0_answer", [P, K0, NT, D], F32, ctx)
        gathered = k.sem("m0_gathered")
        order = k.sem("m0_add_order", ctx)
        with nc.Block() as block:
            @block.gpsimd
            def _(pool):
                for T in range(NT):
                    for c in range(K0):
                        pool.indirect_dma_start(out=answer[:, c, T, :], out_offset=None, in_=answers,
                                                in_offset=bass.IndirectOffsetOnAxis(ap=get[:, c, T:T + 1], axis=0)).then_inc(gathered, 16)
                pool.wait_ge(gathered, 16 * K0 * NT)

            @block.vector
            def _(dve):
                step = Steps(dve, order)
                dve.wait_ge(gathered, 16 * K0 * NT)
                for c in range(K0):
                    for T in range(NT):
                        ins = nc.vector.scalar_tensor_tensor(k.x[:, ds(T)], answer[:, c, T, :], weight[:, c, T:T + 1], k.x[:, ds(T)],
                                                             ALU.mult, ALU.add)
                    step.then(ins)


def route(k, slots, put, get, weight):
    nc = k.nc
    TE = [P, NT, E0]
    flat = lambda a: a[:].rearrange("p t e -> p (t e)")
    over_experts = lambda a: a[:, :, None].broadcast_to(TE)
    over_tiles = lambda a: a[:, None, :].broadcast_to(TE)
    with Scope(k) as ctx:
        names = ("m0_gate_w", "m0_gate_b", "iota16", "slot_base", "spare_slot", "before")
        gate_w, gate_b, iota, base, spare, before = homes = [load(k, ctx, n) for n in names]
        bits = k.sb("m0_bits", [P, MAG_BITS * E0], I32, ctx)
        zeros = k.sb("m0_zeros", [P, SLOTS], F32, ctx)
        fetched, emptied, zeroed = (k.sem(f"m0_{n}", ctx) for n in ("fetched", "emptied", "zeroed"))
        t = {n: k.sb(f"m0_{n}", TE, F32, ctx) for n in ("logit", "work", "score", "hit1", "hit2", "member", "signed", "keep", "number", "tmp")}
        e = {n: k.sb(f"m0_{n}", [P, E0], F32, ctx) for n in ("far", "count", "positive", "sign", "want", "cut", "above")}
        best, first, sums = (k.sb(f"m0_{n}", [P, NT], F32, ctx) for n in ("best", "first", "sums"))
        threshold = k.sb("m0_threshold", [P, E0], I32, ctx)
        trial = k.sb("m0_trial", [P, E0], I32, ctx)
        enough = k.sb("m0_enough", [P, E0], F32, ctx)
        taken = k.sb("m0_taken_bit", [P, E0], I32, ctx)
        mark = k.sb("m0_mark", TE, BF16, ctx)
        marks = k.sb("m0_marks", [P, NT, 2, E0], BF16, ctx)
        offset = k.sb("m0_offset", [P, NT + 1, 2 * E0], F32, ctx)
        rank = k.sb("m0_rank", [P, NT, 2, E0], F32, ctx)
        ones = k.sb("m0_ones", [P, P], BF16, ctx)
        before16 = k.sb("m0_before16", [P, P], BF16, ctx)
        order, logits_made, shifted, exped, marked, counted, mark2, rank_made = (
            k.sem(f"m0_{n}", ctx) for n in ("order", "logits_made", "shifted", "exped", "marked", "counted", "marked2", "rank_made"))
        with nc.Block() as block:
            @block.sync
            def _(sp):
                for n, home in zip(names, homes):
                    sp.dma_start(home[:], k.dram[n]).then_inc(fetched, 16)
                sp.dma_start(bits[:], k.dram["bits"]).then_inc(fetched, 16)
                sp.wait_ge(emptied, 1)
                sp.dma_start(slots[0:SLOTS, :].rearrange("(p s) d -> p (s d)", p=P), zeros[:]).then_inc(zeroed, 16)
                sp.wait_ge(zeroed, 16)

            @block.gpsimd
            def _(pool):
                nc.gpsimd.memset(zeros[:], 0.0).then_inc(emptied, 1)

            @block.scalar
            def _(act):
                act.wait_ge(shifted, 1)
                nc.scalar.activation(flat(t["score"]), flat(t["work"]), ACT.Exp).then_inc(exped, 1)

            @block.tensor
            def _(pe):
                pe.wait_ge(fetched, 16 * (len(names) + 1))
                for T in range(NT):
                    ins = nc.tensor.matmul(k.bank[0][:, ds(T, E0)], k.xT[:, ds(T)], gate_w[:], start=True, stop=True)
                ins.then_inc(logits_made, 1)
                pe.wait_ge(marked, 1)
                nc.tensor.matmul(k.bank[1][:, 0:NT * E0], ones[:], flat(mark), start=True, stop=True).then_inc(counted, 1)
                with pe.Fori(0, MAG_BITS) as i:
                    pe.wait_ge(marked, i + 2)
                    nc.tensor.matmul(k.bank[1][:, 0:NT * E0], ones[:], flat(mark), start=True, stop=True).then_inc(counted, 1)
                pe.wait_ge(mark2, 1)
                m = marks[:].rearrange("p t c e -> p (t c e)")
                nc.tensor.matmul(k.bank[2], ones[:], m, start=True, stop=True).then_inc(rank_made, 1)
                nc.tensor.matmul(k.bank[3], before16[:], m, start=True, stop=True).then_inc(rank_made, 1)

            @block.vector
            def _(dve):
                step = Steps(dve, order)
                then, v = step.then, nc.vector
                then(v.memset(ones[:], 1.0))
                dve.wait_ge(fetched, 16 * (len(names) + 1))
                then(v.tensor_copy(before16[:], before[:]))
                then(v.tensor_scalar(e["far"][:], iota[:], 100.0, None, ALU.add))
                dve.wait_ge(logits_made, 1)
                then(v.tensor_copy(flat(t["logit"]), k.bank[0][:, 0:NT * E0]))
                then(v.tensor_reduce(best[:], t["logit"][:], AX_X, ALU.max))
                v.tensor_tensor(t["work"][:], t["logit"][:], over_experts(best), ALU.subtract).then_inc(shifted, 1)
                dve.wait_ge(exped, 1)
                then(v.tensor_reduce(sums[:], t["score"][:], AX_X, ALU.add))
                then(v.reciprocal(sums[:], sums[:]))
                then(v.tensor_tensor(t["score"][:], t["score"][:], over_experts(sums), ALU.mult))
                then(v.tensor_tensor(t["score"][:], t["score"][:], over_tiles(gate_b), ALU.add))
                first_hit(nc, step, t["score"], t["hit1"], best, first, iota[:], e["far"], TE)
                then(v.scalar_tensor_tensor(t["score"][:], t["hit1"][:], -HUGE, t["score"][:], ALU.mult, ALU.add))
                first_hit(nc, step, t["score"], t["hit2"], best, first, iota[:], e["far"], TE)
                then(v.tensor_tensor(t["member"][:], t["hit1"][:], t["hit2"][:], ALU.add))
                then(v.tensor_scalar(t["tmp"][:], t["member"][:], HUGE, HUGE, ALU.mult, ALU.subtract))
                then(v.tensor_tensor(t["work"][:], t["logit"][:], t["member"][:], ALU.mult))
                then(v.tensor_tensor(t["work"][:], t["work"][:], t["tmp"][:], ALU.add))

                def count(n):
                    dve.wait_ge(counted, n)
                    then(v.tensor_reduce(e["count"][:], k.bank[1][:, 0:NT * E0].rearrange("p (t e) -> p e t", e=E0), AX_X, ALU.add))

                v.tensor_scalar(mark[:], t["work"][:], 0.0, None, ALU.is_ge).then_inc(marked, 1)
                count(1)
                then(v.tensor_scalar(e["positive"][:], e["count"][:], float(CAP), None, ALU.is_ge))
                v.tensor_scalar(e["sign"][:], e["positive"][:], 2.0, -1.0, ALU.mult, ALU.add)
                v.memset(threshold[:], 0)
                then(v.tensor_scalar(e["want"][:], e["positive"][:], float(2 * CAP - NTOK - 1), float(NTOK - CAP + 1), ALU.mult, ALU.add))
                then(v.tensor_tensor(t["signed"][:], t["work"][:], over_tiles(e["sign"]), ALU.mult))
                with dve.Fori(0, MAG_BITS) as i:
                    step.turn(i, 5)
                    then(v.tensor_tensor(trial[:], threshold[:], bits[:, ds(i, E0)], ALU.bitwise_or))
                    v.tensor_tensor(mark[:], t["signed"][:], over_tiles(trial[:].bitcast(F32)), ALU.is_ge).then_inc(marked, 1)
                    count(i + 2)
                    then(v.tensor_tensor(enough[:], e["count"][:], e["want"][:], ALU.is_ge))
                    then(v.tensor_tensor(taken[:], enough[:], bits[:, ds(i, E0)], ALU.mult))
                    then(v.tensor_tensor(threshold[:], threshold[:], taken[:], ALU.bitwise_or))
                step.turns_end(MAG_BITS)
                then(v.tensor_tensor(e["cut"][:], threshold[:].bitcast(F32), e["sign"][:], ALU.mult))
                then(v.tensor_tensor(t["tmp"][:], t["work"][:], over_tiles(e["cut"]), ALU.is_equal))
                then(v.tensor_tensor(t["tmp"][:], t["tmp"][:], t["member"][:], ALU.mult))
                v.tensor_copy(marks[:, :, 1, :], t["tmp"][:])
                then(v.tensor_tensor(t["keep"][:], t["work"][:], over_tiles(e["cut"]), ALU.is_gt))
                v.tensor_copy(marks[:, :, 0, :], t["keep"][:]).then_inc(mark2, 1)
                v.memset(offset[:, 0, :], 0.0)
                dve.wait_ge(rank_made, 2)
                totals = k.bank[2].rearrange("p (t c) -> p t c", t=NT)
                for T in range(NT):
                    if T == 0:
                        then(v.tensor_copy(offset[:, 1, :], totals[:, 0, :]))
                    else:
                        then(v.tensor_tensor(offset[:, T + 1, :], totals[:, T, :], offset[:, T, :], ALU.add))
                then(v.tensor_tensor(rank[:].rearrange("p t c e -> p t (c e)"), k.bank[3].rearrange("p (t c) -> p t c", t=NT),
                                     offset[:, 0:NT, :], ALU.add))
                above = offset[:, NT, 0:E0]
                then(v.tensor_tensor(rank[:, :, 1, :], rank[:, :, 1, :], above[:, None, :].broadcast_to(TE), ALU.add))
                then(v.scalar_tensor_tensor(t["tmp"][:], rank[:, :, 1, :], float(CAP), t["tmp"][:], ALU.is_lt, ALU.mult))
                then(v.tensor_tensor(t["number"][:], t["tmp"][:], rank[:, :, 1, :], ALU.mult))
                then(v.tensor_tensor(t["signed"][:], t["keep"][:], rank[:, :, 0, :], ALU.mult))
                then(v.tensor_tensor(t["number"][:], t["number"][:], t["signed"][:], ALU.add))
                then(v.tensor_tensor(t["number"][:], t["number"][:], over_tiles(base), ALU.add))
                then(v.tensor_tensor(t["keep"][:], t["keep"][:], t["tmp"][:], ALU.add))
                for c, hit in enumerate((t["hit1"], t["hit2"])):
                    then(v.tensor_tensor(hit[:], hit[:], t["keep"][:], ALU.mult))
                    then(v.tensor_tensor(t["tmp"][:], hit[:], t["number"][:], ALU.mult))
                    then(v.tensor_reduce(best[:], t["tmp"][:], AX_X, ALU.add))
                    then(v.tensor_copy(get[:, c, :], best[:]))
                    then(v.tensor_tensor(t["tmp"][:], hit[:], t["logit"][:], ALU.mult))
                    then(v.tensor_reduce(weight[:, c, :], t["tmp"][:], AX_X, ALU.add))
                    then(v.tensor_reduce(first[:], hit[:], AX_X, ALU.add))
                    then(v.tensor_scalar(first[:], first[:], -1.0, 1.0, ALU.mult, ALU.add))
                    then(v.scalar_tensor_tensor(first[:], spare[:], float(c * NTOK), first[:], ALU.add, ALU.mult))
                    then(v.tensor_tensor(best[:], best[:], first[:], ALU.add))
                    then(v.tensor_copy(put[:, c, :], best[:]))


def shared_experts(k, slots, xn, put):
    nc = k.nc
    HB = S0 * HID0 // P
    with Scope(k) as ctx:
        w1, w3, w2 = homes = [load(k, ctx, n) for n in ("s0_w1", "s0_w3", "s0_w2")]
        fetch(k, list(zip(("s0_w1", "s0_w3", "s0_w2"), homes)), ctx)
        silu = k.sb("s0_silu", [P, 2, S], F32, ctx)
        hidden = k.sb("s0_hidden", [P, HB, S], F32, ctx)
        scattered = k.sem("m0_scattered")
        made, silued, gated, summed, added = (k.sem(f"s0_{n}", ctx) for n in ("made", "silued", "gated", "summed", "added"))
        with nc.Block() as block:
            @block.gpsimd
            def _(pool):
                for T in range(NT):
                    for c in range(K0):
                        pool.indirect_dma_start(out=slots, out_offset=bass.IndirectOffsetOnAxis(ap=put[:, c, T:T + 1], axis=0),
                                                in_=xn[:, ds(T)], in_offset=None).then_inc(scattered, 16)
                pool.wait_ge(scattered, 16 * K0 * NT)

            @block.tensor
            def _(pe):
                with pe.Fori(0, B) as b:
                    for n in range(HB):
                        pe.wait_ge(gated, b * HB + n + 1)
                        nc.tensor.matmul(k.bank[n % 2], w1[:, ds(n)], k.xT[:, ds(b, S)], start=True, stop=True)
                        nc.tensor.matmul(k.bank[2 + n % 2], w3[:, ds(n)], k.xT[:, ds(b, S)], start=True, stop=True).then_inc(made, 1)
                    pe.wait_ge(gated, b * HB + HB + 2)
                    pe.wait_ge(added, b + 1)
                    for j in range(TB):
                        for n in range(HB):
                            ins = nc.tensor.matmul(k.bank[4][:, ds(j)], hidden[:, n, ds(j)], w2[:, ds(n)], start=n == 0, stop=n == HB - 1)
                    ins.then_inc(summed, 1)

            @block.scalar
            def _(act):
                nc.scalar.copy(silu[:, 0, 0:1], k.ident[:, 0:1]).then_inc(gated, 2)
                with act.Fori(0, B) as b:
                    for n in range(HB):
                        act.wait_ge(made, b * HB + n + 1)
                        nc.scalar.activation(silu[:, n % 2, :], k.bank[n % 2], ACT.Silu).then_inc(silued, 1)

            @block.vector
            def _(dve):
                free_at_first(dve, added)
                with dve.Fori(0, B) as b:
                    for n in range(HB):
                        dve.wait_ge(silued, b * HB + n + 1)
                        nc.vector.tensor_tensor(hidden[:, n, :], k.bank[2 + n % 2], silu[:, n % 2, :], ALU.mult).then_inc(gated, 1)
                    dve.wait_ge(summed, b + 1)
                    nc.vector.scalar_tensor_tensor(k.x[:, ds(b, S)], k.bank[4], 1.0 / S0, k.x[:, ds(b, S)], ALU.mult, ALU.add).then_inc(added, 1)


def routed_experts(k, slots, answers):
    nc = k.nc
    HB = HID0 // P
    cuts = [(at, min(P, CAP - at)) for at in range(0, CAP, P)]
    with Scope(k) as ctx:
        w13 = k.sb("m0_w13", [P, 2, 2 * HID0], F32, ctx)
        w2 = k.sb("m0_w2", [P, 2, HB * D], F32, ctx)
        rows = k.sb("m0_rows", [P, 2, len(cuts), D], F32, ctx)
        rowsT = k.sb("m0_rowsT", [P, CAP], F32, ctx)
        silu = k.sb("m0_silu", [P, HB, CAP], F32, ctx)
        hidden = k.sb("m0_hidden", [P, HB, CAP], F32, ctx)
        result = k.sb("m0_result", [P, 2, len(cuts), D], F32, ctx)
        loaded = [k.sem(f"m0_loaded{u}", ctx) for u in range(2)]
        stored = [k.sem(f"m0_stored{u}", ctx) for u in range(2)]
        turned, copied, made, silued, gated, summed, taken = (k.sem(f"m0_{n}", ctx) for n in ("turned", "copied", "made", "silued", "gated", "summed", "taken"))
        PARTS = 2 + len(cuts)
        with nc.Block() as block:
            def load_expert(eng, u, e):
                one = lambda a: a[bass.ds(e, 1)].rearrange("e p n -> (e p) n") if not isinstance(e, int) else a[e]
                eng.dma_start(w13[:, u, :], one(k.dram["m0_w13"])).then_inc(loaded[u], 16)
                eng.dma_start(w2[:, u, :], one(k.dram["m0_w2"])).then_inc(loaded[u], 16)
                for i, (at, n) in enumerate(cuts):
                    eng.dma_start(rows[0:n, u, i, :], slots[bass.ds(e * CAP + at, n), :]).then_inc(loaded[u], 16)

            @block.sync
            def _(sp):
                load_expert(sp, 0, 0)
                load_expert(sp, 1, 1)
                with sp.Fori(0, E0 // 2 - 1) as turn:
                    for u in range(2):
                        sp.wait_ge(summed, turn * 2 + u + 1)
                        load_expert(sp, u, turn * 2 + u + 2)

            @block.scalar
            def _(act):
                free_at_first(act, *stored, by=16)
                with act.Fori(0, E0 // 2) as turn:
                    for u in range(2):
                        e = turn * 2 + u
                        act.wait_ge(turned, e + 1)
                        nc.scalar.copy(rowsT[:], k.bank[0][:, 0:CAP]).then_inc(copied, 1)
                        for n in range(HB):
                            act.wait_ge(made, e * HB + n + 1)
                            nc.scalar.activation(silu[:, n, :], k.bank[1 + n][:, 0:CAP], ACT.Silu).then_inc(silued, 1)
                        act.wait_ge(taken, e + 2)
                        for i, (at, n) in enumerate(cuts):
                            act.dma_start(answers[bass.ds(e * CAP + at, n), :], result[0:n, u, i, :]).then_inc(stored[u], 16)
                for u in range(2):
                    act.wait_ge(stored[u], 16 * len(cuts) * E0 // 2 + 16)

            @block.vector
            def _(dve):
                free_at_first(dve, taken)
                with dve.Fori(0, E0 // 2) as turn:
                    for u in range(2):
                        e = turn * 2 + u
                        for n in range(HB):
                            dve.wait_ge(silued, e * HB + n + 1)
                            nc.vector.tensor_tensor(hidden[:, n, :], k.bank[3 + n][:, 0:CAP], silu[:, n, :], ALU.mult).then_inc(gated, 1)
                        dve.wait_ge(summed, e + 1)
                        dve.wait_ge(stored[u], turn * (16 * len(cuts)) + 16)
                        for i, (at, n) in enumerate(cuts):
                            ins = nc.vector.tensor_copy(result[0:n, u, i, :], k.bank[5][0:n, ds(i)])
                        ins.then_inc(taken, 1)

            @block.tensor
            def _(pe):
                with pe.Fori(0, E0 // 2) as turn:
                    for u in range(2):
                        e = turn * 2 + u
                        pe.wait_ge(loaded[u], turn * (16 * PARTS) + 16 * PARTS)
                        for i, (at, n) in enumerate(cuts):
                            ins = nc.tensor.transpose(k.bank[0][:, at:at + n], rows[0:n, u, i, :], k.ident[0:n, 0:n])
                        ins.then_inc(turned, 1)
                        pe.wait_ge(copied, e + 1)
                        for n in range(HB):
                            nc.tensor.matmul(k.bank[1 + n][:, 0:CAP], w13[:, u, ds(n)], rowsT[:], start=True, stop=True)
                            nc.tensor.matmul(k.bank[3 + n][:, 0:CAP], w13[:, u, ds(HB + n)], rowsT[:], start=True, stop=True).then_inc(made, 1)
                        pe.wait_ge(gated, e * HB + HB)
                        pe.wait_ge(taken, e + 1)
                        for i, (at, m) in enumerate(cuts):
                            for n in range(HB):
                                ins = nc.tensor.matmul(k.bank[5][0:m, ds(i)], hidden[:, n, at:at + m], w2[:, u, ds(n)], start=n == 0, stop=n == HB - 1)
                        ins.then_inc(summed, 1)


def stage_3f(k):
    nc = k.nc
    NB = HID3 // P
    with Scope(k) as ctx:
        fc, proj, uT, v, bT, gate = homes = [load(k, ctx, n, k.dram[n].shape[0])
                                             for n in ("f3_fc", "f3_proj", "f3_uT", "f3_v", "f3_bT", "f3_gate")]
        normalize(k, k.x, loads=(list(zip(("f3_fc", "f3_proj", "f3_uT", "f3_v", "f3_bT", "f3_gate"), homes)), ctx))
        rank = v.shape[0]
        scale = k.sb("f3_scale", [P, 2, NB], F32, ctx)
        half = k.sb("f3_half", [P, 2, 2, NB], F32, ctx)
        below = k.sb("f3_below", [P, 2, HID3], F32, ctx)
        fv = k.sb("f3_fv", [rank, D], F32, ctx)
        fcT = k.sb("f3_fcT", [P, HID3], F32, ctx)
        projT = k.sb("f3_projT", [P, HID3], F32, ctx)
        order, ready, made, taken = (k.sem(f"f3_{n}", ctx) for n in ("order", "ready", "made", "taken"))
        with nc.Block() as block:
            @block.vector
            def _(dve):
                step = Steps(dve, order)
                step.then(nc.vector.tensor_reduce(scale[:, 0, :], fc[:].rearrange("p (b d) -> p b d", d=D), AX_X, ALU.add,
                                                  apply_absolute_value=True))
                nc.vector.tensor_reduce(scale[:, 1, 0:1], proj[:], AX_X, ALU.add, apply_absolute_value=True)
                step.then(nc.vector.memset(scale[:, 1, 1:NB], 1.0))
                nc.vector.tensor_scalar(scale[:, 0, :], scale[:, 0, :], 1.0 / D, 1e-5, ALU.mult, ALU.max)
                step.then(nc.vector.tensor_scalar(scale[:, 1, :], scale[:, 1, :], 1.0 / HID3, 1e-5, ALU.mult, ALU.max))
                nc.vector.tensor_scalar(half[:, 0], scale[:], 0.5, None, ALU.mult)
                step.then(nc.vector.tensor_scalar(half[:, 1], scale[:], -0.5, None, ALU.mult))
                blocks = [(0, fc, n, slice(n * P, (n + 1) * P), slice(n * P, (n + 1) * P)) for n in range(NB)]
                blocks += [(1, proj, 0, slice(0, HID3), slice(0, HID3))]
                for m, w, n, cols, _ in blocks:
                    ins = nc.vector.tensor_scalar(below[:, m, cols], w[:, cols], half[:, 1, m, n:n + 1], None, ALU.is_lt)
                step.then(ins)
                for m, w, n, cols, _ in blocks:
                    ins = nc.vector.scalar_tensor_tensor(below[:, m, cols], w[:, cols], half[:, 0, m, n:n + 1], below[:, m, cols],
                                                         ALU.is_gt, ALU.subtract)
                step.then(ins)
                for m, w in ((0, fc), (1, proj)):
                    ins = nc.vector.tensor_tensor(below[:, m, :], below[:, m, :], w[:], ALU.subtract)
                step.then(ins)
                for m, w in ((0, fc), (1, proj)):
                    ins = nc.vector.tensor_tensor(below[:, m, :], below[:, m, :], w[:], ALU.add)
                step.then(ins)
                for m, w, n, cols, _ in blocks:
                    ins = nc.vector.tensor_scalar(w[:, cols], below[:, m, cols], scale[:, m, n:n + 1], None, ALU.mult)
                ins.then_inc(ready, 1)
                dve.wait_ge(made, 1)
                nc.vector.tensor_copy(fv[:], k.bank[1][0:rank, 0:D]).then_inc(taken, 1)
                dve.wait_ge(made, 3)
                step.then(nc.vector.tensor_copy(fcT[:], k.bank[2]))
                nc.vector.tensor_copy(projT[:], k.bank[3])
                dve.wait_ge(made, 4)
                nc.vector.scalar_tensor_tensor(fcT[:], k.bank[4], gate[:, 0:1], fcT[:], ALU.mult, ALU.add).then_inc(taken, 1)

            @block.tensor
            def _(pe):
                nc.tensor.matmul(k.bank[1][0:rank, 0:D], bT[:], v[:], start=True, stop=True).then_inc(made, 1)
                pe.wait_ge(ready, 1)
                for w, bank in ((fc, 2), (proj, 3)):
                    for n in range(NB):
                        ins = nc.tensor.transpose(k.bank[bank][:, ds(n)], w[:, ds(n)], k.ident[:])
                    ins.then_inc(made, 1)
                pe.wait_ge(taken, 1)
                nc.tensor.matmul(k.bank[4], fv[:], uT[:], start=True, stop=True).then_inc(made, 1)
        r = k.sb("f3_r", [P, NB, S], F32, ctx)
        sq = k.sb("f3_sq", [P, NB, S], F32, ctx)
        hidden, relued, squared, out_made, added = (k.sem(f"f3_{n}", ctx) for n in ("hidden", "relued", "squared", "out_made", "added"))
        with nc.Block() as block:
            @block.tensor
            def _(pe):
                with pe.Fori(0, B) as b:
                    for n in range(NB):
                        pe.wait_ge(relued, b * NB + 1)
                        nc.tensor.matmul(k.bank[n], fcT[:, ds(n)], k.xT[:, ds(b, S)], start=True, stop=True).then_inc(hidden, 1)
                    pe.wait_ge(squared, b * NB + NB + 1)
                    pe.wait_ge(added, b + 1)
                    for j in range(TB):
                        for n in range(NB):
                            ins = nc.tensor.matmul(k.bank[4][:, ds(j)], sq[:, n, ds(j)], projT[:, ds(n)], start=n == 0, stop=n == NB - 1)
                    ins.then_inc(out_made, 1)

            @block.scalar
            def _(act):
                free_at_first(act, relued)
                with act.Fori(0, B) as b:
                    for n in range(NB):
                        act.wait_ge(hidden, b * NB + n + 1)
                        act.wait_ge(squared, b * NB + 1)
                        nc.scalar.activation(r[:, n, :], k.bank[n], ACT.Relu).then_inc(relued, 1)

            @block.vector
            def _(dve):
                free_at_first(dve, squared, added)
                with dve.Fori(0, B) as b:
                    for n in range(NB):
                        dve.wait_ge(relued, b * NB + n + 2)
                        nc.vector.tensor_tensor(sq[:, n, :], r[:, n, :], r[:, n, :], ALU.mult).then_inc(squared, 1)
                    dve.wait_ge(out_made, b + 1)
                    nc.vector.tensor_tensor(k.x[:, ds(b, S)], k.bank[4], k.x[:, ds(b, S)], ALU.add).then_inc(added, 1)


def stage_lora(k):
    nc = k.nc
    with Scope(k) as ctx:
        names = ("lora_wT", "lora_b", "lora_downT", "lora_down_aux", "lora_upT", "lora_up_auxT")
        w, b, downT, down_aux, upT, up_auxT = (load(k, ctx, n, k.dram[n].shape[0]) for n in names)
        normalize(k, k.x, loads=(list(zip(names, (w, b, downT, down_aux, upT, up_auxT))), ctx))
        rank, mid = upT.shape[0], upT.shape[1]
        a = k.sb("lora_a", [rank, D], F32, ctx)
        c = k.sb("lora_c", [mid, D], F32, ctx)
        w_all = k.sb("lora_w_all", [P, D], F32, ctx)
        made = k.sem("lora_made", ctx)
        taken = k.sem("lora_taken", ctx)
        with nc.Block() as block:
            @block.tensor
            def _(pe):
                nc.tensor.matmul(k.bank[1][0:rank, 0:D], downT[:], down_aux[:], start=True, stop=True).then_inc(made, 1)
                pe.wait_ge(taken, 1)
                nc.tensor.matmul(k.bank[2][0:mid, 0:D], upT[:], a[:], start=True, stop=True).then_inc(made, 1)
                pe.wait_ge(taken, 2)
                nc.tensor.matmul(k.bank[3][:, 0:D], c[:], up_auxT[:], start=True, stop=True).then_inc(made, 1)

            @block.vector
            def _(dve):
                dve.wait_ge(made, 1)
                nc.vector.tensor_copy(a[:], k.bank[1][0:rank, 0:D]).then_inc(taken, 1)
                dve.wait_ge(made, 2)
                nc.vector.tensor_copy(c[:], k.bank[2][0:mid, 0:D]).then_inc(taken, 1)
                dve.wait_ge(made, 3)
                nc.vector.tensor_tensor(w_all[:], k.bank[3][:, 0:D], w[:], ALU.add).then_inc(taken, 1)
        multiplied = k.sem("lora_multiplied", ctx)
        added = k.sem("lora_added", ctx)
        with nc.Block() as block:
            @block.tensor
            def _(pe):
                for T in range(NT):
                    if T % TB == 0 and T >= 2 * TB:
                        pe.wait_ge(added, T // TB - 1)
                    ins = nc.tensor.matmul(k.bank[T // TB % 2][:, ds(T % TB)], k.xT[:, ds(T)], w_all[:],
                                           start=True, stop=True)
                    if T % TB == TB - 1:
                        ins.then_inc(multiplied, 1)

            @block.vector
            def _(dve):
                order = Steps(dve, k.sem("lora_order", ctx))
                x = k.x[:].rearrange("p (t d) -> p t d", d=D)
                for b4 in range(B):
                    part = x[:, b4 * TB:(b4 + 1) * TB, :]
                    order.then(nc.vector.tensor_tensor(part, part, b[:, None, :].broadcast_to([P, TB, D]), ALU.add))
                    dve.wait_ge(multiplied, b4 + 1)
                    nc.vector.tensor_tensor(part, k.bank[b4 % 2].rearrange("p (t d) -> p t d", d=D), part,
                                            ALU.add).then_inc(added, 1)


def cross_attention(k, name, heads, mask, mask_kind, scale, biased, weighted, project):
    nc = k.nc
    dh = D // heads
    KW = P + 32
    HG = min(heads, 4)
    NG = heads // HG
    NB = TB * NG
    PER_BANK = min(HG, 2)
    BANKS = HG // PER_BANK
    CH = -(-HG * KW // P)
    J = KW // CH
    CR = HG * J
    GW = HG * (dh + 1)
    AHEAD = 2
    mask_tiles = k.dram[mask].shape[1] // SC
    centre_here = lambda g: not weighted and g % 2 == 0
    with Scope(k) as ctx:
        wq, wk, wv, bv = (load(k, ctx, f"{name}_{w}") for w in ("wq", "wk", "wv", "bv"))
        pairs = [(f"{name}_wq", wq), (f"{name}_wk", wk), (f"{name}_wv", wv), (f"{name}_bv", bv)]
        if biased:
            bq, bk = load(k, ctx, f"{name}_bq"), load(k, ctx, f"{name}_bk")
            pairs += [(f"{name}_bq", bq), (f"{name}_bk", bk)]
        if project:
            wo, bo = load(k, ctx, f"{name}_wo"), load(k, ctx, f"{name}_bo")
            pairs += [(f"{name}_wo", wo), (f"{name}_bo", bo)]
        mask_raw = k.sb(f"{name}_mask_raw", [P, mask_tiles * SC], k.dram[mask].dtype, ctx)
        mask_rows = mask_raw[:].rearrange("p (t s) -> p t s", s=SC)
        added = k.sb(f"{name}_mask", [P, mask_tiles, PER_BANK, KW], F32, ctx)
        prob = k.sb(f"{name}_prob", [P, NT * SC], F32, ctx) if weighted else None
        pairs += [(mask, mask_raw)] + ([("prob", prob)] if weighted else [])
        normalize(k, k.x, loads=(pairs, ctx))

        q_all = k.sb(f"{name}_q_all", [P, NTOK], F32, ctx)
        kT = k.sb(f"{name}_kT", [P, B, KW], F32, ctx)
        keys = k.sb(f"{name}_keys", [P, B, heads, KW], F32, ctx) if heads > 1 else kT[:].rearrange("p b (h s) -> p b h s", h=1)
        vals = k.sb(f"{name}_vals", [P, B, CH, heads, dh + 1], F32, ctx)
        rows_of = k.sb(f"{name}_rows_of", [P, heads, dh + 1], F32, ctx)
        spread = k.sb(f"{name}_spread", [P, 2, CH, CR], F32, ctx)
        raw = k.sb(f"{name}_raw_vals", [P, CH, heads, dh + 1], F32, ctx)
        k_made, k_taken, q_made, spread_made, v_made, v_taken, order = (
            k.sem(f"{name}_{n}", ctx) for n in ("k_made", "k_taken", "q_all_made", "spread_made", "v_made", "v_taken", "kv_order"))
        zeroed = k.sem(f"{name}_zeroed", ctx)
        HALF = B * SC // 2
        by_head = lambda a, n: a.rearrange("p (h d) -> p h d", h=n)
        with nc.Block() as block:
            @block.tensor
            def _(pe):
                for i in range(2):
                    nc.tensor.matmul(k.bank[i][:, 0:HALF], wk[:], k.ctxT[:, ds(i, HALF)], start=True,
                                     stop=True).then_inc(k_made, 1)
                for b in range(B):
                    pe.wait_ge(spread_made, b + 1)
                    if b > 0:
                        pe.wait_ge(v_taken, b)
                    for c in range(CH):
                        ins = nc.tensor.matmul(k.bank[2 + c // (CH - 1)][0:CR, ds(c % (CH - 1))], spread[:, b % 2, c, :], wv[:],
                                               start=True, stop=True)
                    ins.then_inc(v_made, 1)
                    nc.tensor.matmul(k.bank[4 + b], wq[:], k.xT[:, ds(b, S)], start=True, stop=True).then_inc(q_made, 1)

            @block.scalar
            def _(act):
                def spread_out(b):
                    whole = SC // CH
                    rest = SC - whole * CH
                    home = spread[:, b % 2].rearrange("p c (i j) -> p c i j", i=HG)
                    tokens = k.ctxT[:, bass.ds(b * SC, whole * CH)].rearrange("p (j c) -> p c j", c=CH)
                    for c in range(CH):
                        ins = nc.scalar.copy(home[:, c, :, 0:whole], tokens[:, c, None, :].broadcast_to([P, HG, whole]))
                        if c < rest:
                            one = k.ctxT[:, bass.ds(b * SC + whole * CH + c, 1)]
                            ins = nc.scalar.copy(home[:, c, :, whole:whole + 1], one[:, None, :].broadcast_to([P, HG, 1]))
                    ins.then_inc(spread_made, 1)

                act.wait_ge(zeroed, 1)
                spread_out(0)
                spread_out(1)
                for b in range(B):
                    if b + 2 < B:
                        act.wait_ge(v_made, b + 1)
                        spread_out(b + 2)
                    act.wait_ge(q_made, b + 1)
                    if biased:
                        nc.scalar.activation(q_all[:, ds(b, S)], k.bank[4 + b], ACT.Identity, bias=bq[:, 0:1])
                    else:
                        nc.scalar.copy(q_all[:, ds(b, S)], k.bank[4 + b])

            @block.vector
            def _(dve):
                step = Steps(dve, order)
                nc.vector.memset(spread[:], 0.0).then_inc(zeroed, 1)
                nc.vector.memset(raw[:], 1.0)
                step.then(nc.vector.memset(rows_of[:], 0.0))
                for i in range(HG):
                    own = rows_of[:].rearrange("p (g i) d -> p g i d", i=HG)[i * J:i * J + J, :, i, :]
                    nc.vector.memset(own, 1.0)
                nc.vector.memset(added[:], -HUGE)
                step.then(nc.vector.memset(kT[:, :, SC:KW], 0.0))
                for i in range(2):
                    dve.wait_ge(k_made, i + 1)
                    home = kT[:, 2 * i:2 * i + 2, 0:SC]
                    got = k.bank[i][:, 0:HALF].rearrange("p (b s) -> p b s", b=2)
                    if biased:
                        ins = nc.vector.tensor_scalar(home, got, bk[:, 0:1], None, ALU.add)
                    else:
                        ins = nc.vector.tensor_copy(home, got)
                    ins.then_inc(k_taken, 1)
                for b in range(B):
                    dve.wait_ge(v_made, b + 1)
                    for bank, c, n in ((2, 0, CH - 1), (3, CH - 1, 1)):
                        for c in range(c, c + n):
                            ins = nc.vector.tensor_tensor(raw[0:CR, c, :, 0:dh], by_head(k.bank[bank][0:CR, ds(c % (CH - 1))], heads),
                                                          by_head(bv[0:CR, :], heads), ALU.add)
                    ins.then_inc(v_taken, 1)
                    dve.wait_ge(v_taken, b + 1)
                    step.then(nc.vector.tensor_tensor(vals[0:CR, b], raw[0:CR], rows_of[0:CR, None].broadcast_to([CR, CH, heads, dh + 1]), ALU.mult))
                for i in range(PER_BANK):
                    home = added[:, :, i, 0:SC]
                    if mask_kind == "int":
                        nc.vector.tensor_scalar(home, mask_rows, 1.0, 1e9, ALU.subtract, ALU.mult)
                    elif mask_kind == "where":
                        nc.vector.tensor_scalar(home, mask_rows, 0.0, -HUGE, ALU.is_equal, ALU.mult)
                    else:
                        nc.vector.tensor_copy(home, mask_rows)
                if project:
                    x = k.x[:].rearrange("p (t d) -> p t d", d=D)
                    nc.vector.tensor_tensor(x, x, bo[:, None, :].broadcast_to([P, NT, D]), ALU.add)

            if heads > 1:
                @block.gpsimd
                def _(pool):
                    for b in range(B):
                        pool.wait_ge(k_taken, b // 2 + 1)
                        nc.gpsimd.tensor_tensor(
                            keys[:, b, :, :], kT[:, b, None, :].broadcast_to([P, heads, KW]),
                            k.headmask[:, :, None].broadcast_to([P, heads, KW]), ALU.mult)

        RING = 4
        qT = k.sb(f"{name}_qT", [P, S], F32, ctx)
        probs = k.sb(f"{name}_probs", [P, RING, HG * KW], F32, ctx)
        used = k.sb(f"{name}_weighted", [P, RING, HG * KW], F32, ctx) if weighted else probs
        probsT = k.sb(f"{name}_probsT", [P, 2, CH, P], F32, ctx)
        negmax = k.sb(f"{name}_negmax", [P, 2, heads], F32, ctx)
        sums = k.sb(f"{name}_sums", [P, 2, heads], F32, ctx)
        inv = k.sb(f"{name}_inv", [P, heads], F32, ctx)
        if project:
            outs = k.sb(f"{name}_outs", [P, NT, D], F32, ctx)
            outs_flat = outs[:].rearrange("p t d -> p (t d)")
        s = {n: k.sem(f"{name}_{n}", ctx) for n in ("q_ready", "scored", "score_read", "centred", "exped", "weighed", "turned",
                                                    "rest_copied", "copied", "mixed", "normed", "order", "prob_ready")}
        keys2 = keys[:].rearrange("p b h s -> p (b h s)") if heads > 1 else keys.rearrange("p b h s -> p (b h s)")
        vals2 = vals[:].rearrange("p b c h d -> p (b c h d)")
        added2 = added[:].rearrange("p t i s -> p (t i s)")
        W2 = PER_BANK * KW
        MIX, MISC = k.bank[6], k.bank[7]
        if weighted:
            prob_now = k.sb(f"{name}_prob_now", [P, TB, KW], F32, ctx)

        LAG = min(3, NG)

        def norm_due(G):
            t, g = divmod(G - LAG, NG)
            return t if g == NG - 1 and t >= 0 else None

        with nc.Block() as block:
            @block.tensor
            def _(pe):
                with pe.Fori(0, B) as b:
                    at = b * NB
                    pe.wait_ge(s["q_ready"], b + 1)

                    def score(G):
                        pe.wait_ge(s["score_read"], at + G + 1)
                        t, g = divmod(G, NG)
                        for i in range(BANKS):
                            ins = nc.tensor.matmul(k.bank[BANKS * (G % 2) + i][:, 0:W2], qT[:, ds(t)],
                                                   keys2[:, bass.ds((b * heads + g * HG + i * PER_BANK) * KW, W2)],
                                                   start=True, stop=True)
                        ins.then_inc(s["scored"], 1)

                    def turn(G):
                        pe.wait_ge(s["weighed" if weighted else "exped"], at + G + 1 + weighted)
                        for c in range(CH - 1):
                            nc.tensor.transpose(k.bank[4 + G % 2][0:CR, ds(c)], used[:, G % RING, c::CH], k.ident[:])
                        pe.wait_ge(s["rest_copied"], at + G + 1)
                        nc.tensor.transpose(MISC[0:CR, 0:P], used[:, G % RING, CH - 1::CH], k.ident[:]).then_inc(s["turned"], 1)

                    def mix(G):
                        pe.wait_ge(s["copied"], at + G + 1)
                        t, g = divmod(G, NG)
                        if g == 0:
                            pe.wait_ge(s["normed"], b * TB + t + 1)
                        for c in range(CH):
                            ins = nc.tensor.matmul(MIX[:, ds(g, GW)], probsT[0:CR, G % 2, c, :],
                                                   vals2[0:CR, bass.ds(((b * CH + c) * NG + g) * GW, GW)], start=c == 0, stop=c == CH - 1)
                        if g == NG - 1:
                            ins.then_inc(s["mixed"], 1)

                    score(0)
                    score(1)
                    for G in range(NB):
                        if G + 2 < NB:
                            score(G + 2)
                        turn(G)
                        if G > 0:
                            mix(G - 1)
                    mix(NB - 1)

            @block.scalar
            def _(act):
                free_at_first(act, s["rest_copied"])
                with act.Fori(0, B) as b:
                    at = b * NB
                    nc.scalar.copy(qT[:], q_all[:, ds(b, S)]).then_inc(s["q_ready"], 1)

                    def exp(G):
                        act.wait_ge(s["centred"], at + G + 1)
                        t, g = divmod(G, NG)
                        tile = probs[:, G % RING]
                        if centre_here(g):
                            ins = nc.scalar.activation(tile, tile, ACT.Exp)
                        else:
                            for h in range(HG):
                                hh = g * HG + h
                                ins = nc.scalar.activation(tile[:, ds(h, KW)], tile[:, ds(h, KW)], ACT.Exp, bias=negmax[:, t % 2, hh:hh + 1],
                                                           **({"accum_out": sums[:, t % 2, hh:hh + 1]} if weighted else {}))
                        ins.then_inc(s["exped"], 1)

                    exp(0)
                    for G in range(NB):
                        if G + 1 < NB:
                            exp(G + 1)
                        act.wait_ge(s["turned"], at + G + 1)
                        nc.scalar.copy(probsT[0:CR, G % 2, CH - 1, :], MISC[0:CR, 0:P]).then_inc(s["rest_copied"], 1)
                        nc.scalar.copy(probsT[0:CR, G % 2, 0:CH - 1, :], k.bank[4 + G % 2][0:CR, 0:(CH - 1) * P].rearrange("p (c n) -> p c n", n=P)).then_inc(s["copied"], 1)

            @block.vector
            def _(dve):
                free_at_first(dve, s["score_read"], by=AHEAD)
                free_at_first(dve, s["normed"])
                step = Steps(dve, s["order"])
                centred = sum(centre_here(G % NG) for G in range(NB))
                with dve.Fori(0, B) as b:
                    at = b * NB
                    step.turn(b, centred + TB * (1 + (mask_kind == "where")))

                    def norm(t):
                        dve.wait_ge(s["mixed"], b * TB + t + 1)
                        mix = by_head(MIX[:, 0:heads * (dh + 1)], heads)
                        step.then(nc.vector.reciprocal(inv[:], sums[:, t % 2, :] if weighted else mix[:, :, dh]))
                        if mask_kind == "where":
                            step.then(nc.vector.scalar_tensor_tensor(inv[:], negmax[:, t % 2, :], HUGE / 4, inv[:], ALU.is_lt, ALU.mult))
                        if project:
                            home = by_head(outs_flat[:, ds(b * TB + t)], heads)
                            nc.vector.tensor_tensor(home, mix[:, :, 0:dh], inv[:, :, None].broadcast_to([P, heads, dh]),
                                                    ALU.mult).then_inc(s["normed"], 1)
                        else:
                            home = k.x[:, ds(b * TB + t)]
                            nc.vector.scalar_tensor_tensor(home, MIX[:, 0:D], inv[:, 0:1], home, ALU.mult, ALU.add).then_inc(s["normed"], 1)

                    for G in range(NB):
                        t, g = divmod(G, NG)
                        tile = probs[:, G % RING]
                        mt = added2[:, ds(b * TB + t if mask_tiles == NT else t, W2)]
                        dve.wait_ge(s["scored"], at + G + 1)
                        nc.vector.scalar_tensor_tensor(
                            tile.rearrange("p (i s) -> p i s", i=BANKS), k.psum[:, BANKS * (G % 2):BANKS * (G % 2) + BANKS, 0:W2], scale,
                            mt[:, None, :].broadcast_to([P, BANKS, W2]), ALU.mult, ALU.add).then_inc(s["score_read"], 1)
                        dve.wait_ge(s["score_read"], at + G + 1 + AHEAD)
                        top = negmax[:, t % 2, g * HG:(g + 1) * HG]
                        maximum = nc.vector.tensor_reduce(top, by_head(tile, HG), AX_X, ALU.max, negate=True)
                        if centre_here(g):
                            step.then(maximum)
                            nc.vector.tensor_tensor(by_head(tile, HG), by_head(tile, HG), top[:, :, None].broadcast_to([P, HG, KW]),
                                                    ALU.add).then_inc(s["centred"], 1)
                        else:
                            maximum.then_inc(s["centred"], 1)
                        if norm_due(G) is not None:
                            norm(norm_due(G))
                    norm(TB - 1)
                step.turns_end(B)

            if weighted:
                @block.gpsimd
                def _(pool):
                    free_at_first(pool, s["weighed"], s["prob_ready"])
                    nc.gpsimd.memset(prob_now[:], 0.0).then_inc(s["prob_ready"], 1)
                    pool.wait_ge(s["prob_ready"], 2)
                    with pool.Fori(0, B) as b:
                        pool.wait_ge(s["weighed"], b * NB + 1)
                        nc.gpsimd.tensor_copy(prob_now[:, :, 0:SC], prob[:, ds(b, TB * SC)].rearrange("p (t s) -> p t s", t=TB)).then_inc(s["prob_ready"], 1)
                        pool.wait_ge(s["prob_ready"], b + 3)
                        for G in range(NB):
                            pool.wait_ge(s["exped"], b * NB + G + 1)
                            nc.gpsimd.tensor_tensor(by_head(used[:, G % RING], HG), by_head(probs[:, G % RING], HG),
                                                    prob_now[:, G // NG, None, :].broadcast_to([P, HG, KW]),
                                                    ALU.mult).then_inc(s["weighed"], 1)

        if project:
            add_projection(k, ctx, name, outs, wo, k.x)


def stage_1x(k):
    cross_attention(k, "a1", H16, "mask1", "int", DH ** -0.5, biased=True, weighted=True, project=True)


def stage_2x(k):
    cross_attention(k, "a2", 1, "mask2", "float", D ** -0.5, biased=False, weighted=False, project=False)


def stage_3x(k):
    cross_attention(k, "a3", H16, "mask3", "where", DH ** -0.5, biased=True, weighted=False, project=True)


def program(nc, dram, out):
    with ExitStack() as ctx:
        k = Core(nc, ctx, dram)
        loaded = k.sem("x_loaded")
        stored = k.sem("x_stored")
        x_tiles = k.x[:].rearrange("p (t d) -> p t d", d=D)
        with nc.Block() as block:
            @block.sync
            def _(sp):
                sp.dma_start(x_tiles, dram["x"].rearrange("(t p) d -> p t d", p=P)).then_inc(loaded, 16)
                sp.dma_start(k.ident[:], dram["identity"]).then_inc(loaded, 16)
                sp.dma_start(k.headmask[:], dram["headmask"]).then_inc(loaded, 16)
                sp.dma_start(k.ctxT[:], dram["ctxT"]).then_inc(loaded, 16)
                sp.wait_ge(loaded, 64)
        for stage in (stage_0x, stage_0f, stage_1x, stage_1f, stage_2x, stage_lora, stage_3x, stage_3f):
            stage(k)
        with nc.Block() as block:
            @block.sync
            def _(sp):
                sp.dma_start(out.rearrange("(t p) d -> p t d", p=P), x_tiles).then_inc(stored, 16)
                sp.wait_ge(stored, 16)


def constants():
    part = np.arange(P)
    freq = (1.0 / np.float32(10000.0) ** (np.arange(0, D, 2, dtype=np.float32) / np.float32(D))).astype(np.float64)
    angle = np.concatenate([freq, freq])[:, None] * np.arange(S)[None, :]
    sign = np.where(part < D // 2, 1.0, -1.0)[:, None]
    f = {
        "identity": np.eye(P),
        "headmask": (part[:, None] // DH == np.arange(H16)[None, :]),
        "own_rows": (np.arange(96)[:, None] % 32 // DH == np.arange(4)[None, :]),
        "rot_cos": np.cos(angle),
        "rot_sin": np.sin(angle) * sign,
        "key_waves": np.where(part[:, None] < D // 2, np.sin(angle), np.cos(angle)),
        "before": part[:, None] < part[None, :],
        "iota32": np.tile(np.arange(E1), (P, 1)),
        "iota16": np.tile(np.arange(E0), (P, 1)),
        "slot_base": np.tile(np.arange(E0) * CAP, (P, 1)),
        "spare_slot": SLOTS + np.arange(NT)[None, :] * P + part[:, None],
    }
    c = {n: np.ascontiguousarray(v, dtype=np.float32) for n, v in f.items()}
    bits = (1 << (MAG_BITS - 1 - np.arange(MAG_BITS))).astype(np.int32)
    c["bits"] = np.ascontiguousarray(np.tile(np.repeat(bits, E0), (P, 1)))
    return c


def laid_out(i):
    row = lambda v: np.broadcast_to(v.reshape(1, -1), (P, v.size))
    stack_columns = lambda w: np.tile(w.reshape(D, 4, 1, 32), (1, 1, 3, 1)).reshape(D, -1)
    stack_rows = lambda w: np.tile(w.reshape(4, 1, 32, D), (1, 3, 1, 1)).reshape(4, 96, D).transpose(1, 0, 2).reshape(96, -1)
    in_tiles = lambda v: v.reshape(-1, P, SC).transpose(1, 0, 2).reshape(P, -1)
    col = lambda v: v.reshape(-1, P).T
    a = {
        "x": i["x"].reshape(NTOK, D),
        "ctx": i["ctx_1024"],
        "ctxT": i["ctx_1024"].reshape(B * SC, D).T,
        "prob": in_tiles(i["fside_BxSxS2_0"]),
        "mask1": in_tiles(i["mask_BxSxS2_ik1"]),
        "mask2": in_tiles(i["mask_SxS2_fk0"]),
        "mask3": in_tiles(i["mask_1x1xSxS2_ik0"]),
        "a0_ln": np.stack([i["L0_xattn_gamma_media"], i["L0_xattn_beta_media"], i["L0_xattn_gamma_lat"], i["L0_xattn_beta_lat"]], 1),
        "a0_wq": i["L0_xattn_Wq"], "a0_bq": col(i["L0_xattn_bq"]),
        "a0_wk": i["L0_xattn_Wkv"][:, :8 * P], "a0_bk": col(i["L0_xattn_bkv"][:8 * P]), "a0_bv": col(i["L0_xattn_bkv"][8 * P:]),
        "a0_wvT": i["L0_xattn_Wkv"][:, 8 * P:].reshape(D, 8, P).transpose(2, 1, 0).reshape(P, -1),
        "a0_wo": i["L0_xattn_Wo"].reshape(8, P, D).transpose(1, 0, 2).reshape(P, -1), "a0_bo": row(i["L0_xattn_bo"]),
        "m0_gate_w": i["L0_ffn_gate_w"], "m0_gate_b": row(i["L0_ffn_gate_b"]),
        "m0_w13": np.concatenate([i["L0_ffn_ew1"], i["L0_ffn_ew3"]], 2),
        "m0_w2": i["L0_ffn_ew2"].reshape(E0, 2, P, D).transpose(0, 2, 1, 3).reshape(E0, P, 2 * D),
        "s0_w1": i["L0_ffn_sw1"].transpose(1, 0, 2).reshape(P, -1),
        "s0_w3": i["L0_ffn_sw3"].transpose(1, 0, 2).reshape(P, -1),
        "s0_w2": i["L0_ffn_sw2"].reshape(S0 * 2, P, D).transpose(1, 0, 2).reshape(P, -1),
        "a1_wq": i["L1_xattn_wq_k"], "a1_bq": col(i["L1_xattn_wq_b"]), "a1_wk": i["L1_xattn_wk_k"],
        "a1_bk": col(i["L1_xattn_wk_b"]), "a1_wv": i["L1_xattn_wv_k"], "a1_bv": row(i["L1_xattn_wv_b"]),
        "a1_wo": i["L1_xattn_wo_k"], "a1_bo": row(i["L1_xattn_wo_b"]),
        "f1_ln1": np.stack([i["L1_ffn_ln1_g"], i["L1_ffn_ln1_b"]], 1), "f1_ln2": np.stack([i["L1_ffn_ln2_g"], i["L1_ffn_ln2_b"]], 1),
        "f1_wq": stack_columns(i["L1_ffn_wq"]), "f1_wk": stack_columns(i["L1_ffn_wk"]), "f1_wv": i["L1_ffn_wv"], "f1_wo": i["L1_ffn_wo"],
        "f1_wpT": stack_rows(i["L1_ffn_wp"].T), "f1_wpT_swapped": stack_rows(np.roll(i["L1_ffn_wp"], D // 2, axis=0).T),
        "m1_sel": i["L1_ffn_sel_w"],
        "m1_w": np.concatenate([i["L1_ffn_keys"], i["L1_ffn_values"]], 2),
        "a2_wq": i["L2_xattn_Wq"].T, "a2_wk": i["L2_xattn_Wk"].T, "a2_wv": i["L2_xattn_Wv"].T, "a2_bv": row(i["L2_xattn_bv"]),
        "lora_wT": i["L2_ffn_W"].T, "lora_b": row(i["L2_ffn_b"]), "lora_downT": i["L2_ffn_lora_down"].T,
        "lora_down_aux": i["L2_ffn_down_aux"], "lora_upT": i["L2_ffn_lora_up"].T, "lora_up_auxT": i["L2_ffn_up_aux"].T,
        "a3_wq": i["L3_xattn_Wq"].T, "a3_bq": col(i["L3_xattn_bq"]), "a3_wk": i["L3_xattn_Wk"].T, "a3_bk": col(i["L3_xattn_bk"]),
        "a3_wv": i["L3_xattn_Wv"].T, "a3_bv": row(i["L3_xattn_bv"]), "a3_wo": i["L3_xattn_Wo"].T, "a3_bo": row(i["L3_xattn_bo"]),
        "f3_fc": i["L3_ffn_w_fc"].reshape(HID3 // P, P, D).transpose(1, 0, 2).reshape(P, -1),
        "f3_proj": i["L3_ffn_w_proj"], "f3_uT": i["L3_ffn_u"].T, "f3_v": i["L3_ffn_v"], "f3_bT": i["L3_ffn_fast_b"].T,
        "f3_gate": row(i["L3_ffn_gate"]),
    }
    return {n: np.ascontiguousarray(v) for n, v in a.items()} | constants()


def kernel(**inputs):
    import concourse.bacc as bacc
    from concourse.bass_utils import run_bass_kernel_spmd

    nc = bacc.Bacc("TRN2", target_bir_lowering=False, num_devices=1)
    arrays = laid_out({n: np.asarray(v) for n, v in inputs.items()})
    dram = {n: nc.dram_tensor(n + "_dram", a.shape, mybir.dt.from_np(a.dtype), kind="ExternalInput").ap()
            for n, a in arrays.items()}
    out = nc.dram_tensor("out_dram", (NTOK, D), F32, kind="ExternalOutput").ap()
    program(nc, dram, out)
    r = run_bass_kernel_spmd(nc, [{n + "_dram": a for n, a in arrays.items()}], core_ids=[0])
    return r.results[0]["out_dram"].reshape(B, S, D)
```

```python
from contextlib import ExitStack

import concourse.bass as bass
import numpy as np
from concourse import mybir

F32 = mybir.dt.float32
F32R = mybir.dt.float32r
BF16 = mybir.dt.bfloat16
I32 = mybir.dt.int32
ALU = mybir.AluOpType
ACT = mybir.ActivationFunctionType
AX_X = mybir.AxisListType.X

P = 128
D = 128
B = 4
S = 512
TB = S // P
NT = B * TB
NTOK = B * S
SC = 154
TAIL = SC - P
H16 = 16
DH = D // H16
E0, K0, HID0, S0 = 16, 2, 256, 2
CAP = -(-NTOK * K0 * 5 // (E0 * 4))
E1, K1 = 32, 4
HID3 = 512
SLOTS = E0 * CAP
MAG_BITS = 31
HUGE = 1.0e38
EPS = 1e-5


def ds(i, n=P):
    return bass.ds(i * n, n)


class Steps:

    def __init__(self, eng, sem):
        self.eng, self.sem, self.start, self.index, self.per, self.n = eng, sem, 0, None, 0, 0

    def then(self, ins):
        self.n += 1
        ins.then_inc(self.sem, 1)
        at = self.start + self.n
        self.eng.wait_ge(self.sem, at if self.index is None else self.index * self.per + at)
        return ins

    def turn(self, index, per):
        self.start, self.index, self.per, self.n = self.start + self.n if self.index is None else self.start, index, per, 0

    def turns_end(self, turns):
        assert self.n == self.per, (self.n, self.per)
        self.start, self.index, self.n = self.start + turns * self.per, None, 0


def free_at_first(eng, *sems, by=1):
    for s in sems:
        eng.sem_inc(s, by)


def over_batches(eng, heads, lead, first, steps, last):
    with eng.Fori(0, B) as b:
        first(b)
        if lead:
            steps(b, 0, 0, lead)
        with eng.Fori(0, TB - 1) as t:
            steps(b, t, lead, heads + lead)
        steps(b, TB - 1, lead, heads)
        last(b)


class Scope(ExitStack):

    def __init__(self, k):
        super().__init__()
        self.nc, self.sems = k.nc, []

    def __exit__(self, *error):
        if error[0] is None:
            numbers = sorted(s.num for s in self.sems)
            while numbers:
                run = next((i for i in range(1, len(numbers)) if numbers[i] != numbers[i - 1] + 1), len(numbers))
                self.nc.all_engine_barrier(sems_to_clear=range(numbers[0], numbers[run - 1] + 1))
                numbers = numbers[run:]
        return super().__exit__(*error)


class Core:

    def __init__(self, nc, ctx, dram):
        self.nc, self.dram, self.ctx = nc, dram, ctx
        self.x = self.sb("x_rows", [P, NT * D])
        self.xT = self.sb("xn_cols", [P, NTOK])
        self.norm = self.sb("norm_rows", [P, NT * D])
        self.stats = self.sb("bn_stats_out", [P, NT * 6])
        self.mv = self.sb("mean_var", [P, NT, 2])
        self.rstd = self.sb("rstd", [P, 4, NT])
        self.ident = self.sb("identity", [P, P])
        self.headmask = self.sb("headmask", [P, H16])
        self.ctxT = self.sb("ctx_cols", [P, B * SC])
        self.psum = ctx.enter_context(nc.psum_tensor("psum", [P, 8, 512], F32))
        self.bank = [self.psum[:, i, :] for i in range(8)]
        self.norms = self.ln_turns = 0
        self.ln_order = self.sem("ln_order")
        self.ln_var = self.sem("ln_var")
        self.ln_sqrt = self.sem("ln_sqrt")
        self.ln_normed = self.sem("ln_normed")
        self.ln_turned = self.sem("ln_turned")
        self.ln_steps = 0

    def sb(self, name, shape, dt=F32, ctx=None):
        return (ctx or self.ctx).enter_context(self.nc.sbuf_tensor(name, shape, dt))

    def sem(self, name, ctx=None):
        s = (ctx or self.ctx).enter_context(self.nc.semaphore(name))
        if ctx is not None:
            ctx.sems.append(s)
        return s


def load(k, ctx, name, parts=P):
    return k.sb(name, [parts, k.dram[name].shape[1]], F32, ctx)


def normalize(k, src, gain=None, bias=None, rows=None, turned=True, loads=None):
    nc = k.nc
    n, k.norms = k.norms, k.norms + 1
    turns, k.ln_turns = k.ln_turns, k.ln_turns + turned
    steps0 = k.ln_steps
    k.ln_steps += 7
    r = k.rstd
    to = k.norm[:] if rows is None else rows
    pairs, ctx = loads or ((), None)
    loaded = k.sem("fetched_" + pairs[0][0], ctx) if pairs else None
    with nc.Block() as block:
        @block.sync
        def _(sp):
            for name, home in pairs:
                sp.dma_start(home[:], k.dram[name]).then_inc(loaded, 16)
            if pairs:
                sp.wait_ge(loaded, 16 * len(pairs))

        @block.vector
        def _(dve):
            step = Steps(dve, k.ln_order)
            step.start = steps0
            for T in range(NT):
                ins = nc.vector.bn_stats(k.stats[:, ds(T, 6)], src[:, ds(T)])
            step.then(ins)
            for T in range(NT):
                ins = nc.vector.bn_aggr(k.mv[:, T, :], k.stats[:, ds(T, 6)])
            step.then(ins)
            nc.vector.tensor_scalar(r[:, 0, :], k.mv[:, :, 1], EPS, None, ALU.add).then_inc(k.ln_var, 1)
            dve.wait_ge(k.ln_var, n + 1)
            dve.wait_ge(k.ln_sqrt, n + 1)
            step.then(nc.vector.reciprocal(r[:, 1, :], r[:, 1, :]))
            step.then(nc.vector.tensor_tensor(r[:, 2, :], r[:, 1, :], r[:, 1, :], ALU.mult))
            step.then(nc.vector.tensor_tensor(r[:, 2, :], r[:, 2, :], r[:, 0, :], ALU.mult))
            step.then(nc.vector.tensor_scalar(r[:, 2, :], r[:, 2, :], -0.5, 1.5, ALU.mult, ALU.add))
            step.then(nc.vector.tensor_tensor(r[:, 3, :], r[:, 2, :], r[:, 1, :], ALU.mult))
            for T in range(NT):
                nc.vector.tensor_scalar(to[:, ds(T)], src[:, ds(T)], k.mv[:, T, 0:1], r[:, 3, T:T + 1], ALU.subtract,
                                        ALU.mult).then_inc(k.ln_normed, 1)

        @block.scalar
        def _(act):
            act.wait_ge(k.ln_var, n + 1)
            nc.scalar.activation(r[:, 1, :], r[:, 0, :], ACT.Sqrt).then_inc(k.ln_sqrt, 1)
            if turned:
                if gain is not None and pairs:
                    act.wait_ge(loaded, 16 * len(pairs))
                for b in range(B):
                    act.wait_ge(k.ln_turned, turns * B + b + 1)
                    if gain is None:
                        nc.scalar.copy(k.xT[:, ds(b, S)], k.bank[b])
                    else:
                        nc.scalar.activation(k.xT[:, ds(b, S)], k.bank[b], ACT.Identity, scale=gain, bias=bias)

        if turned:
            @block.tensor
            def _(pe):
                for T in range(NT):
                    pe.wait_ge(k.ln_normed, n * NT + T + 1)
                    ins = nc.tensor.transpose(k.bank[T // TB][:, ds(T % TB)], to[:, ds(T)], k.ident[:])
                    if T % TB == TB - 1:
                        ins.then_inc(k.ln_turned, 1)


def add_projection(k, ctx, name, outs, wo, home):
    nc = k.nc
    outsT = k.sb(f"{name}_outsT", [P, NT * P], F32, ctx)
    out_turned, out_copied, projected = (k.sem(f"{name}_{n}", ctx) for n in ("out_turned", "out_copied", "projected"))
    with nc.Block() as block:
        @block.tensor
        def _(pe):
            for T in range(NT):
                ins = nc.tensor.transpose(k.bank[T // TB][:, ds(T % TB)], outs[:, T, :], k.ident[:])
                if T % TB == TB - 1:
                    ins.then_inc(out_turned, 1)
            for b in range(B):
                pe.wait_ge(out_copied, b + 1)
                for t in range(TB):
                    ins = nc.tensor.matmul(k.bank[4 + b][:, ds(t)], outsT[:, ds(b * TB + t)], wo[:], start=True, stop=True)
                ins.then_inc(projected, 1)

        @block.scalar
        def _(act):
            for b in range(B):
                act.wait_ge(out_turned, b + 1)
                nc.scalar.copy(outsT[:, ds(b, S)], k.bank[b]).then_inc(out_copied, 1)

        @block.vector
        def _(dve):
            for b in range(B):
                dve.wait_ge(projected, b + 1)
                nc.vector.tensor_tensor(home[:, ds(b, S)], k.bank[4 + b], home[:, ds(b, S)], ALU.add)


def first_hit(nc, step, left, hit, best, first, iota, far, shape):
    step.then(nc.vector.tensor_reduce(best[:], left[:], AX_X, ALU.max))
    step.then(nc.vector.tensor_tensor(hit[:], left[:], best[:, :, None].broadcast_to(shape), ALU.is_equal))
    step.then(nc.vector.scalar_tensor_tensor(hit[:], hit[:], -100.0, far[:, None, :].broadcast_to(shape), ALU.mult, ALU.add))
    step.then(nc.vector.tensor_reduce(first[:], hit[:], AX_X, ALU.min))
    step.then(nc.vector.tensor_tensor(hit[:], iota[:, None, :].broadcast_to(shape), first[:, :, None].broadcast_to(shape), ALU.is_equal))


def stage_0x(k):
    nc = k.nc
    H = 8
    KEYS = SC + S
    CHUNKS = -(-KEYS // P)
    LAST = KEYS - (CHUNKS - 1) * P
    HALF = KEYS // 2
    WIDE = HALF + HALF % 2
    HB = TB * H
    scale = P ** -0.5
    with Scope(k) as ctx:
        names = ("a0_ln", "a0_wq", "a0_bq", "a0_wk", "a0_wvT", "a0_bk", "a0_bv", "a0_wo", "a0_bo")
        ln, wq, bq, wk, wvT, bk, bv, wo, bo = homes = [load(k, ctx, n) for n in names]
        CT = 2 * B
        rows = load(k, ctx, "ctx_rows")
        rows3 = rows[:].rearrange("p (t d) -> p t d", d=D)
        cT = k.sb("a0_ctxT", [P, B * SC], F32, ctx)
        xn = k.sb("a0_xn", [P, NT * D], F32, ctx)
        normalize(k, k.x, rows=xn, turned=False, loads=(list(zip(names + ("ctx_rows",), homes + [rows])), ctx))

        sizes = [(P, TAIL)[i % 2] for i in range(CT)]
        stats = k.sb("a0_ctx_stats", [P, CT, 6], F32, ctx)
        mv = k.sb("a0_ctx_mv", [P, CT, 2], F32, ctx)
        r = k.sb("a0_ctx_rstd", [P, 4, CT], F32, ctx)
        order, var, root, turned, stored = (k.sem(f"a0_ctx_{n}", ctx) for n in ("order", "var", "root", "turned", "stored"))
        with nc.Block() as block:
            @block.vector
            def _(dve):
                step = Steps(dve, order)
                nc.vector.memset(stats[:], 0.0)
                step.then(nc.vector.memset(mv[:], 1.0))
                for i, n in enumerate(sizes):
                    ins = nc.vector.bn_stats(stats[0:n, i, :], rows3[0:n, i, :])
                step.then(ins)
                for i, n in enumerate(sizes):
                    ins = nc.vector.bn_aggr(mv[0:n, i, :], stats[0:n, i, :])
                step.then(ins)
                nc.vector.tensor_scalar(r[:, 0, :], mv[:, :, 1], EPS, None, ALU.add).then_inc(var, 1)
                dve.wait_ge(root, 1)
                step.then(nc.vector.reciprocal(r[:, 1, :], r[:, 1, :]))
                step.then(nc.vector.tensor_tensor(r[:, 2, :], r[:, 1, :], r[:, 1, :], ALU.mult))
                step.then(nc.vector.tensor_tensor(r[:, 2, :], r[:, 2, :], r[:, 0, :], ALU.mult))
                step.then(nc.vector.tensor_scalar(r[:, 2, :], r[:, 2, :], -0.5, 1.5, ALU.mult, ALU.add))
                step.then(nc.vector.tensor_tensor(r[:, 3, :], r[:, 2, :], r[:, 1, :], ALU.mult))
                for i, n in enumerate(sizes):
                    nc.vector.tensor_scalar(rows3[0:n, i, :], rows3[0:n, i, :], mv[0:n, i, 0:1], r[0:n, 3, i:i + 1],
                                            ALU.subtract, ALU.mult).then_inc(stored, 1)

            @block.scalar
            def _(act):
                act.wait_ge(var, 1)
                nc.scalar.activation(r[:, 1, :], r[:, 0, :], ACT.Sqrt).then_inc(root, 1)
                for b in range(B):
                    act.wait_ge(turned, b + 1)
                    nc.scalar.activation(cT[:, ds(b, SC)], k.bank[b][:, 0:SC], ACT.Identity, scale=ln[:, 0:1], bias=ln[:, 1:2])

            @block.tensor
            def _(pe):
                for i, n in enumerate(sizes):
                    pe.wait_ge(stored, i + 1)
                    ins = nc.tensor.transpose(k.bank[i // 2][:, (i % 2) * P:(i % 2) * P + n], rows3[0:n, i, :], k.ident[0:n, 0:n])
                    if i % 2:
                        ins.then_inc(turned, 1)
        normalize(k, xn, ln[:, 2:3], ln[:, 3:4])

        w_vo = k.sb("a0_w_vo", [P, H, D], F32, ctx)
        b_vo = k.sb("a0_b_vo", [P, H, D], F32, ctx)
        bv_columns = k.sb("a0_bv_columns", [P, H, P], F32, ctx)
        bq_scaled = k.sb("a0_bq_scaled", [P, H], F32, ctx)
        k_high = k.sb("a0_k_high", [P, H, 2 * WIDE], F32R, ctx)
        k_low = k.sb("a0_k_low", [P, H, 2 * WIDE], F32R, ctx)
        spread, scaled, folded, folded_b = (k.sem(f"a0_{n}", ctx) for n in ("bv_spread", "bq_scaled", "w_folded", "b_folded"))
        with nc.Block() as block:
            @block.tensor
            def _(pe):
                for h in range(H):
                    ins = nc.tensor.matmul(k.bank[h // 4][:, ds(h % 4)], wvT[:, ds(h)], wo[:, ds(h)], start=True, stop=True)
                ins.then_inc(folded, 1)
                pe.wait_ge(spread, 1)
                for h in range(H):
                    ins = nc.tensor.matmul(k.bank[2 + h // 4][:, ds(h % 4)], bv_columns[:, h, :], wo[:, ds(h)], start=True, stop=True)
                ins.then_inc(folded_b, 1)

            @block.scalar
            def _(act):
                act.wait_ge(folded, 1)
                for i in range(2):
                    nc.scalar.copy(w_vo[:, 4 * i:4 * i + 4, :], k.bank[i].rearrange("p (h d) -> p h d", h=4))

            @block.vector
            def _(dve):
                nc.vector.tensor_copy(bv_columns[:], bv[:, :, None].broadcast_to([P, H, P])).then_inc(spread, 1)
                nc.vector.tensor_scalar(bq_scaled[:], bq[:], scale, None, ALU.mult).then_inc(scaled, 1)
                dve.wait_ge(scaled, 1)
                x = k.x[:].rearrange("p (t d) -> p t d", d=D)
                nc.vector.tensor_tensor(x, x, bo[:, None, :].broadcast_to([P, NT, D]), ALU.add)
                for cut in (k_high, k_low):
                    for i in range(2):
                        nc.vector.tensor_scalar(cut[:, :, i * WIDE + HALF], bq_scaled[:], 0.0, None, ALU.mult)
                dve.wait_ge(folded_b, 1)
                for i in range(2):
                    nc.vector.tensor_copy(b_vo[:, 4 * i:4 * i + 4, :], k.bank[2 + i].rearrange("p (h d) -> p h d", h=4))

        inputs = k.sb("a0_inputs", [P, KEYS], F32, ctx)
        q_all = k.sb("a0_q", [P, H, S], F32, ctx)
        q_high = k.sb("a0_q_high", [P, H, P], F32R, ctx)
        q_low = k.sb("a0_q_low", [P, H, P], F32R, ctx)
        q_now = k.sb("a0_q_now", [P, 4, P], F32, ctx)
        one = k.sb("a0_one", [P, 4], F32, ctx)
        vo = k.sb("a0_vo", [P, CHUNKS, H * D], F32, ctx)
        probs = k.sb("a0_probs", [P, 2, KEYS], F32, ctx)
        probsT = k.sb("a0_probsT", [P, 2, CHUNKS, P], F32, ctx)
        negmax = k.sb("a0_negmax", [P, H], F32, ctx)
        sums = k.sb("a0_sums", [P, H], F32, ctx)
        inv = k.sb("a0_inv", [P, H], F32, ctx)
        s = {n: k.sem(f"a0_{n}", ctx) for n in ("inputs_ready", "k_made", "k_high_made", "k_low_made", "q_made", "q_taken", "q_cut", "q_fetched",
                                                "q_high_made", "vo_made", "vo_taken", "scored", "maxed", "exped", "turned",
                                                "copied_a", "copied_v", "mixed", "inverted", "added")}
        w_vo2 = w_vo[:].rearrange("p h d -> p (h d)")
        b_vo2 = b_vo[:].rearrange("p h d -> p (h d)")
        PARTS = ((0, 0, 0, SC), (1, 0, SC, HALF - SC), (1, HALF - SC, WIDE, HALF))
        rows_of = lambda c: P if c < CHUNKS - 1 else LAST

        def heads_before(b, t, h):
            return b * HB + t * H + h

        def ahead(t, h):
            return h < H or not isinstance(t, int) or t < TB - 1

        with nc.Block() as block:
            @block.tensor
            def _(pe):
                def score(b, t, h):
                    if h % 4 == 0:
                        pe.wait_ge(s["q_cut"], (b * TB + t) * 2 + h // 4 + 2)
                    pe.wait_ge(s["exped"], heads_before(b, t, h) + 1)
                    n = h % H
                    for i in range(2):
                        bank = k.bank[2 * (h % 2) + i][:, 0:WIDE]
                        nc.tensor.matmul(bank, q_high[:, n, :], k_high[:, n, ds(i, WIDE)], start=True, stop=False)
                        nc.tensor.matmul(bank, q_high[:, n, :], k_low[:, n, ds(i, WIDE)], start=False, stop=False)
                        ins = nc.tensor.matmul(bank, q_low[:, n, :], k_high[:, n, ds(i, WIDE)], start=False, stop=True)
                    ins.then_inc(s["scored"], 1)

                def turn(b, t, h):
                    pe.wait_ge(s["exped"], heads_before(b, t, h) + 3)
                    pe.wait_ge(s["copied_a"], heads_before(b, t, h) + 1)
                    pe.wait_ge(s["copied_v"], heads_before(b, t, h) + 1)
                    for c in range(CHUNKS):
                        n = rows_of(c)
                        ins = nc.tensor.transpose(k.bank[4 + c // 4][0:n, ds(c % 4)], probs[:, h % 2, c * P:c * P + n], k.ident[:])
                    ins.then_inc(s["turned"], 1)

                def mix(b, t, h):
                    pe.wait_ge(s["copied_a"], heads_before(b, t, h) + 2)
                    pe.wait_ge(s["copied_v"], heads_before(b, t, h) + 2)
                    pe.wait_ge(s["added"], heads_before(b, t, h) + 1)
                    for c in range(CHUNKS):
                        n = rows_of(c)
                        ins = nc.tensor.matmul(k.bank[6 + h % 2][:, 0:D], probsT[0:n, h % 2, c, :], vo[0:n, c, ds(h)],
                                               start=c == 0, stop=c == CHUNKS - 1)
                    ins.then_inc(s["mixed"], 1)

                def first(b):
                    pe.wait_ge(s["added"], b * HB + 2)
                    for h in range(H):
                        pe.wait_ge(s["k_low_made"], b * H + h + 1)
                        nc.tensor.matmul(k.bank[2 * (h % 2)][:, 0:SC], wk[:, ds(h)], cT[:, ds(b, SC)], start=True, stop=True)
                        nc.tensor.matmul(k.bank[2 * (h % 2) + 1], wk[:, ds(h)], k.xT[:, ds(b, S)], start=True, stop=True).then_inc(s["k_made"], 1)
                        pe.wait_ge(s["q_taken"], b * H + h + 1)
                        nc.tensor.matmul(k.bank[6 + h % 2], wq[:, ds(h)], k.xT[:, ds(b, S)], start=True, stop=True).then_inc(s["q_made"], 1)
                    pe.wait_ge(s["inputs_ready"], b + 1)
                    for c in range(CHUNKS):
                        n = rows_of(c)
                        if c == 1:
                            pe.wait_ge(s["q_taken"], b * H + H + 2)
                        pe.wait_ge(s["vo_taken"], b * CHUNKS + c + 1)
                        for i in range(2):
                            ins = nc.tensor.matmul(k.bank[4 + 2 * (c % 2) + i][0:n, :], inputs[:, c * P:c * P + n], w_vo2[:, ds(i, 4 * D)],
                                                   start=True, stop=True)
                        ins.then_inc(s["vo_made"], 1)
                    pe.wait_ge(s["k_low_made"], b * H + H + 2)
                    score(b, 0, 0)
                    pe.wait_ge(s["vo_taken"], b * CHUNKS + CHUNKS + 2)

                def steps(b, t, start, end):
                    for h in range(start, end):
                        if ahead(t, h + 1):
                            score(b, t, h + 1)
                        turn(b, t, h)
                        if h > 0:
                            mix(b, t, h - 1)

                over_batches(pe, H, 1, first, steps, lambda b: mix(b, TB - 1, H - 1))

            @block.gpsimd
            def _(pool):
                def cut(b, t, half):
                    heads = slice(4 * half, 4 * half + 4)
                    n = (b * TB + t) * 2 + half
                    if isinstance(t, int) and t == 0:
                        q = q_all[:, heads, 0:P]
                    else:
                        pool.wait_ge(s["q_cut"], n + 1)
                        q = q_now[:]
                        nc.gpsimd.tensor_copy(q, q_all[:, heads, bass.ds(t * P, P)]).then_inc(s["q_fetched"], 1)
                        pool.wait_ge(s["q_fetched"], b * (2 * TB - 2) + t * 2 + half - 1)
                    nc.gpsimd.tensor_tensor(q_high[:, heads, :], q, one[:, :, None].broadcast_to([P, 4, P]), ALU.mult).then_inc(s["q_high_made"], 1)
                    pool.wait_ge(s["q_high_made"], n + 1)
                    nc.gpsimd.tensor_tensor(q_low[:, heads, :], q, q_high[:, heads, :].bitcast(F32), ALU.subtract).then_inc(s["q_cut"], 1)

                def first(b):
                    nc.gpsimd.tensor_copy(inputs[:, 0:SC], cT[:, ds(b, SC)])
                    nc.gpsimd.tensor_copy(inputs[:, SC:KEYS], k.xT[:, ds(b, S)]).then_inc(s["inputs_ready"], 1)
                    pool.wait_ge(s["q_taken"], b * H + H + 2)
                    cut(b, 0, 0)
                    cut(b, 0, 1)

                def steps(b, t, start, end):
                    for half in range(2):
                        if ahead(t, H):
                            pool.wait_ge(s["scored"], heads_before(b, t, 4 * half + 4))
                            cut(b, t + 1, half)

                nc.gpsimd.memset(one[:], 1.0).then_inc(s["q_cut"], 1)
                pool.wait_ge(s["q_cut"], 1)
                over_batches(pool, H, 0, first, steps, lambda b: None)

            @block.scalar
            def _(act):
                def exp(b, t, h):
                    act.wait_ge(s["maxed"], heads_before(b, t, h) + 1)
                    n = h % H
                    nc.scalar.activation(probs[:, h % 2, :].rearrange("p (i k) -> p i k", i=2), k.psum[:, 2 * (h % 2):2 * (h % 2) + 2, 0:HALF],
                                         ACT.Exp, bias=negmax[:, n:n + 1], accum_out=sums[:, n:n + 1]).then_inc(s["exped"], 1)

                def first(b):
                    act.wait_ge(s["q_cut"], b * TB * 2 + 1)
                    for h in range(H):
                        act.wait_ge(s["k_made"], b * H + h + 1)
                        for bank, start, home, n in PARTS:
                            ins = nc.scalar.activation(k_high[:, h, home:home + n], k.bank[2 * (h % 2) + bank][:, start:start + n],
                                                       ACT.Identity, bias=bk[:, h:h + 1])
                        ins.then_inc(s["k_high_made"], 1)
                        act.wait_ge(s["q_made"], b * H + h + 1)
                        nc.scalar.activation(q_all[:, h, :], k.bank[6 + h % 2], ACT.Identity, scale=scale, bias=bq_scaled[:, h:h + 1]).then_inc(s["q_taken"], 1)
                    exp(b, 0, 0)

                def steps(b, t, start, end):
                    for h in range(start, end):
                        if ahead(t, h + 1):
                            exp(b, t, h + 1)
                        act.wait_ge(s["turned"], heads_before(b, t, h) + 1)
                        nc.scalar.copy(probsT[:, h % 2, 0:4, :], k.bank[4].rearrange("p (c q) -> p c q", c=4)).then_inc(s["copied_a"], 1)

                free_at_first(act, s["exped"], s["q_taken"], by=2)
                free_at_first(act, s["copied_a"])
                over_batches(act, H, 1, first, steps, lambda b: None)

            @block.vector
            def _(dve):
                def maximum(b, t, h):
                    n = h % H
                    dve.wait_ge(s["scored"], heads_before(b, t, h) + 1)
                    nc.vector.tensor_reduce(negmax[:, n:n + 1], k.psum[:, 2 * (h % 2):2 * (h % 2) + 2, 0:HALF],
                                            mybir.AxisListType.XY, ALU.max, negate=True).then_inc(s["maxed"], 1)

                def add(b, t, h):
                    nc.vector.reciprocal(inv[:, h:h + 1], sums[:, h:h + 1]).then_inc(s["inverted"], 1)
                    dve.wait_ge(s["inverted"], heads_before(b, t, h) + 1)
                    dve.wait_ge(s["mixed"], heads_before(b, t, h) + 1)
                    x = k.x[:, ds(b * TB + t)]
                    nc.vector.scalar_tensor_tensor(x, k.bank[6 + h % 2][:, 0:D], inv[:, h:h + 1], x, ALU.mult, ALU.add).then_inc(s["added"], 1)

                def first(b):
                    for h in range(H):
                        dve.wait_ge(s["k_high_made"], b * H + h + 1)
                        for bank, start, home, n in PARTS:
                            ins = nc.vector.scalar_tensor_tensor(k_low[:, h, home:home + n], k.bank[2 * (h % 2) + bank][:, start:start + n],
                                                                 bk[:, h:h + 1], k_high[:, h, home:home + n].bitcast(F32), ALU.add, ALU.subtract)
                        ins.then_inc(s["k_low_made"], 1)
                    for c in range(CHUNKS):
                        n = rows_of(c)
                        dve.wait_ge(s["vo_made"], b * CHUNKS + c + 1)
                        for i in range(2):
                            ins = nc.vector.tensor_tensor(vo[0:n, c, ds(i, 4 * D)], k.bank[4 + 2 * (c % 2) + i][0:n, :],
                                                          b_vo2[0:n, ds(i, 4 * D)], ALU.add)
                        ins.then_inc(s["vo_taken"], 1)
                    maximum(b, 0, 0)

                def steps(b, t, start, end):
                    for h in range(start, end):
                        if ahead(t, h + 1):
                            maximum(b, t, h + 1)
                        dve.wait_ge(s["turned"], heads_before(b, t, h) + 1)
                        nc.vector.tensor_copy(probsT[:, h % 2, 4:6, :], k.bank[5][:, 0:2 * P].rearrange("p (c q) -> p c q", c=2)).then_inc(s["copied_v"], 1)
                        if h > 0:
                            add(b, t, h - 1)

                free_at_first(dve, s["k_low_made"], s["vo_taken"], s["added"], by=2)
                free_at_first(dve, s["copied_v"])
                over_batches(dve, H, 1, first, steps, lambda b: add(b, TB - 1, H - 1))


def stage_1f(k):
    nc = k.nc
    with Scope(k) as ctx:
        src = k.sb("f1_src", [P, NT * D], F32, ctx)
        normalize(k, k.x, rows=src, turned=False)
        relative_attention(k, src)
        relu_experts(k, src)
        with nc.Block() as block:
            @block.vector
            def _(dve):
                nc.vector.tensor_tensor(k.x[:], k.x[:], src[:], ALU.add)


def relative_attention(k, src):
    nc = k.nc
    scale = DH ** -0.5
    QUADS = H16 // 4
    TERMS = 3
    R = TERMS * 4 * DH
    LOW_OF_Q, LOW_OF_K = slice(2 * R // 3, R), slice(R // 3, 2 * R // 3)
    W1 = H16 * (DH + 1)
    SCORES, RING = 2, 8
    HB = TB * H16
    with Scope(k) as ctx:
        names = ("f1_ln1", "f1_wq", "f1_wk", "f1_wv", "f1_wo", "rot_cos", "rot_sin", "key_waves")
        ln, wq, wk, wv, wo, rot_cos, rot_sin, waves = homes = [load(k, ctx, n) for n in names]
        position_names = ("f1_wpT", "f1_wpT_swapped")
        position_w = [k.sb(n, [R, QUADS * D], F32, ctx) for n in position_names]
        own_rows = load(k, ctx, "own_rows", R)
        normalize(k, src, ln[:, 0:1], ln[:, 1:2],
                  loads=(list(zip(names + position_names + ("own_rows",), homes + position_w + [own_rows])), ctx))
        q_stack = k.sb("f1_q_stack", [R, QUADS, NTOK], F32R, ctx)
        k_stack = k.sb("f1_k_stack", [R, QUADS, NTOK], F32R, ctx)
        w_stack = [k.sb(f"f1_w_stack{i}", [R, QUADS, D], F32R, ctx) for i in range(2)]
        waves_high = k.sb("f1_waves_high", [P, S], F32R, ctx)
        waves_low = k.sb("f1_waves_low", [P, S], F32R, ctx)
        vals = k.sb("f1_vals", [P, NT, H16, DH + 1], F32, ctx)
        made, high_made, split, ones, v_made, v_taken, high_w = (
            k.sem(f"f1_prepare_{n}", ctx) for n in ("made", "high_made", "split", "ones", "v_made", "v_taken", "high_weights"))
        work = [(b, j, w, home, low, factor) for b in range(B) for j in range(QUADS)
                for w, home, low, factor in ((wq, q_stack, LOW_OF_Q, scale), (wk, k_stack, LOW_OF_K, 1.0))]
        with nc.Block() as block:
            @block.tensor
            def _(pe):
                for n, (b, j, w, *_) in enumerate(work):
                    if n >= 4:
                        pe.wait_ge(split, n - 3)
                    nc.tensor.matmul(k.bank[n % 4][0:R], w[:, ds(j, R)], k.xT[:, ds(b, S)], start=True, stop=True).then_inc(made, 1)
                    if n % 2 == 1:
                        T = n // 2
                        if T >= 4:
                            pe.wait_ge(v_taken, T - 3)
                        nc.tensor.matmul(k.bank[4 + T % 4][:, 0:D], k.xT[:, ds(T)], wv[:], start=True, stop=True).then_inc(v_made, 1)

            @block.scalar
            def _(act):
                for i in range(2):
                    ins = nc.scalar.copy(w_stack[i][:].rearrange("r j d -> r (j d)"), position_w[i][:])
                nc.scalar.copy(waves_high[:], waves[:]).then_inc(high_w, 1)
                for n, (b, j, w, home, low, factor) in enumerate(work):
                    act.wait_ge(made, n + 1)
                    nc.scalar.activation(home[:, j, ds(b, S)], k.bank[n % 4][0:R], ACT.Copy, scale=factor).then_inc(high_made, 1)

            @block.vector
            def _(dve):
                nc.vector.memset(vals[:], 1.0).then_inc(ones, 1)
                dve.wait_ge(high_w, 1)
                for i in range(2):
                    cut = w_stack[i][LOW_OF_K].rearrange("r j d -> r (j d)")
                    nc.vector.tensor_tensor(cut, position_w[i][LOW_OF_K, :], cut.bitcast(F32), ALU.subtract)
                nc.vector.tensor_tensor(waves_low[:], waves[:], waves_high[:].bitcast(F32), ALU.subtract)
                dve.wait_ge(ones, 1)
                for n, (b, j, w, home, low, factor) in enumerate(work):
                    dve.wait_ge(high_made, n + 1)
                    cut = home[low, j, ds(b, S)]
                    nc.vector.scalar_tensor_tensor(cut, k.bank[n % 4][low], factor, cut.bitcast(F32), ALU.mult, ALU.subtract).then_inc(split, 1)
                    if n % 2 == 1:
                        T = n // 2
                        dve.wait_ge(v_made, T + 1)
                        nc.vector.tensor_copy(vals[:, T, :, 0:DH], k.bank[4 + T % 4][:, 0:D].rearrange("p (h d) -> p h d", d=DH)).then_inc(v_taken, 1)

        q_head = k.sb("f1_q_head", [R, H16, P], F32R, ctx)
        turn_cos = k.sb("f1_turn_cos", [P, 4, P], F32, ctx)
        turn_sin = k.sb("f1_turn_sin", [P, 4, P], F32, ctx)
        turned = k.sb("f1_turned_u", [P, 4, P], F32, ctx)
        turned_high = k.sb("f1_turned_high", [P, 2, 4, P], F32R, ctx)
        turned_low = k.sb("f1_turned_low", [P, 2, 4, P], F32R, ctx)
        probs = k.sb("f1_probs", [P, 2, S], F32, ctx)
        probsT = k.sb("f1_probsT", [P, RING, S], F32, ctx)
        mixT = k.sb("f1_mixT", [P, P], F32, ctx)
        negmax = k.sb("f1_negmax", [P, H16], F32, ctx)
        inv = k.sb("f1_inv", [P, H16], F32, ctx)
        outs = k.sb("f1_outs", [P, NT, D], F32, ctx)
        s = {n: k.sem(f"f1_{n}", ctx) for n in ("masked", "u_made", "u_read", "summed", "turned_high_made", "turned_split", "scored",
                                                "maxed", "exped", "transposed", "copied", "mixed", "mix_copied", "turned_back",
                                                "inverted", "normed", "bank_cleared")}
        MIX, MISC = k.bank[6], k.bank[7]
        vals2 = vals[:].rearrange("p t h d -> p (t h d)")
        batch_vals = k.sb("f1_batch_vals", [P, TB, H16, DH + 1], F32, ctx)
        k_keys = k_stack[:].rearrange("r j n -> r (j n)")
        q_flat = q_stack[:].rearrange("r j n -> r (j n)")
        outs_flat = outs[:].rearrange("p t d -> p (t d)")
        SLOT, MIXED = 8, 3
        LEAD = 4

        def heads_before(b, t, h):
            return b * HB + t * H16 + h

        def quads_before(b, t, j):
            return (b * TB + t) * QUADS + j

        def ahead(t, h):
            return h < H16 or not isinstance(t, int) or t < TB - 1

        with nc.Block() as block:
            @block.tensor
            def _(pe):
                def positions(b, t, j):
                    pe.wait_ge(s["masked"], quads_before(b, t, j) + 1)
                    pe.wait_ge(s["u_read"], quads_before(b, t, j) + 1)
                    q = q_head[:, 4 * (j % QUADS):4 * (j % QUADS) + 4, :]
                    nc.tensor.matmul(k.bank[0], w_stack[0][:, j % QUADS, :], q, start=True, stop=True)
                    nc.tensor.matmul(k.bank[1], w_stack[1][:, j % QUADS, :], q, start=True, stop=True).then_inc(s["u_made"], 1)

                def score(b, t, h):
                    j, i = h // 4, h % 4
                    if i == 0:
                        pe.wait_ge(s["turned_split"], quads_before(b, t, j) + 2)
                    pe.wait_ge(s["exped"], heads_before(b, t, h) + 1)
                    bank = k.bank[2 + h % 2]
                    nc.tensor.matmul(bank, q_head[:, h % H16, :], k_keys[:, bass.ds(j % QUADS * NTOK + b * S, S)], start=True, stop=False)
                    nc.tensor.matmul(bank, turned_high[:, j % 2, i, :], waves_high[:], start=False, stop=False)
                    nc.tensor.matmul(bank, turned_high[:, j % 2, i, :], waves_low[:], start=False, stop=False)
                    nc.tensor.matmul(bank, turned_low[:, j % 2, i, :], waves_high[:], start=False, stop=True).then_inc(s["scored"], 1)

                def turn(b, t, h):
                    pe.wait_ge(s["exped"], heads_before(b, t, h) + 1 + SCORES)
                    pe.wait_ge(s["copied"], heads_before(b, t, h) + 1)
                    for c in range(TB):
                        ins = nc.tensor.transpose(k.bank[4 + h % 2][:, ds(c)], probs[:, h % 2, ds(c)], k.ident[:])
                    ins.then_inc(s["transposed"], 1)

                def mix(b, t, j):
                    pe.wait_ge(s["copied"], heads_before(b, t, 4 * j + 3) + 1 + 2)
                    pe.wait_ge(s["mix_copied"], quads_before(b, t, j) + 1)
                    for c in range(TB):
                        for i in range(4):
                            h = 4 * j + i
                            ins = nc.tensor.matmul(MIX[32 * i:32 * i + DH + 1, 0:P], batch_vals[:, c, h, :], probsT[:, h % RING, ds(c)],
                                                   start=c == 0, stop=c == TB - 1)
                    ins.then_inc(s["mixed"], 1)

                def turn_back(b, t, j):
                    pe.wait_ge(s["mix_copied"], quads_before(b, t, j) + 2)
                    if j == 0:
                        pe.wait_ge(s["normed"], b * TB + t + 1)
                    nc.tensor.transpose(MISC[:, ds(j)], mixT[:], k.ident[:]).then_inc(s["turned_back"], 1)

                def first(b):
                    positions(b, 0, 0)
                    positions(b, 0, 1)
                    score(b, 0, 0)
                    score(b, 0, 1)
                    positions(b, 0, 2)

                def steps(b, t, start, end):
                    for h in range(start, end):
                        if ahead(t, h + 2):
                            score(b, t, h + 2)
                        turn(b, t, h)
                        if h % 4 == 1:
                            if h > 4:
                                mix(b, t, h // 4 - 1)
                        if h % 4 == 3:
                            if h >= 7:
                                turn_back(b, t, h // 4 - 1)
                            if ahead(t, h + 9):
                                positions(b, t, h // 4 + 3)

                def last(b):
                    mix(b, TB - 1, QUADS - 1)
                    turn_back(b, TB - 1, QUADS - 1)

                pe.wait_ge(s["bank_cleared"], 1)
                over_batches(pe, H16, LEAD, first, steps, last)

            @block.gpsimd
            def _(pool):
                def stacks(b, t, j):
                    nc.gpsimd.tensor_tensor(q_head[:, 4 * (j % QUADS):4 * (j % QUADS) + 4, :],
                                            q_flat[:, None, bass.ds(j % QUADS * NTOK + b * S + (t + j // QUADS) * P, P)].broadcast_to([R, 4, P]),
                                            own_rows[:, :, None].broadcast_to([R, 4, P]), ALU.mult).then_inc(s["masked"], 1)

                def cut(b, t, j):
                    pool.wait_ge(s["u_read"], quads_before(b, t, j) + 2)
                    pool.wait_ge(s["turned_split"], quads_before(b, t, j) + 1)
                    nc.gpsimd.tensor_tensor(turned[:], turn_cos[:], turn_sin[:], ALU.add).then_inc(s["summed"], 1)
                    pool.wait_ge(s["turned_high_made"], quads_before(b, t, j) + 1)
                    nc.gpsimd.tensor_tensor(turned_low[:, j % 2], turned[:], turned_high[:, j % 2].bitcast(F32),
                                            ALU.subtract).then_inc(s["turned_split"], 1)

                def first(b):
                    stacks(b, 0, 0)
                    stacks(b, 0, 1)
                    cut(b, 0, 0)
                    stacks(b, 0, 2)
                    cut(b, 0, 1)

                def steps(b, t, start, end):
                    for j in range(start // 4, end // 4):
                        if ahead(t, 4 * (j + 3)):
                            stacks(b, t, j + 3)
                        if ahead(t, 4 * (j + 2)):
                            cut(b, t, j + 2)

                free_at_first(pool, s["turned_split"])
                over_batches(pool, H16, 0, first, steps, lambda b: None)

            @block.scalar
            def _(act):
                def exp(b, t, h):
                    act.wait_ge(s["maxed"], heads_before(b, t, h) + 1)
                    nc.scalar.activation(probs[:, h % 2], k.bank[2 + h % 2], ACT.Exp, bias=negmax[:, h % H16:h % H16 + 1]).then_inc(s["exped"], 1)

                def mix_copy(b, t, j):
                    act.wait_ge(s["mixed"], quads_before(b, t, j) + MIXED)
                    act.wait_ge(s["turned_back"], quads_before(b, t, j) + 1)
                    nc.scalar.copy(mixT[:], MIX[:, 0:P]).then_inc(s["mix_copied"], 1)

                def first(b):
                    nc.scalar.copy(batch_vals[:].rearrange("p t h d -> p (t h d)"), vals2[:, ds(b, TB * W1)])
                    exp(b, 0, 0)

                def steps(b, t, start, end):
                    for h in range(start, end):
                        if ahead(t, h + 1):
                            exp(b, t, h + 1)
                        if h % 4 == 2 and h >= 6:
                            mix_copy(b, t, h // 4 - 1)
                        act.wait_ge(s["transposed"], heads_before(b, t, h) + 1)
                        if h % 4 == 0:
                            act.wait_ge(s["mixed"], quads_before(b, t, h // 4) + 1)
                        nc.scalar.copy(probsT[:, h % RING], k.bank[4 + h % 2]).then_inc(s["copied"], 1)

                free_at_first(act, s["exped"], s["copied"], by=SCORES)
                free_at_first(act, s["mix_copied"])
                free_at_first(act, s["mixed"], by=MIXED - 1)
                over_batches(act, H16, LEAD, first, steps, lambda b: mix_copy(b, TB - 1, QUADS - 1))

            @block.vector
            def _(dve):
                def rotate(b, t, j):
                    dve.wait_ge(s["u_made"], quads_before(b, t, j) + 1)
                    dve.wait_ge(s["summed"], quads_before(b, t, j) + 1)
                    start = (t + j // QUADS) * P
                    for bank, table, home in ((0, rot_cos, turn_cos), (1, rot_sin, turn_sin)):
                        ins = nc.vector.tensor_tensor(home[:], k.bank[bank].rearrange("p (h q) -> p h q", h=4),
                                                      table[:, None, bass.ds(start, P)].broadcast_to([P, 4, P]), ALU.mult)
                    ins.then_inc(s["u_read"], 1)

                def high(b, t, j):
                    dve.wait_ge(s["summed"], quads_before(b, t, j) + 2)
                    dve.wait_ge(s["scored"], heads_before(b, t, 4 * j) - 4 + SLOT)
                    nc.vector.tensor_copy(turned_high[:, j % 2], turned[:]).then_inc(s["turned_high_made"], 1)

                def norm(b, t):
                    T = b * TB + t
                    dve.wait_ge(s["turned_back"], quads_before(b, t, QUADS - 1) + 2)
                    mixed = MISC.rearrange("p (h d) -> p h d", h=H16)
                    nc.vector.reciprocal(inv[:], mixed[:, :, DH]).then_inc(s["inverted"], 1)
                    dve.wait_ge(s["inverted"], T + 1)
                    nc.vector.tensor_tensor(outs_flat[:, ds(T)].rearrange("p (h d) -> p h d", h=H16), mixed[:, :, 0:DH],
                                            inv[:, :, None].broadcast_to([P, H16, DH]), ALU.mult).then_inc(s["normed"], 1)

                def first(b):
                    rotate(b, 0, 0)
                    high(b, 0, 0)
                    rotate(b, 0, 1)

                def steps(b, t, start, end):
                    for h in range(start, end):
                        dve.wait_ge(s["scored"], heads_before(b, t, h) + 1 + SLOT)
                        nc.vector.tensor_reduce(negmax[:, h % H16:h % H16 + 1], k.bank[2 + h % 2], AX_X, ALU.max, negate=True).then_inc(s["maxed"], 1)
                        if h % 4 == 0 and ahead(t, h + 4):
                            high(b, t, h // 4 + 1)
                        if h % 4 == 2 and ahead(t, h + 6):
                            rotate(b, t, h // 4 + 2)
                        if h == H16 + 5:
                            norm(b, t)

                nc.vector.memset(MIX, 0.0).then_inc(s["bank_cleared"], 1)
                free_at_first(dve, s["normed"], s["u_read"], s["summed"], s["turned_back"])
                free_at_first(dve, s["scored"], by=SLOT)
                over_batches(dve, H16, LEAD + 2, first, steps, lambda b: norm(b, TB - 1))

        add_projection(k, ctx, "f1", outs, wo, src)


def relu_experts(k, src):
    nc = k.nc
    AHEAD = 4
    with Scope(k) as ctx:
        ln, sel, iota = homes = [load(k, ctx, n) for n in ("f1_ln2", "m1_sel", "iota32")]
        normalize(k, src, ln[:, 0:1], ln[:, 1:2], loads=(list(zip(("f1_ln2", "m1_sel", "iota32"), homes)), ctx))
        shape = [P, NT, E1]
        chance = k.sb("m1_chance", shape, F32, ctx)
        left = k.sb("m1_left", shape, F32, ctx)
        hit = k.sb("m1_hit", shape, F32, ctx)
        gate = k.sb("m1_gate", shape, F32, ctx)
        far = k.sb("m1_far", [P, E1], F32, ctx)
        best = k.sb("m1_best", [P, NT], F32, ctx)
        first = k.sb("m1_first", [P, NT], F32, ctx)
        n_high = k.sb("m1_n_high", [P, NTOK], F32R, ctx)
        n_low = k.sb("m1_n_low", [P, NTOK], F32R, ctx)
        order, made, ready, high_made = (k.sem(f"m1_{n}", ctx) for n in ("order", "sel_made", "sel_ready", "n_high_made"))
        with nc.Block() as block:
            @block.tensor
            def _(pe):
                for T in range(NT):
                    ins = nc.tensor.matmul(k.bank[0][:, ds(T, E1)], k.xT[:, ds(T)], sel[:], start=True, stop=True)
                ins.then_inc(made, 1)

            @block.scalar
            def _(act):
                act.wait_ge(made, 1)
                nc.scalar.activation(chance[:].rearrange("p t e -> p (t e)"), k.bank[0], ACT.Exp, scale=-1.0).then_inc(ready, 1)
                nc.scalar.copy(n_high[:], k.xT[:]).then_inc(high_made, 1)

            @block.vector
            def _(dve):
                step = Steps(dve, order)
                step.then(nc.vector.tensor_scalar(far[:], iota[:], 100.0, None, ALU.add))
                nc.vector.memset(gate[:], 0.0)
                dve.wait_ge(ready, 1)
                step.then(nc.vector.tensor_scalar(chance[:], chance[:], 1.0, None, ALU.add))
                step.then(nc.vector.reciprocal(chance[:], chance[:]))
                step.then(nc.vector.tensor_copy(left[:], chance[:]))
                dve.wait_ge(high_made, 1)
                nc.vector.tensor_tensor(n_low[:], k.xT[:], n_high[:].bitcast(F32), ALU.subtract)
                for _ in range(K1):
                    first_hit(nc, step, left, hit, best, first, iota[:], far, shape)
                    nc.vector.scalar_tensor_tensor(left[:], hit[:], -HUGE, left[:], ALU.mult, ALU.add)
                    step.then(nc.vector.tensor_tensor(hit[:], hit[:], chance[:], ALU.mult))
                    step.then(nc.vector.tensor_tensor(gate[:], gate[:], hit[:], ALU.add))

        w = k.sb("m1_weights", [P, 2, P + D], F32, ctx)
        keys_high = k.sb("m1_keys_high", [P, 2, P], F32R, ctx)
        keys_low = k.sb("m1_keys_low", [P, 2, P], F32R, ctx)
        one = k.sb("m1_one", [P, 1], F32, ctx)
        hT = k.sb("m1_hT", [P, B, S], F32, ctx)
        loaded = [k.sem(f"m1_loaded{u}", ctx) for u in range(2)]
        h_made, relued, y_made, y_read, keys_high_made, keys_cut = (
            k.sem(f"m1_{n}", ctx) for n in ("h_made", "relued", "y_made", "y_read", "keys_high_made", "keys_cut"))
        gate2 = gate[:].rearrange("p t e -> p (t e)")
        source = k.dram["m1_w"]
        with nc.Block() as block:
            @block.sync
            def _(sp):
                for u in range(2):
                    sp.dma_start(w[:, u, :], source[u]).then_inc(loaded[u], 16)
                with sp.Fori(0, E1 // 2 - 1) as turn:
                    for u in range(2):
                        e = turn * 2 + u
                        sp.wait_ge(y_made, e * B + B)
                        sp.dma_start(w[:, u, :], source[bass.ds(e + 2, 1)].rearrange("e p n -> (e p) n")).then_inc(loaded[u], 16)

            @block.tensor
            def _(pe):
                with pe.Fori(0, E1 // 2) as turn:
                    for u in range(2):
                        e = turn * 2 + u
                        pe.wait_ge(keys_cut, e + 2)

                        def hidden(c):
                            pe.wait_ge(relued, e * B + c + 1)
                            nc.tensor.matmul(k.bank[c], keys_high[:, u, :], n_high[:, ds(c, S)], start=True, stop=False)
                            nc.tensor.matmul(k.bank[c], keys_high[:, u, :], n_low[:, ds(c, S)], start=False, stop=False)
                            nc.tensor.matmul(k.bank[c], keys_low[:, u, :], n_high[:, ds(c, S)], start=False, stop=True).then_inc(h_made, 1)

                        def values(c):
                            pe.wait_ge(relued, e * B + c + 1 + AHEAD)
                            pe.wait_ge(y_read, e * B + c + 1)
                            for j in range(TB):
                                ins = nc.tensor.matmul(k.bank[4 + c][:, ds(j)], hT[:, c, ds(j)], w[:, u, P:P + D], start=True, stop=True)
                            ins.then_inc(y_made, 1)

                        hidden(0)
                        hidden(1)
                        for c in range(2, B):
                            hidden(c)
                            values(c - 2)
                        values(B - 2)
                        values(B - 1)

            @block.gpsimd
            def _(pool):
                nc.gpsimd.memset(one[:], 1.0).then_inc(keys_cut, 1)
                pool.wait_ge(keys_cut, 1)
                with pool.Fori(0, E1 // 2) as turn:
                    for u in range(2):
                        pool.wait_ge(loaded[u], turn * 16 + 16)
                        nc.gpsimd.tensor_tensor(keys_high[:, u, :], w[:, u, 0:P], one[:].broadcast_to([P, P]), ALU.mult).then_inc(keys_high_made, 1)
                        pool.wait_ge(keys_high_made, turn * 2 + u + 1)
                        nc.gpsimd.tensor_tensor(keys_low[:, u, :], w[:, u, 0:P], keys_high[:, u, :].bitcast(F32), ALU.subtract).then_inc(keys_cut, 1)

            @block.scalar
            def _(act):
                nc.scalar.copy(hT[:, 0, 0:1], k.ident[:, 0:1]).then_inc(relued, AHEAD)
                with act.Fori(0, E1) as e:
                    for c in range(B):
                        act.wait_ge(h_made, e * B + c + 1)
                        nc.scalar.activation(hT[:, c, :], k.bank[c], ACT.Relu).then_inc(relued, 1)

            @block.vector
            def _(dve):
                nc.vector.memset(best[:], 0.0).then_inc(y_read, AHEAD)
                with dve.Fori(0, E1) as e:
                    for c in range(B):
                        dve.wait_ge(y_made, e * B + c + 1)
                        for j in range(TB):
                            T = c * TB + j
                            ins = nc.vector.scalar_tensor_tensor(src[:, ds(T)], k.bank[4 + c][:, ds(j)], gate2[:, bass.ds(e + T * E1, 1)],
                                                                 src[:, ds(T)], ALU.mult, ALU.add)
                        ins.then_inc(y_read, 1)


def stage_0f(k):
    nc = k.nc
    with Scope(k) as ctx:
        xn = k.sb("m0_xn", [P, NT * D], F32, ctx)
        shared_names = ("s0_w1", "s0_w3", "s0_w2")
        shared_w = [load(k, ctx, n) for n in shared_names]
        route_names = ("m0_gate_w", "m0_gate_b", "iota16", "slot_base", "spare_slot", "before", "bits")
        route_w = [k.sb(n + "_in", [P, k.dram[n].shape[1]], k.dram[n].dtype, ctx) for n in route_names]
        normalize(k, k.x, rows=xn, loads=(list(zip(route_names + shared_names, route_w + shared_w)), ctx))
        slots = nc.dram_tensor("m0_slots", (SLOTS + K0 * NTOK, D), F32).ap()
        answers = nc.dram_tensor("m0_answers", (SLOTS, D), F32).ap()
        put = k.sb("m0_put", [P, K0, NT], I32, ctx)
        get = k.sb("m0_get", [P, K0, NT], I32, ctx)
        weight = k.sb("m0_weight", [P, K0, NT], F32, ctx)
        route(k, slots, put, get, weight, *route_w)
        scattered = k.sem("m0_scattered")
        gathered = [k.sem(f"m0_gathered{i}") for i in range(2)]
        order = k.sem("m0_add_order", ctx)
        answer = k.sb("m0_answer", [P, K0, NT, D], F32, ctx)

        def scatter(pool):
            for T in range(NT):
                for c in range(K0):
                    pool.indirect_dma_start(out=slots, out_offset=bass.IndirectOffsetOnAxis(ap=put[:, c, T:T + 1], axis=0),
                                            in_=xn[:, ds(T)], in_offset=None).then_inc(scattered, 16)
            pool.wait_ge(scattered, 16 * K0 * NT)

        def gather(pool):
            for T in range(NT):
                for c in range(K0):
                    pool.indirect_dma_start(out=answer[:, c, T, :], out_offset=None, in_=answers,
                                            in_offset=bass.IndirectOffsetOnAxis(ap=get[:, c, T:T + 1], axis=0)).then_inc(gathered[T // (NT // 2)], 16)
            for half in gathered:
                pool.wait_ge(half, 16 * K0 * NT // 2)

        def add_answers(dve):
            for c in range(K0):
                for i, half in enumerate(gathered):
                    dve.wait_ge(half, 16 * K0 * NT // 2)
                    if c > 0:
                        dve.wait_ge(order, i + 1)
                    for T in range(i * NT // 2, (i + 1) * NT // 2):
                        ins = nc.vector.scalar_tensor_tensor(k.x[:, ds(T)], answer[:, c, T, :], weight[:, c, T:T + 1], k.x[:, ds(T)],
                                                             ALU.mult, ALU.add)
                    ins.then_inc(order, 1)

        shared_experts(k, 0, *shared_w, scatter, lambda dve: None)
        routed_experts(k, slots, answers)
        shared_experts(k, 1, *shared_w, gather, add_answers)


def route(k, slots, put, get, weight, gate_w, gate_b, iota, base, spare, before, bits):
    nc = k.nc
    TE = [P, NT, E0]
    flat = lambda a: a[:].rearrange("p t e -> p (t e)")
    over_experts = lambda a: a[:, :, None].broadcast_to(TE)
    over_tiles = lambda a: a[:, None, :].broadcast_to(TE)
    with Scope(k) as ctx:
        zeros = k.sb("m0_zeros", [P, SLOTS], F32, ctx)
        emptied, zeroed = k.sem("m0_emptied", ctx), k.sem("m0_zeroed", ctx)
        t = {n: k.sb(f"m0_{n}", TE, F32, ctx) for n in ("logit", "work", "score", "hit1", "hit2", "member", "signed", "keep", "number", "tmp")}
        e = {n: k.sb(f"m0_{n}", [P, E0], F32, ctx) for n in ("far", "count", "positive", "sign", "want", "cut", "above")}
        best, first, sums = (k.sb(f"m0_{n}", [P, NT], F32, ctx) for n in ("best", "first", "sums"))
        threshold = k.sb("m0_threshold", [P, E0], I32, ctx)
        trial = k.sb("m0_trial", [P, E0], I32, ctx)
        enough = k.sb("m0_enough", [P, E0], F32, ctx)
        taken = k.sb("m0_taken_bit", [P, E0], I32, ctx)
        mark = k.sb("m0_mark", TE, BF16, ctx)
        marks = k.sb("m0_marks", [P, NT, 2, E0], BF16, ctx)
        offset = k.sb("m0_offset", [P, NT + 1, 2 * E0], F32, ctx)
        rank = k.sb("m0_rank", [P, NT, 2, E0], F32, ctx)
        ones = k.sb("m0_ones", [P, P], BF16, ctx)
        before16 = k.sb("m0_before16", [P, P], BF16, ctx)
        order, logits_made, shifted, exped, marked, counted, mark2, rank_made = (
            k.sem(f"m0_{n}", ctx) for n in ("order", "logits_made", "shifted", "exped", "marked", "counted", "marked2", "rank_made"))
        with nc.Block() as block:
            @block.sync
            def _(sp):
                sp.wait_ge(emptied, 1)
                sp.dma_start(slots[0:SLOTS, :].rearrange("(p s) d -> p (s d)", p=P), zeros[:]).then_inc(zeroed, 16)
                sp.wait_ge(zeroed, 16)

            @block.gpsimd
            def _(pool):
                nc.gpsimd.memset(zeros[:], 0.0).then_inc(emptied, 1)

            @block.scalar
            def _(act):
                act.wait_ge(shifted, 1)
                nc.scalar.activation(flat(t["score"]), flat(t["work"]), ACT.Exp).then_inc(exped, 1)

            @block.tensor
            def _(pe):
                for T in range(NT):
                    ins = nc.tensor.matmul(k.bank[0][:, ds(T, E0)], k.xT[:, ds(T)], gate_w[:], start=True, stop=True)
                ins.then_inc(logits_made, 1)
                pe.wait_ge(marked, 1)
                nc.tensor.matmul(k.bank[1][:, 0:NT * E0], ones[:], flat(mark), start=True, stop=True).then_inc(counted, 1)
                with pe.Fori(0, MAG_BITS) as i:
                    pe.wait_ge(marked, i + 2)
                    nc.tensor.matmul(k.bank[1][:, 0:NT * E0], ones[:], flat(mark), start=True, stop=True).then_inc(counted, 1)
                pe.wait_ge(mark2, 1)
                m = marks[:].rearrange("p t c e -> p (t c e)")
                nc.tensor.matmul(k.bank[2], ones[:], m, start=True, stop=True).then_inc(rank_made, 1)
                nc.tensor.matmul(k.bank[3], before16[:], m, start=True, stop=True).then_inc(rank_made, 1)

            @block.vector
            def _(dve):
                step = Steps(dve, order)
                then, v = step.then, nc.vector
                then(v.memset(ones[:], 1.0))
                then(v.tensor_copy(before16[:], before[:]))
                then(v.tensor_scalar(e["far"][:], iota[:], 100.0, None, ALU.add))
                dve.wait_ge(logits_made, 1)
                then(v.tensor_copy(flat(t["logit"]), k.bank[0][:, 0:NT * E0]))
                then(v.tensor_reduce(best[:], t["logit"][:], AX_X, ALU.max))
                v.tensor_tensor(t["work"][:], t["logit"][:], over_experts(best), ALU.subtract).then_inc(shifted, 1)
                dve.wait_ge(exped, 1)
                then(v.tensor_reduce(sums[:], t["score"][:], AX_X, ALU.add))
                then(v.reciprocal(sums[:], sums[:]))
                then(v.tensor_tensor(t["score"][:], t["score"][:], over_experts(sums), ALU.mult))
                then(v.tensor_tensor(t["score"][:], t["score"][:], over_tiles(gate_b), ALU.add))
                first_hit(nc, step, t["score"], t["hit1"], best, first, iota[:], e["far"], TE)
                then(v.scalar_tensor_tensor(t["score"][:], t["hit1"][:], -HUGE, t["score"][:], ALU.mult, ALU.add))
                first_hit(nc, step, t["score"], t["hit2"], best, first, iota[:], e["far"], TE)
                then(v.tensor_tensor(t["member"][:], t["hit1"][:], t["hit2"][:], ALU.add))
                then(v.tensor_scalar(t["tmp"][:], t["member"][:], HUGE, HUGE, ALU.mult, ALU.subtract))
                then(v.tensor_tensor(t["work"][:], t["logit"][:], t["member"][:], ALU.mult))
                then(v.tensor_tensor(t["work"][:], t["work"][:], t["tmp"][:], ALU.add))

                def count(n):
                    dve.wait_ge(counted, n)
                    then(v.tensor_reduce(e["count"][:], k.bank[1][:, 0:NT * E0].rearrange("p (t e) -> p e t", e=E0), AX_X, ALU.add))

                v.tensor_scalar(mark[:], t["work"][:], 0.0, None, ALU.is_ge).then_inc(marked, 1)
                count(1)
                then(v.tensor_scalar(e["positive"][:], e["count"][:], float(CAP), None, ALU.is_ge))
                v.tensor_scalar(e["sign"][:], e["positive"][:], 2.0, -1.0, ALU.mult, ALU.add)
                v.memset(threshold[:], 0)
                then(v.tensor_scalar(e["want"][:], e["positive"][:], float(2 * CAP - NTOK - 1), float(NTOK - CAP + 1), ALU.mult, ALU.add))
                then(v.tensor_tensor(t["signed"][:], t["work"][:], over_tiles(e["sign"]), ALU.mult))
                with dve.Fori(0, MAG_BITS) as i:
                    step.turn(i, 5)
                    then(v.tensor_tensor(trial[:], threshold[:], bits[:, ds(i, E0)], ALU.bitwise_or))
                    v.tensor_tensor(mark[:], t["signed"][:], over_tiles(trial[:].bitcast(F32)), ALU.is_ge).then_inc(marked, 1)
                    count(i + 2)
                    then(v.tensor_tensor(enough[:], e["count"][:], e["want"][:], ALU.is_ge))
                    then(v.tensor_tensor(taken[:], enough[:], bits[:, ds(i, E0)], ALU.mult))
                    then(v.tensor_tensor(threshold[:], threshold[:], taken[:], ALU.bitwise_or))
                step.turns_end(MAG_BITS)
                then(v.tensor_tensor(e["cut"][:], threshold[:].bitcast(F32), e["sign"][:], ALU.mult))
                then(v.tensor_tensor(t["tmp"][:], t["work"][:], over_tiles(e["cut"]), ALU.is_equal))
                then(v.tensor_tensor(t["tmp"][:], t["tmp"][:], t["member"][:], ALU.mult))
                v.tensor_copy(marks[:, :, 1, :], t["tmp"][:])
                then(v.tensor_tensor(t["keep"][:], t["work"][:], over_tiles(e["cut"]), ALU.is_gt))
                v.tensor_copy(marks[:, :, 0, :], t["keep"][:]).then_inc(mark2, 1)
                v.memset(offset[:, 0, :], 0.0)
                dve.wait_ge(rank_made, 2)
                totals = k.bank[2].rearrange("p (t c) -> p t c", t=NT)
                for T in range(NT):
                    if T == 0:
                        then(v.tensor_copy(offset[:, 1, :], totals[:, 0, :]))
                    else:
                        then(v.tensor_tensor(offset[:, T + 1, :], totals[:, T, :], offset[:, T, :], ALU.add))
                then(v.tensor_tensor(rank[:].rearrange("p t c e -> p t (c e)"), k.bank[3].rearrange("p (t c) -> p t c", t=NT),
                                     offset[:, 0:NT, :], ALU.add))
                above = offset[:, NT, 0:E0]
                then(v.tensor_tensor(rank[:, :, 1, :], rank[:, :, 1, :], above[:, None, :].broadcast_to(TE), ALU.add))
                then(v.scalar_tensor_tensor(t["tmp"][:], rank[:, :, 1, :], float(CAP), t["tmp"][:], ALU.is_lt, ALU.mult))
                then(v.tensor_tensor(t["number"][:], t["tmp"][:], rank[:, :, 1, :], ALU.mult))
                then(v.tensor_tensor(t["signed"][:], t["keep"][:], rank[:, :, 0, :], ALU.mult))
                then(v.tensor_tensor(t["number"][:], t["number"][:], t["signed"][:], ALU.add))
                then(v.tensor_tensor(t["number"][:], t["number"][:], over_tiles(base), ALU.add))
                then(v.tensor_tensor(t["keep"][:], t["keep"][:], t["tmp"][:], ALU.add))
                for c, hit in enumerate((t["hit1"], t["hit2"])):
                    then(v.tensor_tensor(hit[:], hit[:], t["keep"][:], ALU.mult))
                    then(v.tensor_tensor(t["tmp"][:], hit[:], t["number"][:], ALU.mult))
                    then(v.tensor_reduce(best[:], t["tmp"][:], AX_X, ALU.add))
                    then(v.tensor_copy(get[:, c, :], best[:]))
                    then(v.tensor_tensor(t["tmp"][:], hit[:], t["logit"][:], ALU.mult))
                    then(v.tensor_reduce(weight[:, c, :], t["tmp"][:], AX_X, ALU.add))
                    then(v.tensor_reduce(first[:], hit[:], AX_X, ALU.add))
                    then(v.tensor_scalar(first[:], first[:], -1.0, 1.0, ALU.mult, ALU.add))
                    then(v.scalar_tensor_tensor(first[:], spare[:], float(c * NTOK), first[:], ALU.add, ALU.mult))
                    then(v.tensor_tensor(best[:], best[:], first[:], ALU.add))
                    then(v.tensor_copy(put[:, c, :], best[:]))


def shared_experts(k, part, w1, w3, w2, move, then):
    nc = k.nc
    HB = S0 * HID0 // P
    N = B // 2
    with Scope(k) as ctx:
        silu = k.sb(f"s{part}_silu", [P, 2, S], F32, ctx)
        hidden = k.sb(f"s{part}_hidden", [P, HB, S], F32, ctx)
        made, silued, gated, summed, added = (
            k.sem(f"s{part}_{n}", ctx) for n in ("made", "silued", "gated", "summed", "added"))
        with nc.Block() as block:
            @block.gpsimd
            def _(pool):
                move(pool)

            @block.tensor
            def _(pe):
                with pe.Fori(0, N) as b:
                    for n in range(HB):
                        pe.wait_ge(gated, b * HB + n + 1)
                        nc.tensor.matmul(k.bank[n % 2], w1[:, ds(n)], k.xT[:, ds(part * N + b, S)], start=True, stop=True)
                        nc.tensor.matmul(k.bank[2 + n % 2], w3[:, ds(n)], k.xT[:, ds(part * N + b, S)], start=True, stop=True).then_inc(made, 1)
                    pe.wait_ge(gated, b * HB + HB + 2)
                    pe.wait_ge(added, b + 1)
                    for j in range(TB):
                        for n in range(HB):
                            ins = nc.tensor.matmul(k.bank[4][:, ds(j)], hidden[:, n, ds(j)], w2[:, ds(n)], start=n == 0, stop=n == HB - 1)
                    ins.then_inc(summed, 1)

            @block.scalar
            def _(act):
                nc.scalar.copy(silu[:, 0, 0:1], k.ident[:, 0:1]).then_inc(gated, 2)
                with act.Fori(0, N) as b:
                    for n in range(HB):
                        act.wait_ge(made, b * HB + n + 1)
                        nc.scalar.activation(silu[:, n % 2, :], k.bank[n % 2], ACT.Silu).then_inc(silued, 1)

            @block.vector
            def _(dve):
                free_at_first(dve, added)
                with dve.Fori(0, N) as b:
                    for n in range(HB):
                        dve.wait_ge(silued, b * HB + n + 1)
                        nc.vector.tensor_tensor(hidden[:, n, :], k.bank[2 + n % 2], silu[:, n % 2, :], ALU.mult).then_inc(gated, 1)
                    dve.wait_ge(summed, b + 1)
                    nc.vector.scalar_tensor_tensor(k.x[:, ds(part * N + b, S)], k.bank[4], 1.0 / S0, k.x[:, ds(part * N + b, S)], ALU.mult, ALU.add).then_inc(added, 1)
                dve.wait_ge(added, N + 1)
                then(dve)


def routed_experts(k, slots, answers):
    nc = k.nc
    HB = HID0 // P
    RING = 4
    cuts = [(at, min(P, CAP - at)) for at in range(0, CAP, P)]
    with Scope(k) as ctx:
        w13 = k.sb("m0_w13", [P, RING, 2 * HID0], F32, ctx)
        w2 = k.sb("m0_w2", [P, RING, HB * D], F32, ctx)
        rows = k.sb("m0_rows", [P, RING, len(cuts), D], F32, ctx)
        rowsT = k.sb("m0_rowsT", [P, 2, CAP], F32, ctx)
        silu = k.sb("m0_silu", [P, HB, CAP], F32, ctx)
        hidden = k.sb("m0_hidden", [P, 2, HB, CAP], F32, ctx)
        result = k.sb("m0_result", [P, RING, len(cuts), D], F32, ctx)
        loaded = [k.sem(f"m0_loaded{u}", ctx) for u in range(RING)]
        stored = [k.sem(f"m0_stored{u}", ctx) for u in range(RING)]
        turned, copied, made, silued, gated, summed, taken = (k.sem(f"m0_{n}", ctx) for n in ("turned", "copied", "made", "silued", "gated", "summed", "taken"))
        PARTS = 2 + len(cuts)
        with nc.Block() as block:
            def load_expert(eng, u, e):
                one = lambda a: a[bass.ds(e, 1)].rearrange("e p n -> (e p) n") if not isinstance(e, int) else a[e]
                eng.dma_start(w13[:, u, :], one(k.dram["m0_w13"])).then_inc(loaded[u], 16)
                eng.dma_start(w2[:, u, :], one(k.dram["m0_w2"])).then_inc(loaded[u], 16)
                for i, (at, n) in enumerate(cuts):
                    eng.dma_start(rows[0:n, u, i, :], slots[bass.ds(e * CAP + at, n), :]).then_inc(loaded[u], 16)

            @block.sync
            def _(sp):
                for u in range(RING):
                    load_expert(sp, u, u)

                def store(u, e):
                    sp.wait_ge(taken, e + 2)
                    for i, (at, n) in enumerate(cuts):
                        sp.dma_start(answers[bass.ds(e * CAP + at, n), :], result[0:n, u, i, :]).then_inc(stored[u], 16)

                free_at_first(sp, *stored, by=16)
                with sp.Fori(0, E0 // RING - 1) as turn:
                    for u in range(RING):
                        sp.wait_ge(summed, turn * RING + u + 1)
                        load_expert(sp, u, turn * RING + u + RING)
                        store(u, turn * RING + u)
                for u in range(RING):
                    store(u, E0 - RING + u)
                for u in range(RING):
                    sp.wait_ge(stored[u], 16 * len(cuts) * E0 // RING + 16)

            @block.scalar
            def _(act):
                def before(u, e):
                    act.wait_ge(turned, e + 1)
                    nc.scalar.copy(rowsT[:, u % 2, :], k.bank[6 + u % 2][:, 0:CAP]).then_inc(copied, 1)
                    for n in range(HB):
                        act.wait_ge(made, e * HB + n + 1)
                        nc.scalar.activation(silu[:, n, :], k.bank[1 + n][:, 0:CAP], ACT.Silu).then_inc(silued, 1)

                free_at_first(act, gated, by=HB)
                with act.Fori(0, E0 // RING) as turn:
                    for u in range(RING):
                        before(u, turn * RING + u)

            @block.vector
            def _(dve):
                free_at_first(dve, taken)
                with dve.Fori(0, E0 // RING) as turn:
                    for u in range(RING):
                        e = turn * RING + u
                        for n in range(HB):
                            dve.wait_ge(silued, e * HB + n + 1)
                            nc.vector.tensor_tensor(hidden[:, u % 2, n, :], k.bank[3 + n][:, 0:CAP], silu[:, n, :], ALU.mult).then_inc(gated, 1)
                        dve.wait_ge(summed, e + 1)
                        dve.wait_ge(stored[u], turn * (16 * len(cuts)) + 16)
                        for i, (at, n) in enumerate(cuts):
                            ins = nc.vector.tensor_copy(result[0:n, u, i, :], k.bank[5][0:n, ds(i)])
                        ins.then_inc(taken, 1)

            @block.tensor
            def _(pe):
                def turn_rows(turn, u, e):
                    pe.wait_ge(loaded[u], turn * (16 * PARTS) + 16 * PARTS)
                    for i, (at, n) in enumerate(cuts):
                        ins = nc.tensor.transpose(k.bank[6 + u % 2][:, at:at + n], rows[0:n, u, i, :], k.ident[0:n, 0:n])
                    ins.then_inc(turned, 1)

                def up(u, e):
                    pe.wait_ge(copied, e + 1)
                    for n in range(HB):
                        pe.wait_ge(gated, e * HB + n + 1)
                        nc.tensor.matmul(k.bank[1 + n][:, 0:CAP], w13[:, u, ds(n)], rowsT[:, u % 2, :], start=True, stop=True)
                        nc.tensor.matmul(k.bank[3 + n][:, 0:CAP], w13[:, u, ds(HB + n)], rowsT[:, u % 2, :], start=True, stop=True).then_inc(made, 1)

                def down(u, e):
                    pe.wait_ge(gated, e * HB + 2 * HB)
                    pe.wait_ge(taken, e + 1)
                    for i, (at, m) in enumerate(cuts):
                        for n in range(HB):
                            ins = nc.tensor.matmul(k.bank[5][0:m, ds(i)], hidden[:, u % 2, n, at:at + m], w2[:, u, ds(n)], start=n == 0, stop=n == HB - 1)
                    ins.then_inc(summed, 1)

                turn_rows(0, 0, 0)
                up(0, 0)
                with pe.Fori(0, E0 // RING - 1) as turn:
                    for u in range(RING):
                        v = (u + 1) % RING
                        e = turn * RING + u
                        turn_rows(turn + (u + 1) // RING, v, e + 1)
                        up(v, e + 1)
                        down(u, e)
                for u in range(RING):
                    e = E0 - RING + u
                    if u + 1 < RING:
                        turn_rows(E0 // RING - 1, u + 1, e + 1)
                        up(u + 1, e + 1)
                    down(u, e)


def stage_3f(k):
    nc = k.nc
    NB = HID3 // P
    with Scope(k) as ctx:
        fc, proj, uT, v, bT, gate = homes = [load(k, ctx, n, k.dram[n].shape[0])
                                             for n in ("f3_fc", "f3_proj", "f3_uT", "f3_v", "f3_bT", "f3_gate")]
        normalize(k, k.x, loads=(list(zip(("f3_fc", "f3_proj", "f3_uT", "f3_v", "f3_bT", "f3_gate"), homes)), ctx))
        rank = v.shape[0]
        scale = k.sb("f3_scale", [P, 2, NB], F32, ctx)
        half = k.sb("f3_half", [P, 2, 2, NB], F32, ctx)
        below = k.sb("f3_below", [P, 2, HID3], F32, ctx)
        fv = k.sb("f3_fv", [rank, D], F32, ctx)
        fcT = k.sb("f3_fcT", [P, HID3], F32, ctx)
        projT = k.sb("f3_projT", [P, HID3], F32, ctx)
        order, ready, made, taken = (k.sem(f"f3_{n}", ctx) for n in ("order", "ready", "made", "taken"))
        with nc.Block() as block:
            @block.vector
            def _(dve):
                step = Steps(dve, order)
                step.then(nc.vector.tensor_reduce(scale[:, 0, :], fc[:].rearrange("p (b d) -> p b d", d=D), AX_X, ALU.add,
                                                  apply_absolute_value=True))
                nc.vector.tensor_reduce(scale[:, 1, 0:1], proj[:], AX_X, ALU.add, apply_absolute_value=True)
                step.then(nc.vector.memset(scale[:, 1, 1:NB], 1.0))
                nc.vector.tensor_scalar(scale[:, 0, :], scale[:, 0, :], 1.0 / D, 1e-5, ALU.mult, ALU.max)
                step.then(nc.vector.tensor_scalar(scale[:, 1, :], scale[:, 1, :], 1.0 / HID3, 1e-5, ALU.mult, ALU.max))
                nc.vector.tensor_scalar(half[:, 0], scale[:], 0.5, None, ALU.mult)
                step.then(nc.vector.tensor_scalar(half[:, 1], scale[:], -0.5, None, ALU.mult))
                blocks = [(0, fc, n, slice(n * P, (n + 1) * P), slice(n * P, (n + 1) * P)) for n in range(NB)]
                blocks += [(1, proj, 0, slice(0, HID3), slice(0, HID3))]
                for m, w, n, cols, _ in blocks:
                    ins = nc.vector.tensor_scalar(below[:, m, cols], w[:, cols], half[:, 1, m, n:n + 1], None, ALU.is_lt)
                step.then(ins)
                for m, w, n, cols, _ in blocks:
                    ins = nc.vector.scalar_tensor_tensor(below[:, m, cols], w[:, cols], half[:, 0, m, n:n + 1], below[:, m, cols],
                                                         ALU.is_gt, ALU.subtract)
                step.then(ins)
                for m, w in ((0, fc), (1, proj)):
                    ins = nc.vector.tensor_tensor(below[:, m, :], below[:, m, :], w[:], ALU.subtract)
                step.then(ins)
                for m, w in ((0, fc), (1, proj)):
                    ins = nc.vector.tensor_tensor(below[:, m, :], below[:, m, :], w[:], ALU.add)
                step.then(ins)
                for m, w, n, cols, _ in blocks:
                    ins = nc.vector.tensor_scalar(w[:, cols], below[:, m, cols], scale[:, m, n:n + 1], None, ALU.mult)
                ins.then_inc(ready, 1)
                dve.wait_ge(made, 1)
                nc.vector.tensor_copy(fv[:], k.bank[1][0:rank, 0:D]).then_inc(taken, 1)
                dve.wait_ge(made, 3)
                step.then(nc.vector.tensor_copy(fcT[:], k.bank[2]))
                nc.vector.tensor_copy(projT[:], k.bank[3])
                dve.wait_ge(made, 4)
                nc.vector.scalar_tensor_tensor(fcT[:], k.bank[4], gate[:, 0:1], fcT[:], ALU.mult, ALU.add).then_inc(taken, 1)

            @block.tensor
            def _(pe):
                nc.tensor.matmul(k.bank[1][0:rank, 0:D], bT[:], v[:], start=True, stop=True).then_inc(made, 1)
                pe.wait_ge(ready, 1)
                for w, bank in ((fc, 2), (proj, 3)):
                    for n in range(NB):
                        ins = nc.tensor.transpose(k.bank[bank][:, ds(n)], w[:, ds(n)], k.ident[:])
                    ins.then_inc(made, 1)
                pe.wait_ge(taken, 1)
                nc.tensor.matmul(k.bank[4], fv[:], uT[:], start=True, stop=True).then_inc(made, 1)
        r = k.sb("f3_r", [P, NB, S], F32, ctx)
        sq = k.sb("f3_sq", [P, NB, S], F32, ctx)
        hidden, relued, squared, out_made, added = (k.sem(f"f3_{n}", ctx) for n in ("hidden", "relued", "squared", "out_made", "added"))
        with nc.Block() as block:
            @block.tensor
            def _(pe):
                with pe.Fori(0, B) as b:
                    for n in range(NB):
                        pe.wait_ge(relued, b * NB + 1)
                        nc.tensor.matmul(k.bank[n], fcT[:, ds(n)], k.xT[:, ds(b, S)], start=True, stop=True).then_inc(hidden, 1)
                    pe.wait_ge(squared, b * NB + NB + 1)
                    pe.wait_ge(added, b + 1)
                    for j in range(TB):
                        for n in range(NB):
                            ins = nc.tensor.matmul(k.bank[4][:, ds(j)], sq[:, n, ds(j)], projT[:, ds(n)], start=n == 0, stop=n == NB - 1)
                    ins.then_inc(out_made, 1)

            @block.scalar
            def _(act):
                free_at_first(act, relued)
                with act.Fori(0, B) as b:
                    for n in range(NB):
                        act.wait_ge(hidden, b * NB + n + 1)
                        act.wait_ge(squared, b * NB + 1)
                        nc.scalar.activation(r[:, n, :], k.bank[n], ACT.Relu).then_inc(relued, 1)

            @block.vector
            def _(dve):
                free_at_first(dve, squared, added)
                with dve.Fori(0, B) as b:
                    for n in range(NB):
                        dve.wait_ge(relued, b * NB + n + 2)
                        nc.vector.tensor_tensor(sq[:, n, :], r[:, n, :], r[:, n, :], ALU.mult).then_inc(squared, 1)
                    dve.wait_ge(out_made, b + 1)
                    nc.vector.tensor_tensor(k.x[:, ds(b, S)], k.bank[4], k.x[:, ds(b, S)], ALU.add).then_inc(added, 1)


def stage_lora(k):
    nc = k.nc
    with Scope(k) as ctx:
        names = ("lora_wT", "lora_b", "lora_downT", "lora_down_aux", "lora_upT", "lora_up_auxT")
        w, b, downT, down_aux, upT, up_auxT = (load(k, ctx, n, k.dram[n].shape[0]) for n in names)
        normalize(k, k.x, loads=(list(zip(names, (w, b, downT, down_aux, upT, up_auxT))), ctx))
        rank, mid = upT.shape[0], upT.shape[1]
        a = k.sb("lora_a", [rank, D], F32, ctx)
        c = k.sb("lora_c", [mid, D], F32, ctx)
        w_all = k.sb("lora_w_all", [P, D], F32, ctx)
        made = k.sem("lora_made", ctx)
        taken = k.sem("lora_taken", ctx)
        with nc.Block() as block:
            @block.tensor
            def _(pe):
                nc.tensor.matmul(k.bank[1][0:rank, 0:D], downT[:], down_aux[:], start=True, stop=True).then_inc(made, 1)
                pe.wait_ge(taken, 1)
                nc.tensor.matmul(k.bank[2][0:mid, 0:D], upT[:], a[:], start=True, stop=True).then_inc(made, 1)
                pe.wait_ge(taken, 2)
                nc.tensor.matmul(k.bank[3][:, 0:D], c[:], up_auxT[:], start=True, stop=True).then_inc(made, 1)

            @block.vector
            def _(dve):
                dve.wait_ge(made, 1)
                nc.vector.tensor_copy(a[:], k.bank[1][0:rank, 0:D]).then_inc(taken, 1)
                dve.wait_ge(made, 2)
                nc.vector.tensor_copy(c[:], k.bank[2][0:mid, 0:D]).then_inc(taken, 1)
                dve.wait_ge(made, 3)
                nc.vector.tensor_tensor(w_all[:], k.bank[3][:, 0:D], w[:], ALU.add).then_inc(taken, 1)
        multiplied = k.sem("lora_multiplied", ctx)
        added = k.sem("lora_added", ctx)
        with nc.Block() as block:
            @block.tensor
            def _(pe):
                for T in range(NT):
                    if T % TB == 0 and T >= 2 * TB:
                        pe.wait_ge(added, T // TB - 1)
                    ins = nc.tensor.matmul(k.bank[T // TB % 2][:, ds(T % TB)], k.xT[:, ds(T)], w_all[:],
                                           start=True, stop=True)
                    if T % TB == TB - 1:
                        ins.then_inc(multiplied, 1)

            @block.vector
            def _(dve):
                order = Steps(dve, k.sem("lora_order", ctx))
                x = k.x[:].rearrange("p (t d) -> p t d", d=D)
                for b4 in range(B):
                    part = x[:, b4 * TB:(b4 + 1) * TB, :]
                    order.then(nc.vector.tensor_tensor(part, part, b[:, None, :].broadcast_to([P, TB, D]), ALU.add))
                    dve.wait_ge(multiplied, b4 + 1)
                    nc.vector.tensor_tensor(part, k.bank[b4 % 2].rearrange("p (t d) -> p t d", d=D), part,
                                            ALU.add).then_inc(added, 1)


def cross_attention(k, name, heads, mask, mask_kind, scale, biased, weighted, project):
    nc = k.nc
    dh = D // heads
    KW = P + 32
    HG = min(heads, 4)
    NG = heads // HG
    NB = TB * NG
    PER_BANK = min(HG, 2)
    BANKS = HG // PER_BANK
    CH = -(-HG * KW // P)
    J = KW // CH
    CR = HG * J
    GW = HG * (dh + 1)
    AHEAD = 2
    mask_tiles = k.dram[mask].shape[1] // SC
    centre_here = lambda g: not weighted and g % 2 == 0
    with Scope(k) as ctx:
        wq, wk, wv, bv = (load(k, ctx, f"{name}_{w}") for w in ("wq", "wk", "wv", "bv"))
        pairs = [(f"{name}_wq", wq), (f"{name}_wk", wk), (f"{name}_wv", wv), (f"{name}_bv", bv)]
        if biased:
            bq, bk = load(k, ctx, f"{name}_bq"), load(k, ctx, f"{name}_bk")
            pairs += [(f"{name}_bq", bq), (f"{name}_bk", bk)]
        if project:
            wo, bo = load(k, ctx, f"{name}_wo"), load(k, ctx, f"{name}_bo")
            pairs += [(f"{name}_wo", wo), (f"{name}_bo", bo)]
        mask_raw = k.sb(f"{name}_mask_raw", [P, mask_tiles * SC], k.dram[mask].dtype, ctx)
        mask_rows = mask_raw[:].rearrange("p (t s) -> p t s", s=SC)
        added = k.sb(f"{name}_mask", [P, mask_tiles, PER_BANK, KW], F32, ctx)
        prob = k.sb(f"{name}_prob", [P, NT * SC], F32, ctx) if weighted else None
        pairs += [(mask, mask_raw)] + ([("prob", prob)] if weighted else [])
        normalize(k, k.x, loads=(pairs, ctx))

        q_all = k.sb(f"{name}_q_all", [P, NTOK], F32, ctx)
        kT = k.sb(f"{name}_kT", [P, B, KW], F32, ctx)
        keys = k.sb(f"{name}_keys", [P, B, heads, KW], F32, ctx) if heads > 1 else kT[:].rearrange("p b (h s) -> p b h s", h=1)
        vals = k.sb(f"{name}_vals", [P, B, CH, heads, dh + 1], F32, ctx)
        rows_of = k.sb(f"{name}_rows_of", [P, heads, dh + 1], F32, ctx)
        spread = k.sb(f"{name}_spread", [P, 2, CH, CR], F32, ctx)
        raw = k.sb(f"{name}_raw_vals", [P, CH, heads, dh + 1], F32, ctx)
        k_made, k_taken, q_made, spread_made, v_made, v_taken, order = (
            k.sem(f"{name}_{n}", ctx) for n in ("k_made", "k_taken", "q_all_made", "spread_made", "v_made", "v_taken", "kv_order"))
        zeroed = k.sem(f"{name}_zeroed", ctx)
        HALF = B * SC // 2
        by_head = lambda a, n: a.rearrange("p (h d) -> p h d", h=n)
        with nc.Block() as block:
            @block.tensor
            def _(pe):
                for i in range(2):
                    nc.tensor.matmul(k.bank[i][:, 0:HALF], wk[:], k.ctxT[:, ds(i, HALF)], start=True,
                                     stop=True).then_inc(k_made, 1)
                for b in range(B):
                    pe.wait_ge(spread_made, b + 1)
                    if b > 0:
                        pe.wait_ge(v_taken, b)
                    for c in range(CH):
                        ins = nc.tensor.matmul(k.bank[2 + c // (CH - 1)][0:CR, ds(c % (CH - 1))], spread[:, b % 2, c, :], wv[:],
                                               start=True, stop=True)
                    ins.then_inc(v_made, 1)
                    nc.tensor.matmul(k.bank[4 + b], wq[:], k.xT[:, ds(b, S)], start=True, stop=True).then_inc(q_made, 1)

            @block.scalar
            def _(act):
                def spread_out(b):
                    whole = SC // CH
                    rest = SC - whole * CH
                    home = spread[:, b % 2].rearrange("p c (i j) -> p c i j", i=HG)
                    tokens = k.ctxT[:, bass.ds(b * SC, whole * CH)].rearrange("p (j c) -> p c j", c=CH)
                    for c in range(CH):
                        ins = nc.scalar.copy(home[:, c, :, 0:whole], tokens[:, c, None, :].broadcast_to([P, HG, whole]))
                        if c < rest:
                            one = k.ctxT[:, bass.ds(b * SC + whole * CH + c, 1)]
                            ins = nc.scalar.copy(home[:, c, :, whole:whole + 1], one[:, None, :].broadcast_to([P, HG, 1]))
                    ins.then_inc(spread_made, 1)

                act.wait_ge(zeroed, 1)
                spread_out(0)
                spread_out(1)
                for b in range(B):
                    if b + 2 < B:
                        act.wait_ge(v_made, b + 1)
                        spread_out(b + 2)
                    act.wait_ge(q_made, b + 1)
                    if biased:
                        nc.scalar.activation(q_all[:, ds(b, S)], k.bank[4 + b], ACT.Identity, bias=bq[:, 0:1])
                    else:
                        nc.scalar.copy(q_all[:, ds(b, S)], k.bank[4 + b])

            @block.vector
            def _(dve):
                step = Steps(dve, order)
                nc.vector.memset(spread[:], 0.0).then_inc(zeroed, 1)
                nc.vector.memset(raw[:], 1.0)
                step.then(nc.vector.memset(rows_of[:], 0.0))
                for i in range(HG):
                    own = rows_of[:].rearrange("p (g i) d -> p g i d", i=HG)[i * J:i * J + J, :, i, :]
                    nc.vector.memset(own, 1.0)
                nc.vector.memset(added[:], -HUGE)
                step.then(nc.vector.memset(kT[:, :, SC:KW], 0.0))
                for i in range(2):
                    dve.wait_ge(k_made, i + 1)
                    home = kT[:, 2 * i:2 * i + 2, 0:SC]
                    got = k.bank[i][:, 0:HALF].rearrange("p (b s) -> p b s", b=2)
                    if biased:
                        ins = nc.vector.tensor_scalar(home, got, bk[:, 0:1], None, ALU.add)
                    else:
                        ins = nc.vector.tensor_copy(home, got)
                    ins.then_inc(k_taken, 1)
                for b in range(B):
                    dve.wait_ge(v_made, b + 1)
                    for bank, c, n in ((2, 0, CH - 1), (3, CH - 1, 1)):
                        for c in range(c, c + n):
                            ins = nc.vector.tensor_tensor(raw[0:CR, c, :, 0:dh], by_head(k.bank[bank][0:CR, ds(c % (CH - 1))], heads),
                                                          by_head(bv[0:CR, :], heads), ALU.add)
                    ins.then_inc(v_taken, 1)
                    dve.wait_ge(v_taken, b + 1)
                    step.then(nc.vector.tensor_tensor(vals[0:CR, b], raw[0:CR], rows_of[0:CR, None].broadcast_to([CR, CH, heads, dh + 1]), ALU.mult))
                for i in range(PER_BANK):
                    home = added[:, :, i, 0:SC]
                    if mask_kind == "int":
                        nc.vector.tensor_scalar(home, mask_rows, 1.0, 1e9, ALU.subtract, ALU.mult)
                    elif mask_kind == "where":
                        nc.vector.tensor_scalar(home, mask_rows, 0.0, -HUGE, ALU.is_equal, ALU.mult)
                    else:
                        nc.vector.tensor_copy(home, mask_rows)
                if project:
                    x = k.x[:].rearrange("p (t d) -> p t d", d=D)
                    nc.vector.tensor_tensor(x, x, bo[:, None, :].broadcast_to([P, NT, D]), ALU.add)

            if heads > 1:
                @block.gpsimd
                def _(pool):
                    for b in range(B):
                        pool.wait_ge(k_taken, b // 2 + 1)
                        nc.gpsimd.tensor_tensor(
                            keys[:, b, :, :], kT[:, b, None, :].broadcast_to([P, heads, KW]),
                            k.headmask[:, :, None].broadcast_to([P, heads, KW]), ALU.mult)

        RING = 4
        qT = k.sb(f"{name}_qT", [P, S], F32, ctx)
        probs = k.sb(f"{name}_probs", [P, RING, HG * KW], F32, ctx)
        used = k.sb(f"{name}_weighted", [P, RING, HG * KW], F32, ctx) if weighted else probs
        probsT = k.sb(f"{name}_probsT", [P, 2, CH, P], F32, ctx)
        negmax = k.sb(f"{name}_negmax", [P, 2, heads], F32, ctx)
        sums = k.sb(f"{name}_sums", [P, 2, heads], F32, ctx)
        inv = k.sb(f"{name}_inv", [P, heads], F32, ctx)
        if project:
            outs = k.sb(f"{name}_outs", [P, NT, D], F32, ctx)
            outs_flat = outs[:].rearrange("p t d -> p (t d)")
        s = {n: k.sem(f"{name}_{n}", ctx) for n in ("q_ready", "scored", "score_read", "centred", "exped", "weighed", "turned",
                                                    "rest_copied", "copied", "mixed", "normed", "topped", "inverted", "prob_ready")}
        keys2 = keys[:].rearrange("p b h s -> p (b h s)") if heads > 1 else keys.rearrange("p b h s -> p (b h s)")
        vals2 = vals[:].rearrange("p b c h d -> p (b c h d)")
        added2 = added[:].rearrange("p t i s -> p (t i s)")
        W2 = PER_BANK * KW
        MIX, MISC = k.bank[6], k.bank[7]
        if weighted:
            prob_now = k.sb(f"{name}_prob_now", [P, TB, KW], F32, ctx)

        LAG = 3

        def over_groups(eng, lead, first, steps, last):
            first()
            steps(0, 0, lead)
            with eng.Fori(0, B - 1) as b:
                steps(b, lead, NB + lead)
            steps(B - 1, lead, NB)
            last()

        def ahead(b, G):
            return G < NB or not isinstance(b, int) or b < B - 1

        def tops_before(b, G):
            return b * (NB // NG * sum(centre_here(g) for g in range(NG))) + sum(centre_here(i % NG) for i in range(G))

        def norm_due(G):
            t, g = divmod(G - LAG, NG)
            return t if g == NG - 1 and t >= 0 else None

        with nc.Block() as block:
            @block.tensor
            def _(pe):
                def score(b, G):
                    pe.wait_ge(s["score_read"], b * NB + G + 1)
                    t, g = divmod(G, NG)
                    if g == 0:
                        pe.wait_ge(s["q_ready"], b * TB + t + 1)
                    for i in range(BANKS):
                        ins = nc.tensor.matmul(k.bank[BANKS * (G % 2) + i][:, 0:W2], qT[:, ds(t % TB)],
                                               keys2[:, bass.ds(((b + t // TB) * heads + g * HG + i * PER_BANK) * KW, W2)],
                                               start=True, stop=True)
                    ins.then_inc(s["scored"], 1)

                def turn(b, G):
                    pe.wait_ge(s["weighed" if weighted else "exped"], b * NB + G + 1 + weighted)
                    for c in range(CH - 1):
                        nc.tensor.transpose(k.bank[4 + G % 2][0:CR, ds(c)], used[:, G % RING, c::CH], k.ident[:])
                    pe.wait_ge(s["rest_copied"], b * NB + G + 1)
                    nc.tensor.transpose(MISC[0:CR, 0:P], used[:, G % RING, CH - 1::CH], k.ident[:]).then_inc(s["turned"], 1)

                def mix(b, G):
                    pe.wait_ge(s["copied"], b * NB + G + 1)
                    t, g = divmod(G, NG)
                    if g == 0:
                        pe.wait_ge(s["normed"], b * TB + t + 1)
                    for c in range(CH):
                        ins = nc.tensor.matmul(MIX[:, ds(g, GW)], probsT[0:CR, G % 2, c, :],
                                               vals2[0:CR, bass.ds((((b + t // TB) * CH + c) * NG + g) * GW, GW)], start=c == 0, stop=c == CH - 1)
                    if g == NG - 1:
                        ins.then_inc(s["mixed"], 1)

                def first():
                    score(0, 0)
                    score(0, 1)

                def steps(b, start, end):
                    for G in range(start, end):
                        if ahead(b, G + 2):
                            score(b, G + 2)
                        turn(b, G)
                        if G > 0:
                            mix(b, G - 1)

                over_groups(pe, 1, first, steps, lambda: mix(B - 1, NB - 1))

            @block.scalar
            def _(act):
                free_at_first(act, s["rest_copied"])

                def take_q(b, t):
                    nc.scalar.copy(qT[:, ds(t)], q_all[:, ds(b * TB + t)]).then_inc(s["q_ready"], 1)

                def exp(b, G):
                    act.wait_ge(s["centred"], b * NB + G + 1)
                    t, g = divmod(G, NG)
                    tile = probs[:, G % RING]
                    if centre_here(g):
                        ins = nc.scalar.activation(tile, tile, ACT.Exp)
                    else:
                        for h in range(HG):
                            hh = g * HG + h
                            ins = nc.scalar.activation(tile[:, ds(h, KW)], tile[:, ds(h, KW)], ACT.Exp, bias=negmax[:, t % 2, hh:hh + 1],
                                                       **({"accum_out": sums[:, t % 2, hh:hh + 1]} if weighted else {}))
                    ins.then_inc(s["exped"], 1)

                def first():
                    for t in range(TB):
                        take_q(0, t)
                    exp(0, 0)

                def steps(b, start, end):
                    for G in range(start, end):
                        if ahead(b, G + 1):
                            exp(b, G + 1)
                        act.wait_ge(s["turned"], b * NB + G + 1)
                        nc.scalar.copy(probsT[0:CR, G % 2, CH - 1, :], MISC[0:CR, 0:P]).then_inc(s["rest_copied"], 1)
                        nc.scalar.copy(probsT[0:CR, G % 2, 0:CH - 1, :],
                                       k.bank[4 + G % 2][0:CR, 0:(CH - 1) * P].rearrange("p (c n) -> p c n", n=P)).then_inc(s["copied"], 1)
                        if G % NG == 0 and G > 0 and ahead(b, NB):
                            take_q(b + 1, G // NG - 1)

                over_groups(act, 1, first, steps, lambda: None)

            @block.vector
            def _(dve):
                free_at_first(dve, s["score_read"], by=AHEAD)
                free_at_first(dve, s["normed"])
                NORM_STEPS = 1 + (mask_kind == "where")

                def norm(b, t):
                    dve.wait_ge(s["mixed"], b * TB + t + 1)
                    mix = by_head(MIX[:, 0:heads * (dh + 1)], heads)
                    nc.vector.reciprocal(inv[:], sums[:, t % 2, :] if weighted else mix[:, :, dh]).then_inc(s["inverted"], 1)
                    dve.wait_ge(s["inverted"], (b * TB + t) * NORM_STEPS + 1)
                    if mask_kind == "where":
                        nc.vector.scalar_tensor_tensor(inv[:], negmax[:, t % 2, :], HUGE / 4, inv[:], ALU.is_lt, ALU.mult).then_inc(s["inverted"], 1)
                        dve.wait_ge(s["inverted"], (b * TB + t) * NORM_STEPS + 2)
                    if project:
                        home = by_head(outs_flat[:, ds(b * TB + t)], heads)
                        nc.vector.tensor_tensor(home, mix[:, :, 0:dh], inv[:, :, None].broadcast_to([P, heads, dh]),
                                                ALU.mult).then_inc(s["normed"], 1)
                    else:
                        home = k.x[:, ds(b * TB + t)]
                        nc.vector.scalar_tensor_tensor(home, MIX[:, 0:D], inv[:, 0:1], home, ALU.mult, ALU.add).then_inc(s["normed"], 1)

                def steps(b, start, end):
                    for G in range(start, end):
                        t, g = divmod(G, NG)
                        tile = probs[:, G % RING]
                        mt = added2[:, ds(b * TB + t if mask_tiles == NT else t % TB, W2)]
                        dve.wait_ge(s["scored"], b * NB + G + 1)
                        nc.vector.scalar_tensor_tensor(
                            tile.rearrange("p (i s) -> p i s", i=BANKS), k.psum[:, BANKS * (G % 2):BANKS * (G % 2) + BANKS, 0:W2], scale,
                            mt[:, None, :].broadcast_to([P, BANKS, W2]), ALU.mult, ALU.add).then_inc(s["score_read"], 1)
                        dve.wait_ge(s["score_read"], b * NB + G + 1 + AHEAD)
                        top = negmax[:, t % 2, g * HG:(g + 1) * HG]
                        maximum = nc.vector.tensor_reduce(top, by_head(tile, HG), AX_X, ALU.max, negate=True)
                        if centre_here(g):
                            maximum.then_inc(s["topped"], 1)
                            dve.wait_ge(s["topped"], tops_before(b, G) + 1)
                            nc.vector.tensor_tensor(by_head(tile, HG), by_head(tile, HG), top[:, :, None].broadcast_to([P, HG, KW]),
                                                    ALU.add).then_inc(s["centred"], 1)
                        else:
                            maximum.then_inc(s["centred"], 1)
                        if norm_due(G) is not None:
                            norm(b, norm_due(G))

                def last():
                    for t in range(TB):
                        if t * NG + NG - 1 + LAG >= NB:
                            norm(B - 1, t)

                over_groups(dve, LAG, lambda: None, steps, last)

            if weighted:
                @block.gpsimd
                def _(pool):
                    free_at_first(pool, s["weighed"], s["prob_ready"])
                    nc.gpsimd.memset(prob_now[:], 0.0).then_inc(s["prob_ready"], 1)
                    pool.wait_ge(s["prob_ready"], 2)
                    with pool.Fori(0, B) as b:
                        pool.wait_ge(s["weighed"], b * NB + 1)
                        nc.gpsimd.tensor_copy(prob_now[:, :, 0:SC], prob[:, ds(b, TB * SC)].rearrange("p (t s) -> p t s", t=TB)).then_inc(s["prob_ready"], 1)
                        pool.wait_ge(s["prob_ready"], b + 3)
                        for G in range(NB):
                            pool.wait_ge(s["exped"], b * NB + G + 1)
                            nc.gpsimd.tensor_tensor(by_head(used[:, G % RING], HG), by_head(probs[:, G % RING], HG),
                                                    prob_now[:, G // NG, None, :].broadcast_to([P, HG, KW]),
                                                    ALU.mult).then_inc(s["weighed"], 1)

        if project:
            add_projection(k, ctx, name, outs, wo, k.x)


def stage_1x(k):
    cross_attention(k, "a1", H16, "mask1", "int", DH ** -0.5, biased=True, weighted=True, project=True)


def stage_2x(k):
    cross_attention(k, "a2", 1, "mask2", "float", D ** -0.5, biased=False, weighted=False, project=False)


def stage_3x(k):
    cross_attention(k, "a3", H16, "mask3", "where", DH ** -0.5, biased=True, weighted=False, project=True)


def program(nc, dram, out):
    with ExitStack() as ctx:
        k = Core(nc, ctx, dram)
        loaded = k.sem("x_loaded")
        stored = k.sem("x_stored")
        x_tiles = k.x[:].rearrange("p (t d) -> p t d", d=D)
        with nc.Block() as block:
            @block.sync
            def _(sp):
                sp.dma_start(x_tiles, dram["x"].rearrange("(t p) d -> p t d", p=P)).then_inc(loaded, 16)
                sp.dma_start(k.ident[:], dram["identity"]).then_inc(loaded, 16)
                sp.dma_start(k.headmask[:], dram["headmask"]).then_inc(loaded, 16)
                sp.dma_start(k.ctxT[:], dram["ctxT"]).then_inc(loaded, 16)
                sp.wait_ge(loaded, 64)
        for stage in (stage_0x, stage_0f, stage_1x, stage_1f, stage_2x, stage_lora, stage_3x, stage_3f):
            stage(k)
        with nc.Block() as block:
            @block.sync
            def _(sp):
                sp.dma_start(out.rearrange("(t p) d -> p t d", p=P), x_tiles).then_inc(stored, 16)
                sp.wait_ge(stored, 16)


def constants():
    part = np.arange(P)
    freq = (1.0 / np.float32(10000.0) ** (np.arange(0, D, 2, dtype=np.float32) / np.float32(D))).astype(np.float64)
    angle = np.concatenate([freq, freq])[:, None] * np.arange(S)[None, :]
    sign = np.where(part < D // 2, 1.0, -1.0)[:, None]
    f = {
        "identity": np.eye(P),
        "headmask": (part[:, None] // DH == np.arange(H16)[None, :]),
        "own_rows": (np.arange(96)[:, None] % 32 // DH == np.arange(4)[None, :]),
        "rot_cos": np.cos(angle),
        "rot_sin": np.sin(angle) * sign,
        "key_waves": np.where(part[:, None] < D // 2, np.sin(angle), np.cos(angle)),
        "before": part[:, None] < part[None, :],
        "iota32": np.tile(np.arange(E1), (P, 1)),
        "iota16": np.tile(np.arange(E0), (P, 1)),
        "slot_base": np.tile(np.arange(E0) * CAP, (P, 1)),
        "spare_slot": SLOTS + np.arange(NT)[None, :] * P + part[:, None],
    }
    c = {n: np.ascontiguousarray(v, dtype=np.float32) for n, v in f.items()}
    bits = (1 << (MAG_BITS - 1 - np.arange(MAG_BITS))).astype(np.int32)
    c["bits"] = np.ascontiguousarray(np.tile(np.repeat(bits, E0), (P, 1)))
    return c


def laid_out(i):
    row = lambda v: np.broadcast_to(v.reshape(1, -1), (P, v.size))
    stack_columns = lambda w: np.tile(w.reshape(D, 4, 1, 32), (1, 1, 3, 1)).reshape(D, -1)
    stack_rows = lambda w: np.tile(w.reshape(4, 1, 32, D), (1, 3, 1, 1)).reshape(4, 96, D).transpose(1, 0, 2).reshape(96, -1)
    context_tiles = lambda v: np.pad(v, ((0, 0), (0, 2 * P - SC), (0, 0))).reshape(B * 2, P, D).transpose(1, 0, 2).reshape(P, -1)
    in_tiles = lambda v: v.reshape(-1, P, SC).transpose(1, 0, 2).reshape(P, -1)
    col = lambda v: v.reshape(-1, P).T
    a = {
        "x": i["x"].reshape(NTOK, D),
        "ctx_rows": context_tiles(i["ctx_1024"]),
        "ctxT": i["ctx_1024"].reshape(B * SC, D).T,
        "prob": in_tiles(i["fside_BxSxS2_0"]),
        "mask1": in_tiles(i["mask_BxSxS2_ik1"]),
        "mask2": in_tiles(i["mask_SxS2_fk0"]),
        "mask3": in_tiles(i["mask_1x1xSxS2_ik0"]),
        "a0_ln": np.stack([i["L0_xattn_gamma_media"], i["L0_xattn_beta_media"], i["L0_xattn_gamma_lat"], i["L0_xattn_beta_lat"]], 1),
        "a0_wq": i["L0_xattn_Wq"], "a0_bq": col(i["L0_xattn_bq"]),
        "a0_wk": i["L0_xattn_Wkv"][:, :8 * P], "a0_bk": col(i["L0_xattn_bkv"][:8 * P]), "a0_bv": col(i["L0_xattn_bkv"][8 * P:]),
        "a0_wvT": i["L0_xattn_Wkv"][:, 8 * P:].reshape(D, 8, P).transpose(2, 1, 0).reshape(P, -1),
        "a0_wo": i["L0_xattn_Wo"].reshape(8, P, D).transpose(1, 0, 2).reshape(P, -1), "a0_bo": row(i["L0_xattn_bo"]),
        "m0_gate_w": i["L0_ffn_gate_w"], "m0_gate_b": row(i["L0_ffn_gate_b"]),
        "m0_w13": np.concatenate([i["L0_ffn_ew1"], i["L0_ffn_ew3"]], 2),
        "m0_w2": i["L0_ffn_ew2"].reshape(E0, 2, P, D).transpose(0, 2, 1, 3).reshape(E0, P, 2 * D),
        "s0_w1": i["L0_ffn_sw1"].transpose(1, 0, 2).reshape(P, -1),
        "s0_w3": i["L0_ffn_sw3"].transpose(1, 0, 2).reshape(P, -1),
        "s0_w2": i["L0_ffn_sw2"].reshape(S0 * 2, P, D).transpose(1, 0, 2).reshape(P, -1),
        "a1_wq": i["L1_xattn_wq_k"], "a1_bq": col(i["L1_xattn_wq_b"]), "a1_wk": i["L1_xattn_wk_k"],
        "a1_bk": col(i["L1_xattn_wk_b"]), "a1_wv": i["L1_xattn_wv_k"], "a1_bv": row(i["L1_xattn_wv_b"]),
        "a1_wo": i["L1_xattn_wo_k"], "a1_bo": row(i["L1_xattn_wo_b"]),
        "f1_ln1": np.stack([i["L1_ffn_ln1_g"], i["L1_ffn_ln1_b"]], 1), "f1_ln2": np.stack([i["L1_ffn_ln2_g"], i["L1_ffn_ln2_b"]], 1),
        "f1_wq": stack_columns(i["L1_ffn_wq"]), "f1_wk": stack_columns(i["L1_ffn_wk"]), "f1_wv": i["L1_ffn_wv"], "f1_wo": i["L1_ffn_wo"],
        "f1_wpT": stack_rows(i["L1_ffn_wp"].T), "f1_wpT_swapped": stack_rows(np.roll(i["L1_ffn_wp"], D // 2, axis=0).T),
        "m1_sel": i["L1_ffn_sel_w"],
        "m1_w": np.concatenate([i["L1_ffn_keys"], i["L1_ffn_values"]], 2),
        "a2_wq": i["L2_xattn_Wq"].T, "a2_wk": i["L2_xattn_Wk"].T, "a2_wv": i["L2_xattn_Wv"].T, "a2_bv": row(i["L2_xattn_bv"]),
        "lora_wT": i["L2_ffn_W"].T, "lora_b": row(i["L2_ffn_b"]), "lora_downT": i["L2_ffn_lora_down"].T,
        "lora_down_aux": i["L2_ffn_down_aux"], "lora_upT": i["L2_ffn_lora_up"].T, "lora_up_auxT": i["L2_ffn_up_aux"].T,
        "a3_wq": i["L3_xattn_Wq"].T, "a3_bq": col(i["L3_xattn_bq"]), "a3_wk": i["L3_xattn_Wk"].T, "a3_bk": col(i["L3_xattn_bk"]),
        "a3_wv": i["L3_xattn_Wv"].T, "a3_bv": row(i["L3_xattn_bv"]), "a3_wo": i["L3_xattn_Wo"].T, "a3_bo": row(i["L3_xattn_bo"]),
        "f3_fc": i["L3_ffn_w_fc"].reshape(HID3 // P, P, D).transpose(1, 0, 2).reshape(P, -1),
        "f3_proj": i["L3_ffn_w_proj"], "f3_uT": i["L3_ffn_u"].T, "f3_v": i["L3_ffn_v"], "f3_bT": i["L3_ffn_fast_b"].T,
        "f3_gate": row(i["L3_ffn_gate"]),
    }
    return {n: np.ascontiguousarray(v) for n, v in a.items()} | constants()


def kernel(**inputs):
    import concourse.bacc as bacc
    from concourse.bass_utils import run_bass_kernel_spmd

    nc = bacc.Bacc("TRN2", target_bir_lowering=False, num_devices=1)
    arrays = laid_out({n: np.asarray(v) for n, v in inputs.items()})
    dram = {n: nc.dram_tensor(n + "_dram", a.shape, mybir.dt.from_np(a.dtype), kind="ExternalInput").ap()
            for n, a in arrays.items()}
    out = nc.dram_tensor("out_dram", (NTOK, D), F32, kind="ExternalOutput").ap()
    program(nc, dram, out)
    r = run_bass_kernel_spmd(nc, [{n + "_dram": a for n, a in arrays.items()}], core_ids=[0])
    return r.results[0]["out_dram"].reshape(B, S, D)
```
